# Optimizing a Trainium2 kernel written in Bass

```python
import numpy as np
import jax
import jax.numpy as jnp

def _softmax(x, axis=-1):
    return jax.nn.softmax(x, axis=axis)

def _gelu(x):
    return jax.nn.gelu(x, approximate=True)

def _silu(x):
    return jax.nn.silu(x)

def _sigmoid(x):
    return jax.nn.sigmoid(x)

def _layernorm(x, axis=-1, eps=1e-05):
    m = jnp.mean(x, axis=axis, keepdims=True)
    v = jnp.var(x, axis=axis, keepdims=True)
    return (x - m) / jnp.sqrt(v + eps)

def _scatter_add(tgt, idx, src, axis=0):
    return tgt.at[idx].add(src)

def _segment_sum(src, seg, n):
    return jax.ops.segment_sum(src, seg, n)
kernel_name = 'mk_perceiver_d1_seqx_r4_8b0b00'

def setup_inputs(seed: int=0):
    np.random.seed(seed)
    _w = jnp.asarray

    def _rec_inputs():
        import jax
        import jax.numpy as jnp
        _rk = jax.random.key(seed)
        x = -0.0003929 + 0.9999 * jax.random.normal(jax.random.fold_in(_rk, 1), (128, 32, 256), jnp.float32)
        _lenS = 32 - jax.random.randint(jax.random.fold_in(_rk, 7), (128,), 0, max(1, 32 // 4) + 1, jnp.int32)
        _lenS2 = 257 - jax.random.randint(jax.random.fold_in(_rk, 8), (128,), 0, max(1, 257 // 4) + 1, jnp.int32)
        _ctx_1024P = jax.random.normal(jax.random.fold_in(_rk, 11), (128, 16, 256), jnp.float32)
        _ctx_1024c = jax.random.dirichlet(jax.random.fold_in(_rk, 511), 0.3 * jnp.ones((16,), jnp.float32), (128, 257))
        _ctx_1024t = jnp.einsum('bsk,bkd->bsd', _ctx_1024c, _ctx_1024P)
        _ctx_1024t = _ctx_1024t * jax.lax.rsqrt(jnp.mean(jnp.square(_ctx_1024t)) + 1e-12) * 0.953939
        ctx_1024 = 0.00208318 + 0.999174 * (_ctx_1024t + 0.3 * jax.random.normal(jax.random.fold_in(_rk, 611), (128, 257, 256), jnp.float32))
        _validS = jnp.arange(32)[None, :] < _lenS[:, None]
        _validS2 = jnp.arange(257)[None, :] < _lenS2[:, None]
        _causal = jnp.tril(jnp.ones((32, 32), dtype=bool))
        mask_BxSxS2_ff0 = jnp.where(jnp.ones((128, 32, 257), dtype=bool), 0.0, -1000000000.0).astype(jnp.float32)
        return (x, ctx_1024, mask_BxSxS2_ff0)
    x, ctx_1024, mask_BxSxS2_ff0 = _rec_inputs()

    def _L0_xattn_setup():
        import jax, jax.numpy as jnp
        import numpy as np
        NUM_HEADS = 16
        DIM = 256
        key = jax.random.key(seed)
        ks = jax.random.split(key, 12)
        B, N, T, C = (4, 1024, 77, DIM)
        s = 1.0 / np.sqrt(C)
        return {'hidden_states': jax.random.normal(ks[0], (B, N, C), jnp.float32), 'encoder_hidden_states': jax.random.normal(ks[1], (B, T, C), jnp.float32), 'attention_mask': jnp.zeros((B, N, T), jnp.float32), 'Wq': jax.random.normal(ks[2], (C, C), jnp.float32) * s, 'bq': jnp.zeros((C,), jnp.float32), 'Wk': jax.random.normal(ks[3], (C, C), jnp.float32) * s, 'bk': jnp.zeros((C,), jnp.float32), 'Wv': jax.random.normal(ks[4], (C, C), jnp.float32) * s, 'bv': jnp.zeros((C,), jnp.float32), 'Wo': jax.random.normal(ks[5], (C, C), jnp.float32) * s, 'bo': jnp.zeros((C,), jnp.float32)}
    _L0_xattn_all = _L0_xattn_setup()
    _L0_xattn_in = {k: v for k, v in _L0_xattn_all.items() if k in ('Wq', 'bq', 'Wk', 'bk', 'Wv', 'bv', 'Wo', 'bo')}
    del _L0_xattn_all

    def _L0_attn_setup():
        import jax, jax.numpy as jnp
        import numpy as np
        D_CONV = 4
        CHUNK = 64

        def segsum(x):
            T = x.shape[-1]
            strict = jnp.tril(jnp.ones((T, T), dtype=bool), -1)
            xr = jnp.where(strict, x[..., :, None], 0.0)
            x_segsum = jnp.cumsum(xr, axis=-2)
            return jnp.where(jnp.tril(jnp.ones((T, T), dtype=bool)), x_segsum, -jnp.inf)

        def ssd(x, A, B, C, chunk):
            b, s, h, p = x.shape
            c = s // chunk
            x = x.reshape(b, c, chunk, h, p)
            B = B.reshape(b, c, chunk, h, -1)
            C = C.reshape(b, c, chunk, h, -1)
            A = A.reshape(b, c, chunk, h).transpose(0, 3, 1, 2)
            A_cumsum = jnp.cumsum(A, axis=-1)
            L = jnp.exp(segsum(A))
            Y_diag = jnp.einsum('bclhn,bcshn,bhcls,bcshp->bclhp', C, B, L, x)
            decay_states = jnp.exp(A_cumsum[..., -1:] - A_cumsum)
            states = jnp.einsum('bclhn,bhcl,bclhp->bchpn', B, decay_states, x)
            states = jnp.concatenate([jnp.zeros_like(states[:, :1]), states], axis=1)
            A_last = jnp.pad(A_cumsum[..., -1], ((0, 0), (0, 0), (1, 0)))
            decay_chunk = jnp.exp(segsum(A_last))
            states = jnp.einsum('bhzc,bchpn->bzhpn', decay_chunk, states)[:, :-1]
            Y_off = jnp.einsum('bclhn,bchpn,bhcl->bclhp', C, states, jnp.exp(A_cumsum))
            return (Y_diag + Y_off).reshape(b, s, h, p)
        key = jax.random.key(seed)
        ks = jax.random.split(key, 6)
        d_model, d_state, d_inner, n_heads = (256, 256, 256, 16)
        d_in_proj = 2 * d_state + d_inner + n_heads
        d_conv_c = 2 * d_state + d_inner
        b, s = (4, 1024)

        def xavier(k, shape):
            bnd = float(np.sqrt(6.0 / (shape[0] + shape[1])))
            return jax.random.uniform(k, shape, minval=-bnd, maxval=bnd, dtype=jnp.float32)
        return {'x': jax.random.normal(ks[0], (b, s, d_model), dtype=jnp.float32), 'W_in': xavier(ks[1], (d_in_proj, d_model)), 'conv_w': jax.random.uniform(ks[2], (d_conv_c, D_CONV), minval=-0.8, maxval=0.8, dtype=jnp.float32), 'conv_b': jnp.zeros((d_conv_c,), dtype=jnp.float32), 'A_param': jax.random.uniform(ks[3], (16,), minval=-0.01, maxval=0.01, dtype=jnp.float32), 'dt_bias': jax.random.uniform(ks[4], (16,), minval=-0.1, maxval=0.1, dtype=jnp.float32), 'W_out': xavier(ks[5], (d_model, d_inner))}
    _L0_attn_all = _L0_attn_setup()
    _L0_attn_in = {k: v for k, v in _L0_attn_all.items() if k in ('W_in', 'conv_w', 'conv_b', 'A_param', 'dt_bias', 'W_out')}
    del _L0_attn_all

    def _L0_ffn_setup():
        import jax, jax.numpy as jnp
        import numpy as np
        NUM_EXPERTS = 8
        TOP_K = 2
        HIDDEN = 256
        INTER = 704
        key = jax.random.key(seed)
        ks = jax.random.split(key, 5)
        scale = 0.02
        return {'x': jax.random.normal(ks[0], (4, 512, HIDDEN), dtype=jnp.float32), 'w_router': jax.random.normal(ks[1], (NUM_EXPERTS, HIDDEN), dtype=jnp.float32) * scale, 'w_gate': jax.random.normal(ks[2], (NUM_EXPERTS, HIDDEN, INTER), dtype=jnp.float32) * scale, 'w_up': jax.random.normal(ks[3], (NUM_EXPERTS, HIDDEN, INTER), dtype=jnp.float32) * scale, 'w_down': jax.random.normal(ks[4], (NUM_EXPERTS, INTER, HIDDEN), dtype=jnp.float32) * scale}
    _L0_ffn_all = _L0_ffn_setup()
    _L0_ffn_in = {k: v for k, v in _L0_ffn_all.items() if k in ('w_router', 'w_gate', 'w_up', 'w_down')}
    del _L0_ffn_all
    return {'x': x, 'ctx_1024': ctx_1024, 'mask_BxSxS2_ff0': mask_BxSxS2_ff0, 'L0_xattn_Wq': _L0_xattn_in['Wq'], 'L0_xattn_bq': _L0_xattn_in['bq'], 'L0_xattn_Wk': _L0_xattn_in['Wk'], 'L0_xattn_bk': _L0_xattn_in['bk'], 'L0_xattn_Wv': _L0_xattn_in['Wv'], 'L0_xattn_bv': _L0_xattn_in['bv'], 'L0_xattn_Wo': _L0_xattn_in['Wo'], 'L0_xattn_bo': _L0_xattn_in['bo'], 'L0_attn_W_in': _L0_attn_in['W_in'], 'L0_attn_conv_w': _L0_attn_in['conv_w'], 'L0_attn_conv_b': _L0_attn_in['conv_b'], 'L0_attn_A_param': _L0_attn_in['A_param'], 'L0_attn_dt_bias': _L0_attn_in['dt_bias'], 'L0_attn_W_out': _L0_attn_in['W_out'], 'L0_ffn_w_router': _L0_ffn_in['w_router'], 'L0_ffn_w_gate': _L0_ffn_in['w_gate'], 'L0_ffn_w_up': _L0_ffn_in['w_up'], 'L0_ffn_w_down': _L0_ffn_in['w_down']}

def reference(x, ctx_1024, mask_BxSxS2_ff0, L0_xattn_Wq, L0_xattn_bq, L0_xattn_Wk, L0_xattn_bk, L0_xattn_Wv, L0_xattn_bv, L0_xattn_Wo, L0_xattn_bo, L0_attn_W_in, L0_attn_conv_w, L0_attn_conv_b, L0_attn_A_param, L0_attn_dt_bias, L0_attn_W_out, L0_ffn_w_router, L0_ffn_w_gate, L0_ffn_w_up, L0_ffn_w_down):
    import jax
    import jax.numpy as jnp

    def _L0_xattn_ref(hidden_states, encoder_hidden_states, attention_mask, Wq, bq, Wk, bk, Wv, bv, Wo, bo):
        import jax, jax.numpy as jnp
        import numpy as np
        NUM_HEADS = 16
        DIM = 256
        B, N, C = hidden_states.shape
        T = encoder_hidden_states.shape[1]
        H = NUM_HEADS
        D = C // H
        q = (hidden_states @ Wq.T + bq).reshape(B, N, H, D).transpose(0, 2, 1, 3)
        k = (encoder_hidden_states @ Wk.T + bk).reshape(B, T, H, D).transpose(0, 2, 1, 3)
        v = (encoder_hidden_states @ Wv.T + bv).reshape(B, T, H, D).transpose(0, 2, 1, 3)
        scale = 1.0 / jnp.sqrt(jnp.asarray(D, q.dtype))
        scores = jnp.einsum('bhnd,bhtd->bhnt', q, k) * scale + attention_mask[:, None, :, :]
        attn = jax.nn.softmax(scores, axis=-1)
        out = jnp.einsum('bhnt,bhtd->bhnd', attn, v)
        out = out.transpose(0, 2, 1, 3).reshape(B, N, C)
        return out @ Wo.T + bo

    def _L0_attn_ref(x, W_in, conv_w, conv_b, A_param, dt_bias, W_out):
        import jax, jax.numpy as jnp
        import numpy as np
        D_CONV = 4
        CHUNK = 64

        def segsum(x):
            T = x.shape[-1]
            strict = jnp.tril(jnp.ones((T, T), dtype=bool), -1)
            xr = jnp.where(strict, x[..., :, None], 0.0)
            x_segsum = jnp.cumsum(xr, axis=-2)
            return jnp.where(jnp.tril(jnp.ones((T, T), dtype=bool)), x_segsum, -jnp.inf)

        def ssd(x, A, B, C, chunk):
            b, s, h, p = x.shape
            c = s // chunk
            x = x.reshape(b, c, chunk, h, p)
            B = B.reshape(b, c, chunk, h, -1)
            C = C.reshape(b, c, chunk, h, -1)
            A = A.reshape(b, c, chunk, h).transpose(0, 3, 1, 2)
            A_cumsum = jnp.cumsum(A, axis=-1)
            L = jnp.exp(segsum(A))
            Y_diag = jnp.einsum('bclhn,bcshn,bhcls,bcshp->bclhp', C, B, L, x)
            decay_states = jnp.exp(A_cumsum[..., -1:] - A_cumsum)
            states = jnp.einsum('bclhn,bhcl,bclhp->bchpn', B, decay_states, x)
            states = jnp.concatenate([jnp.zeros_like(states[:, :1]), states], axis=1)
            A_last = jnp.pad(A_cumsum[..., -1], ((0, 0), (0, 0), (1, 0)))
            decay_chunk = jnp.exp(segsum(A_last))
            states = jnp.einsum('bhzc,bchpn->bzhpn', decay_chunk, states)[:, :-1]
            Y_off = jnp.einsum('bclhn,bchpn,bhcl->bclhp', C, states, jnp.exp(A_cumsum))
            return (Y_diag + Y_off).reshape(b, s, h, p)
        b, src_len, d_model = x.shape
        n_heads = A_param.shape[0]
        d_conv_c = conv_w.shape[0]
        d_inner = W_out.shape[1]
        d_state = (d_conv_c - d_inner) // 2
        pad = -src_len % CHUNK
        xs = jnp.pad(x, ((0, 0), (0, pad), (0, 0)))
        s = xs.shape[1]
        proj = xs @ W_in.T
        xBC, dt = (proj[..., :d_conv_c], proj[..., d_conv_c:])
        xp = jnp.pad(xBC, ((0, 0), (D_CONV - 1, 0), (0, 0)))
        conv_out = sum((xp[:, k:k + s, :] * conv_w[:, k] for k in range(D_CONV))) + conv_b
        C_ = conv_out[..., :d_state]
        B_ = conv_out[..., d_state:2 * d_state]
        xin = conv_out[..., 2 * d_state:]
        dt = jax.nn.softplus(dt + dt_bias)
        Ch = C_.reshape(b, s, n_heads, -1)
        Bh = B_.reshape(b, s, n_heads, -1)
        xh = xin.reshape(b, s, n_heads, -1)
        A = A_param * dt
        cumA = jnp.cumsum(A, axis=1)
        norm = (jnp.exp(cumA) * jnp.cumsum(jnp.exp(-cumA), axis=1))[..., None]
        Y = ssd(xh, A, Bh, Ch, CHUNK)
        out = Y[0] / norm
        out = out.reshape(b, s, -1) @ W_out.T
        return out[:, :src_len]

    def _L0_ffn_ref(x, w_router, w_gate, w_up, w_down):
        import jax, jax.numpy as jnp
        import numpy as np
        NUM_EXPERTS = 8
        TOP_K = 2
        HIDDEN = 256
        INTER = 704
        B, S, H = x.shape
        T = B * S
        E = w_router.shape[0]
        xf = x.reshape(T, H)
        logits = xf @ w_router.T
        top_w, sel = jax.lax.top_k(logits, TOP_K)
        top_w = jax.nn.softmax(top_w, axis=-1)
        gates = jnp.zeros((T, E), dtype=x.dtype).at[jnp.arange(T)[:, None], sel].add(top_w)
        out = jnp.zeros_like(xf)
        for e in range(E):
            h = jax.nn.silu(xf @ w_gate[e]) * (xf @ w_up[e])
            out = out + gates[:, e:e + 1] * (h @ w_down[e])
        return out.reshape(B, S, H)
    x = x + _L0_xattn_ref(_layernorm(x, axis=-1), ctx_1024, mask_BxSxS2_ff0, L0_xattn_Wq, L0_xattn_bq, L0_xattn_Wk, L0_xattn_bk, L0_xattn_Wv, L0_xattn_bv, L0_xattn_Wo, L0_xattn_bo)
    x = x + _L0_attn_ref(_layernorm(x, axis=-1), L0_attn_W_in, L0_attn_conv_w, L0_attn_conv_b, L0_attn_A_param, L0_attn_dt_bias, L0_attn_W_out)
    x = x + _L0_ffn_ref(_layernorm(x, axis=-1), L0_ffn_w_router, L0_ffn_w_gate, L0_ffn_w_up, L0_ffn_w_down)
    return x

_drawn_inputs = setup_inputs


def setup_inputs(seed=0):
    import zlib

    import numpy as np

    out = dict(_drawn_inputs(seed))
    spreads = {'L0_xattn_bq': (0.0, 0.327),
     'L0_xattn_bk': (0.0, 0.8),
     'L0_xattn_bv': (0.0, 0.1),
     'L0_xattn_bo': (0.0, 0.1),
     'L0_attn_conv_b': (0.0, 0.1)}
    factors = {'L0_attn_A_param': 7.671,
     'L0_attn_dt_bias': 8.0,
     'L0_ffn_w_router': 3.941,
     'L0_ffn_w_gate': 3.475,
     'L0_ffn_w_up': 3.441,
     'L0_ffn_w_down': 3.437}
    for name, (base, spread) in spreads.items():
        noise = np.random.default_rng([zlib.crc32(name.encode()), seed]).standard_normal(out[name].shape)
        drawn = base * np.exp(spread * noise) if base else spread * noise
        out[name] = jnp.asarray(drawn.astype(out[name].dtype))
    for name, factor in factors.items():
        out[name] = (out[name] * factor).astype(out[name].dtype)
    return out
```

```python
import concourse.bass as bass
from concourse import mybir
from contextlib import ExitStack

F32 = mybir.dt.float32
I32 = mybir.dt.int32
U32 = mybir.dt.uint32
ALU = mybir.AluOpType
ACT = mybir.ActivationFunctionType
AX = mybir.AxisListType

P = 128
B, Q, S, D = 128, 32, 257, 256
H, HD = 16, 16
E, F, TOPK = 8, 704, 2
NH = D // P
SP = S + 1
TB = P // Q
NT = B * Q // P
TOK = B * Q
HG = P // Q
NG = H // HG
GW = HG * HD
TC = 2
LAST = TC * P
KC = 4
NC = 3 * D // P
EPS = 1e-5
FC = (F + P - 1) // P
FL = F - (FC - 1) * P
FH = F // 2
NSLOT = (TOK * TOPK + E * (P - 1)) // P + 1
NSLOT += NSLOT % 2
TPE = TOK // P
TCOL = (E + 1) * TPE
ATANH = [2 * k + 1 for k in range(10, 0, -1)]

PARAMS = dict(wq=NH * D, wk=NH * D, wv=NH * D, wo=NH * D, wxbc=NH * 3 * D, wdt=NH * H, wout=NH * D,
              wrt=NH * E, bq=NH, bk=NH, bv=NH, bo=D, convw=NC * KC, convb=NC, apar=H, dtb=H)
CONSTS = dict(ident=P, sel=Q, hm=HG, bm=2 * HG, dm=HG, er=D, ep=D, trib=P, tris=P, ones=P, gt=Q, le=Q,
              bm8=P // HD, iota8=E, iotat=NSLOT, tok=2 * TOPK, nhalf=1, eps=1)


def columns(widths):
    at, out = 0, {}
    for name, w in widths.items():
        out[name] = (at, at + w)
        at += w
    return out, at


PCOL, NPAR = columns(PARAMS)
CCOL, NCON = columns(CONSTS)


def held(eng, met, *waits):
    for _, value in waits:
        if not isinstance(value, int):
            eng.compute_val(value)
    eng.wait_ge(*met)
    for sem, value in waits:
        at_least(eng, sem, value)


def at_least(eng, sem, value):
    if not isinstance(value, int) or value > 0:
        eng.wait_ge(sem, value)


def perceiver(nc, xd, ctxd, ctxl, maskd, pard, cond, padd, wgd, wud, wdd, outd):
    zbuf = nc.dram_tensor("zbuf", (TOK, D), F32).ap()
    table = nc.dram_tensor("slot_table", (P * TCOL, 4), I32).ap()
    ybuf = nc.dram_tensor("ybuf", (TOPK * TOK + P * TCOL, D), F32).ap()
    keep = ExitStack()
    with keep:
        con = keep.enter_context(nc.sbuf_tensor("con", [P, NCON], F32))
        wg = keep.enter_context(nc.sbuf_tensor("wg", [P, E, NH, F], F32))
        wu = keep.enter_context(nc.sbuf_tensor("wu", [P, E, NH, F], F32))
        x2 = keep.enter_context(nc.sbuf_tensor("x2", [P, NT, D], F32))
        chosen = keep.enter_context(nc.sbuf_tensor("chosen", [P, E], F32))
        w_in = keep.enter_context(nc.semaphore("w_in"))

        def cst(name):
            a, b = CCOL[name]
            return con[:, a:b]

        attend(nc, xd, ctxd, ctxl, maskd, pard, cond, padd, wgd, wud, zbuf, table, con, cst, wg, wu, x2, chosen, w_in)
        experts(nc, zbuf, table, ybuf, wdd, outd, cst, wg, wu, x2, chosen, w_in)


def attend(nc, xd, ctxd, ctxl, maskd, pard, cond, padd, wgd, wud, zbuf, table, con, cst, wg, wu, x2, chosen, w_in):
    own = ExitStack()
    with own:
        def sb(name, shape, dt=F32):
            return own.enter_context(nc.sbuf_tensor(name, shape, dt))

        def ps(name):
            return own.enter_context(nc.psum_tensor(name, [P, 512], F32))

        def sem(name):
            return own.enter_context(nc.semaphore(name))

        par = sb("par", [P, NPAR])

        def prm(name):
            a, b = PCOL[name]
            return par[:, a:b]

        def halves(name):
            return prm(name).rearrange("p (a n) -> p a n", a=NH)

        wq, wk, wv, wo = (halves(n) for n in ("wq", "wk", "wv", "wo"))
        wxbc, wdt, wout, wrt = (halves(n) for n in ("wxbc", "wdt", "wout", "wrt"))
        ident, ones = cst("ident"), cst("ones")

        ctx = sb("ctx", [P, TB, NH, SP])
        msk = sb("msk", [P, TB, S])
        qbd = sb("qbd", [P, TB, NG, P])
        kT = sb("kT", [P, NH, S])
        v = sb("v", [P, 2, TC, D])
        sm = sb("sm", [P, NG, S])
        pr = sb("pr", [P, NG, S])
        pT = sb("pT", [P, NG, TC, P])
        mx = sb("mx", [P, NG])
        nmx = sb("nmx", [P, NG])
        rsum = sb("rsum", [P, NG])
        rr = sb("rr", [P, 2, NG])
        px = sb("px", [P, 2 * NG, HG])
        om = sb("om", [P, NH, HG, Q])
        ou = sb("ou", [P, NH, P])
        rp = sb("rp", [2 * H, P])
        vl = sb("vl", [P, NH, B])
        ctl = sb("ctl", [P, NH, B])
        xt, z1, z1T, qs = sb("xt", [P, D]), sb("z1", [P, D]), sb("z1T", [P, NH, P]), sb("qs", [P, NH, P])
        xr, t1, t2, aT = sb("xr", [P, D]), sb("t1", [P, NH, P]), sb("t2", [P, NH, P]), sb("aT", [P, NH, P])
        x1, z2, z2T, yn = sb("x1", [P, D]), sb("z2", [P, D]), sb("z2T", [P, NH, P]), sb("yn", [P, D])
        ynT, z3, z3T = sb("ynT", [P, NH, P]), sb("z3", [P, D]), sb("z3T", [P, NH, P])
        y0 = sb("y0", [P, D])
        st = sb("st", [P, 3, 6])
        mv = sb("mv", [P, 3, 2])
        rs = sb("rs", [P, 3, 2])
        dtv = sb("dtv", [P, 10, H])
        lg = sb("lg", [P, 4, E])
        mi = sb("mi", [P, 8], U32)
        oh = sb("oh", [P, TOPK, E])
        ohr = sb("ohr", [P, TOPK, E])
        sv = sb("sv", [P, 8, TOPK])
        ri = sb("ri", [P, 3, TOPK], I32)
        pay = sb("pay", [P, TOPK, 4], I32)
        tokf = sb("tokf", [P, 2 * TOPK])
        spare = x2[:, 8:NT, :].rearrange("p t d -> p (t d)")
        cut = [0]

        def carve(n):
            cut[0] += n
            assert cut[0] <= (NT - 8) * D
            return spare[:, cut[0] - n:cut[0]]

        xp = carve(NC * (Q + KC - 1)).rearrange("p (c l) -> p c l", c=NC)
        cv = carve(2 * NC * Q).rearrange("p (k c l) -> p k c l", k=2, c=NC)
        cT = carve(NC * Q).rearrange("p (c l) -> p c l", c=NC)
        cbd = carve(NH * 8 * Q).rearrange("p (a h l) -> p a h l", a=NH, h=8)
        gs, at_, ls, ws = (carve(H * Q)[0:Q].rearrange("p (h l) -> p h l", h=H) for _ in range(4))
        w4 = carve(H * P)[0:Q].rearrange("p (h b l) -> p h b l", h=H, b=TB)
        xs = carve(D)[0:Q]

        KV = [ps("kv0"), ps("kv1")]
        SC = [ps("sc0"), ps("sc1")]
        PT = [ps("pt0"), ps("pt1")]
        O = ps("o")
        M = ps("m")
        OT = O[:, 0:NH * P].rearrange("p (a h q) -> p a h q", a=NH, h=HG)
        RP = O[0:2 * H, NH * P:NH * P + Q]
        M2 = M[:, 0:NH * P].rearrange("p (a n) -> p a n", a=NH)

        par_in, con_in, ctl_in, pad_in = sem("par_in"), sem("con_in"), sem("ctl_in"), sem("pad_in")
        ctx_in = [sem(f"ctx_in{b}") for b in range(TB)]
        msk_in = [sem(f"msk_in{b}") for b in range(TB)]
        xt_in, xr_in, z3_out, slots_out = sem("xt_in"), sem("xr_in"), sem("z3_out"), sem("slots_out")
        vl_ready, vl_done = sem("vl_ready"), sem("vl_done")
        k_ready, k_done, v_ready, v_done = sem("k_ready"), sem("k_done"), sem("v_ready"), sem("v_done")
        s_ready, max_done, nmx_done, exp_done = sem("s_ready"), sem("max_done"), sem("nmx_done"), sem("exp_done")
        pt_ready, pt0_done, pt1_done = sem("pt_ready"), sem("pt0_done"), sem("pt1_done")
        rec_done, pl_done, px_done = sem("rec_done"), sem("pl_done"), sem("px_done")
        o_ready, om_done, ou_done, rp_done = sem("o_ready"), sem("om_done"), sem("ou_done"), sem("rp_done")
        st1, mv1, var1, rstd1, z1_done = sem("st1"), sem("mv1"), sem("var1"), sem("rstd1"), sem("z1_done")
        z1T_ready, z1T_done, q_ready, qs_done, qbd_done = (sem("z1T_ready"), sem("z1T_done"), sem("q_ready"),
                                                           sem("qs_done"), sem("qbd_done"))
        ex_ready, t_done, t3_done, aT_done = sem("ex_ready"), sem("t_done"), sem("t3_done"), sem("aT_done")
        wo_ready, xb_done, x1_done = sem("wo_ready"), sem("xb_done"), sem("x1_done")
        st2, mv2, var2, rstd2, z2_done = sem("st2"), sem("mv2"), sem("var2"), sem("rstd2"), sem("z2_done")
        z2T_ready, z2T_done = sem("z2T_ready"), sem("z2T_done")
        dt_ready, dt_done, nabs_done, u_done, soft, a_done = (sem("dt_ready"), sem("dt_done"), sem("nabs_done"),
                                                              sem("u_done"), sem("soft"), sem("a_done"))
        cum_ready, ep_done, en_done, c2_ready = sem("cum_ready"), sem("ep_done"), sem("en_done"), sem("c2_ready")
        norm_done, rn_done, yn_done = sem("norm_done"), sem("rn_done"), sem("yn_done")
        ynT_ready, ynT_done, y_ready, x2_done = sem("ynT_ready"), sem("ynT_done"), sem("y_ready"), sem("x2_done")
        st3, mv3, var3, rstd3, z3_done = sem("st3"), sem("mv3"), sem("var3"), sem("rstd3"), sem("z3_done")
        z3T_ready, z3T_done, lg_ready, lg_done = sem("z3T_ready"), sem("z3T_done"), sem("lg_ready"), sem("lg_done")
        route, oh_done, mm_done, rank_ready, diff_done, gate_e = (sem("route"), sem("oh_done"), sem("mm_done"),
                                                                  sem("rank_ready"), sem("diff_done"), sem("gate_e"))
        pay_done, chosen_done = sem("pay_done"), sem("chosen_done")
        ssd_pe, ssd_act, ssd_dve = sem("ssd_pe"), sem("ssd_act"), sem("ssd_dve")
        init, soft_sum = sem("init"), sem("soft_sum")
        NSOFT = len(ATANH) + 6
        NROUTE = 12

        block = own.enter_context(nc.Block())

        @block.sync
        def _(sp):
            def load_ctx(i, b):
                if not (isinstance(i, int) and i == 0):
                    sp.wait_ge(v_ready, 4 * i + b - 3)
                sp.dma_start(ctx[:, b:b + 1], ctxd[:, bass.ds(4 * i + b, 1), :, :]).then_inc(ctx_in[b], 16)

            def load_mask(i, b):
                if not (isinstance(i, int) and i == 0):
                    sp.wait_ge(max_done, 4 * (4 * i + b - 3))
                for h in range(HG):
                    sp.dma_start(msk[h * Q:(h + 1) * Q, b:b + 1, :],
                                 maskd[bass.ds(4 * i + b, 1), :, :].rearrange("b q t -> q b t")
                                 ).then_inc(msk_in[b], 16)

            def load_x(i):
                if not (isinstance(i, int) and i == 0):
                    sp.wait_ge(z1_done, i)
                sp.dma_start(xt[:, :], xd[bass.ds(P * i, P), :]).then_inc(xt_in, 16)

            def load_residual(j):
                if not (isinstance(j, int) and j == 0):
                    sp.wait_ge(x1_done, j)
                sp.dma_start(xr[:, :], xd[bass.ds(P * j, P), :]).then_inc(xr_in, 16)

            def store_z3(j):
                sp.wait_ge(z3_done, j + 1)
                sp.dma_start(zbuf[bass.ds(P * j, P), :], z3[:, :]).then_inc(z3_out, 16)

            load_x(0)
            sp.dma_start(con[:, :], cond).then_inc(con_in, 16)
            sp.dma_start(par[:, :], pard).then_inc(par_in, 16)
            sp.dma_start(ctl[:, :, :], ctxl).then_inc(ctl_in, 16)
            for b in range(TB):
                load_ctx(0, b)
                load_mask(0, b)
            load_x(1)
            load_residual(0)
            sp.dma_start(table.rearrange("(p n) c -> p (n c)", p=P), padd).then_inc(pad_in, 16)
            for e in range(E):
                sp.dma_start(wg[:, e], wgd[:, e]).then_inc(w_in, 16)
                sp.dma_start(wu[:, e], wud[:, e]).then_inc(w_in, 16)

            def tile(i, first=False, last=False):
                for b in range(TB):
                    if not last:
                        load_mask(i + 1, b)
                        load_ctx(i + 1, b)
                    if b == 2 and not first:
                        load_residual(i)
                    if b == 3:
                        if not first:
                            store_z3(i - 1)
                        if isinstance(i, int):
                            if i + 2 < NT:
                                load_x(i + 2)
                        else:
                            load_x(i + 2)

            tile(0, first=True)
            tile(1)
            with sp.Fori(2, NT - 2) as i:
                tile(i)
            tile(NT - 2)
            tile(NT - 1, last=True)
            store_z3(NT - 1)
            sp.wait_ge(z3_out, 16 * NT)

        @block.tensor
        def _(pe):
            def mm(out, lhsT, rhs, start=True, stop=True):
                return nc.tensor.matmul(out, lhsT, rhs, start=start, stop=stop)

            def last_values():
                pe.wait_ge(par_in, 16)
                pe.wait_ge(con_in, 16)
                pe.wait_ge(ctl_in, 16)
                for a in range(NH):
                    for c in range(NH):
                        last = mm(M2[:, a, :], wv[:, c, a * P:(a + 1) * P], ctl[:, c, :], c == 0, c == NH - 1)
                last.then_inc(vl_ready, 1)

            def project_kv(i, b):
                n = 4 * i + b
                pe.wait_ge(ctx_in[b], 16 * (i + 1))
                for a in range(NH):
                    if a == 0:
                        at_least(pe, v_done, n)
                    else:
                        at_least(pe, k_done, 2 * n)
                    for c in range(NH):
                        last = mm(KV[a][:, 0:S], wk[:, c, a * P:(a + 1) * P], ctx[:, b, c, 0:S], c == 0, c == NH - 1)
                    last.then_inc(k_ready, 1)
                pe.wait_ge(k_done, 2 * n + 1)
                for t in range(TC):
                    for c in range(NH):
                        last = mm(KV[0][:, t * D:(t + 1) * D], ctx[:, b, c, t * P:(t + 1) * P], wv[:, c, :],
                                  c == 0, c == NH - 1)
                last.then_inc(v_ready, 1)

            def scores(i, b):
                n = 4 * i + b
                pe.wait_ge(qbd_done, 2 * n + 2)
                pe.wait_ge(k_done, 2 * n + 2)
                for g in range(NG):
                    at_least(pe, max_done, 4 * n + g - 1)
                    mm(SC[g % 2][:, 0:S], qbd[:, b, g, :], kT[:, g // 2, :]).then_inc(s_ready, 1)

            def transpose_probs(i, b):
                n = 4 * i + b
                for d, done in enumerate((pt0_done, pt1_done)):
                    pe.wait_ge(exp_done, 4 * n + 2 * d + 2)
                    at_least(pe, done, n)
                    for g in (2 * d, 2 * d + 1):
                        for t in range(TC):
                            o = ((g % 2) * TC + t) * P
                            last = nc.tensor.transpose(PT[d][:, o:o + P], pr[:, g, t * P:(t + 1) * P], ident)
                    last.then_inc(pt_ready, 1)

            def weigh_values(i, b):
                n = 4 * i + b
                pe.wait_ge(pt0_done, n + 1)
                pe.wait_ge(pt1_done, n + 1)
                pe.wait_ge(v_done, n + 1)
                at_least(pe, om_done, n)
                at_least(pe, rp_done, n)
                for a in range(NH):
                    for t in range(TC):
                        for g in (2 * a, 2 * a + 1):
                            r = (g % 2) * GW
                            mm(O[r:r + GW, a * P:(a + 1) * P], v[:, b % 2, t, g * GW:(g + 1) * GW], pT[:, g, t, :],
                               t == 0, t == TC - 1)
                pe.wait_ge(px_done, n + 1)
                mm(RP, px[:, :, :].rearrange("p n h -> p (n h)"), cst("sel")).then_inc(o_ready, 1)

            def transpose2(src, done):
                for a in range(NH):
                    last = nc.tensor.transpose(M2[:, a, :], src[:, a * P:(a + 1) * P], ident)
                last.then_inc(done, 1)

            def turn_z1(i):
                pe.wait_ge(z1_done, i + 1)
                transpose2(z1, z1T_ready)

            def queries(i):
                pe.wait_ge(z1T_done, i + 1)
                for a in range(NH):
                    for c in range(NH):
                        last = mm(M2[:, a, :], wq[:, c, a * P:(a + 1) * P], z1T[:, c, :], c == 0, c == NH - 1)
                last.then_inc(q_ready, 1)

            def expand(j, first=False):
                pe.wait_ge(rp_done, 4 * (j + 1))
                if first:
                    pe.wait_ge(qs_done, NH * (j + 2))
                else:
                    pe.wait_ge(chosen_done, j + 1)
                for k, e in enumerate(("er", "ep")):
                    for a in range(NH):
                        o = (k * NH + a) * P
                        last = mm(M[:, o:o + P], cst(e)[0:2 * H, a * P:(a + 1) * P], rp[:, :])
                last.then_inc(ex_ready, 1)

            def project_out(j):
                pe.wait_ge(aT_done, NH * (j + 1))
                for a in range(NH):
                    last = mm(M[:, 0:D], aT[:, a, :], wo[:, a, :], a == 0, a == NH - 1)
                last.then_inc(wo_ready, 1)

            def turn_z2(j):
                pe.wait_ge(z2_done, j + 1)
                transpose2(z2, z2T_ready)

            def project_dt(j):
                pe.wait_ge(z2T_done, j + 1)
                for a in range(NH):
                    last = mm(M[:, 0:H], z2T[:, a, :], wdt[:, a, :], a == 0, a == NH - 1)
                last.then_inc(dt_ready, 1)

            def sum_a(j):
                pe.wait_ge(a_done, j + 1)
                mm(M[:, 0:H], cst("trib"), dtv[:, 5, :]).then_inc(cum_ready, 1)

            def sum_decay(j):
                pe.wait_ge(en_done, j + 1)
                mm(M[:, 0:H], cst("trib"), dtv[:, 7, :]).then_inc(c2_ready, 1)

            def turn_y(j):
                pe.wait_ge(yn_done, j + 1)
                transpose2(yn, ynT_ready)

            def project_y(j):
                pe.wait_ge(ynT_done, j + 1)
                for a in range(NH):
                    last = mm(M[:, 0:D], ynT[:, a, :], wout[:, a, :], a == 0, a == NH - 1)
                last.then_inc(y_ready, 1)

            def turn_z3(j):
                pe.wait_ge(z3_done, j + 1)
                transpose2(z3, z3T_ready)

            def router(j):
                pe.wait_ge(z3T_done, j + 1)
                for a in range(NH):
                    last = mm(M[:, 0:E], z3T[:, a, :], wrt[:, a, :], a == 0, a == NH - 1)
                last.then_inc(lg_ready, 1)

            def rank(j):
                pe.wait_ge(mm_done, j + 1)
                at_least(pe, chosen_done, j + 1)
                mm(M[:, 0:E], cst("tris"), lg[:, 2, :], True, False)
                mm(M[:, 0:E], ones, chosen[:, :], False, True).then_inc(rank_ready, 1)

            def ssd():
                pe.wait_ge(a_done, 1)
                pe.wait_ge(norm_done, 1)
                for c in range(NC):
                    for a in range(NH):
                        last = mm(M[:, c * Q:(c + 1) * Q], wxbc[:, a, c * P:(c + 1) * P], z2T[:, a, 0:Q],
                                  a == 0, a == NH - 1)
                last.then_inc(ssd_pe, 1)
                pe.wait_ge(ssd_dve, 11)
                for a in range(NH):
                    last = mm(M[0:Q, a * 8 * Q:(a + 1) * 8 * Q], cT[:, 2 + a, :],
                              cbd[:, a, :, :].rearrange("p h l -> p (h l)"))
                last.then_inc(ssd_pe, 1)
                pe.wait_ge(ssd_act, 1)
                pe.wait_ge(ssd_dve, 12)
                mm(M[0:Q, :], cst("gt")[0:Q, :], at_[:, :, :].rearrange("p h l -> p (h l)")).then_inc(ssd_pe, 1)
                pe.wait_ge(ssd_act, 2)
                for a in range(NH):
                    last = nc.tensor.transpose(M[0:Q, a * P:(a + 1) * P], cT[:, 4 + a, :], ident)
                last.then_inc(ssd_pe, 1)
                pe.wait_ge(ssd_act, 3)
                pe.wait_ge(ssd_dve, 14)
                for h in range(H):
                    last = mm(M[:, h * HD:(h + 1) * HD], w4[:, h, :, :].rearrange("p b l -> p (b l)"),
                              xs[:, h * HD:(h + 1) * HD])
                last.then_inc(ssd_pe, 1)
                pe.wait_ge(ssd_act, 4)

            def after(j):
                expand(j), project_out(j), turn_z2(j), project_dt(j), sum_a(j), sum_decay(j)
                turn_y(j), project_y(j), turn_z3(j), router(j), rank(j)

            def tile(i, post=True, first=False, more=True):
                j = i - 1
                for b in range(TB):
                    nxt = (i, b + 1) if b < TB - 1 else (i + 1, 0)
                    ahead = b < TB - 1 or more
                    if ahead:
                        project_kv(*nxt)
                    if post and b == 0:
                        expand(j, first)
                    if post and b == 1:
                        project_dt(j)
                    if post and b == 2:
                        sum_decay(j)
                        if first:
                            ssd()
                    if post and b == 3:
                        turn_z3(j)
                    transpose_probs(i, b)
                    if post and b == 0:
                        project_out(j)
                    if more and b == 1:
                        if post:
                            pe.wait_ge(dt_done, j + 1)
                        queries(i + 1)
                    if ahead:
                        scores(*nxt)
                    if more and b == 0:
                        if post:
                            pe.wait_ge(x1_done, j + 1)
                        turn_z1(i + 1)
                    if post and b == 2:
                        turn_y(j)
                    if post and b == 3:
                        router(j)
                    weigh_values(i, b)
                    if post and b == 0:
                        if more:
                            pe.wait_ge(z1T_done, i + 2)
                        turn_z2(j)
                    if post and b == 1:
                        if more:
                            pe.wait_ge(qs_done, NH * (i + 2))
                        sum_a(j)
                    if post and b == 2:
                        project_y(j)
                    if post and b == 3:
                        rank(j)

            last_values()
            pe.wait_ge(vl_done, 1)
            turn_z1(0)
            queries(0)
            project_kv(0, 0)
            scores(0, 0)
            pe.wait_ge(qs_done, NH)
            tile(0, post=False)
            tile(1, first=True)
            with pe.Fori(2, NT - 1) as i:
                tile(i)
            tile(NT - 1, more=False)
            after(NT - 1)

        @block.scalar
        def _(act):
            def copy(out, in_, **kw):
                return nc.scalar.activation(out, in_, ACT.Copy, **kw)

            def take_keys(i, b):
                n = 4 * i + b
                at_least(act, s_ready, 4 * n)
                for a in range(NH):
                    act.wait_ge(k_ready, 2 * n + a + 1)
                    nc.scalar.activation(kT[:, a, :], KV[a][:, 0:S], ACT.Identity,
                                         bias=prm("bk")[:, a:a + 1]).then_inc(k_done, 1)

            def exponentials(i, b):
                n = 4 * i + b
                act.wait_ge(nmx_done, n + 1)
                at_least(act, px_done, n)
                at_least(act, rec_done, n)
                at_least(act, pt_ready, 2 * n)
                for g in range(NG):
                    nc.scalar.activation(pr[:, g, :], sm[:, g, :], ACT.Exp, bias=nmx[:, g:g + 1],
                                         accum_out=rsum[:, g:g + 1]).then_inc(exp_done, 1)

            def take_pt1(i, b):
                n = 4 * i + b
                act.wait_ge(pt_ready, 2 * n + 2)
                at_least(act, o_ready, n)
                copy(pT[:, 2:4, :, :].rearrange("p g t n -> p (g t n)"), PT[1][:, :]).then_inc(pt1_done, 1)

            def take_rp(i, b):
                n = 4 * i + b
                act.wait_ge(om_done, n + 1)
                if b == 0:
                    at_least(act, ex_ready, i)
                copy(rp[:, b * Q:(b + 1) * Q], RP).then_inc(rp_done, 1)

            def take2(dst, ready, done, j):
                act.wait_ge(ready, j + 1)
                copy(dst[:, :, :], M2).then_inc(done, 1)

            def take_z1T(i):
                take2(z1T, z1T_ready, z1T_done, i)

            def decays(j):
                act.wait_ge(cum_ready, j + 1)
                at_least(act, rn_done, j)
                nc.scalar.activation(dtv[:, 6, :], M[:, 0:H], ACT.Exp).then_inc(ep_done, 1)
                nc.scalar.activation(dtv[:, 7, :], M[:, 0:H], ACT.Exp, scale=-1.0).then_inc(en_done, 1)

            def soft_exp(j):
                act.wait_ge(nabs_done, j + 1)
                nc.scalar.activation(dtv[:, 2, :], dtv[:, 1, :], ACT.Exp).then_inc(u_done, 1)

            def gate_exp(j):
                act.wait_ge(diff_done, j + 1)
                nc.scalar.activation(sv[:, 1, 0:1], sv[:, 0, 0:1], ACT.Exp).then_inc(gate_e, 1)

            def ssd():
                act.wait_ge(ssd_pe, 2)
                copy(gs[:, :, :].rearrange("p h l -> p (h l)"), M[0:Q, :]).then_inc(ssd_act, 1)
                act.wait_ge(ssd_pe, 3)
                nc.scalar.activation(ls[:, :, :].rearrange("p h l -> p (h l)"), M[0:Q, :], ACT.Exp).then_inc(ssd_act, 1)
                act.wait_ge(ssd_pe, 4)
                copy(xs, M[0:Q, 0:D]).then_inc(ssd_act, 1)
                act.wait_ge(ssd_pe, 5)
                copy(y0[:, :], M[:, 0:D]).then_inc(ssd_act, 1)

            def take_z2T(j):
                take2(z2T, z2T_ready, z2T_done, j)

            def take_ynT(j):
                take2(ynT, ynT_ready, ynT_done, j)

            def take_z3T(j):
                take2(z3T, z3T_ready, z3T_done, j)

            def after(j):
                take_z2T(j), soft_exp(j), decays(j), take_ynT(j), take_z3T(j), gate_exp(j)

            def tile(i, post=True, first=False, more=True):
                j = i - 1
                for b in range(TB):
                    nxt = (i, b + 1) if b < TB - 1 else (i + 1, 0)
                    ahead = b < TB - 1 or more
                    if ahead:
                        take_keys(*nxt)
                    if post and b == 2:
                        if first:
                            ssd()
                    if post and b == 3:
                        take_z3T(j)
                    take_pt1(i, b)
                    if post and b == 1:
                        soft_exp(j)
                    if ahead:
                        exponentials(*nxt)
                    if more and b == 0:
                        take_z1T(i + 1)
                    if post and b == 2:
                        take_ynT(j)
                    take_rp(i, b)
                    if post and b == 0:
                        take_z2T(j)
                    if post and b == 1:
                        decays(j)
                    if post and b == 3:
                        gate_exp(j)

            act.wait_ge(par_in, 16)
            take_z1T(0)
            take_keys(0, 0)
            exponentials(0, 0)
            tile(0, post=False)
            tile(1, first=True)
            with act.Fori(2, NT - 1) as i:
                tile(i)
            tile(NT - 1, more=False)
            after(NT - 1)

        @block.vector
        def _(dve):
            V = nc.vector

            def take_values(i, b):
                n = 4 * i + b
                dve.wait_ge(v_ready, n + 1)
                at_least(dve, o_ready, n - 1)
                V.tensor_copy(v[:, b % 2, :, :].rearrange("p t d -> p (t d)"), KV[0][:, :]).then_inc(v_done, 1)

            def maxima(i, b):
                n = 4 * i + b
                for g in range(NG):
                    if g == 0:
                        held(dve, (init, 2), (msk_in[b], 64 * (i + 1)), (exp_done, 4 * n), (s_ready, 4 * n + 1))
                    else:
                        held(dve, (init, 2), (s_ready, 4 * n + g + 1))
                    V.tensor_tensor_reduce(sm[:, g, :], SC[g % 2][:, 0:S], msk[:, b, :], 1.0, -3.0e38, ALU.add, ALU.max,
                                           mx[:, g:g + 1]).then_inc(max_done, 1)
                dve.wait_ge(max_done, 4 * n + 4)
                V.tensor_scalar(nmx[:, :], mx[:, :], -1.0, None, ALU.mult).then_inc(nmx_done, 1)

            def take_pt0(i, b):
                n = 4 * i + b
                dve.wait_ge(pt_ready, 2 * n + 1)
                at_least(dve, o_ready, n)
                V.tensor_copy(pT[:, 0:2, :, :].rearrange("p g t n -> p (g t n)"), PT[0][:, :]).then_inc(pt0_done, 1)

            def reciprocals(i, b):
                n = 4 * i + b
                dve.wait_ge(exp_done, 4 * n + 4)
                at_least(dve, px_done, n)
                V.reciprocal(rr[:, 0, :], rsum[:, :]).then_inc(rec_done, 1)

            def take_output(i, b):
                n = 4 * i + b
                dve.wait_ge(o_ready, n + 1)
                at_least(dve, ou_done, n)
                V.tensor_tensor(om[:, :, :, :], OT, cst("hm").unsqueeze(1).unsqueeze(3).broadcast_to([P, NH, HG, Q]),
                                ALU.mult).then_inc(om_done, 1)
                dve.wait_ge(om_done, n + 1)
                V.tensor_reduce(ou[:, :, b * Q:(b + 1) * Q], om[:, :, :, :].rearrange("p a h q -> p a q h"),
                                AX.X, ALU.add).then_inc(ou_done, 1)

            def normalise(src, dst, k, j, s_st, s_mv, s_rstd, s_done):
                V.bn_stats(st[:, k, :], src).then_inc(s_st, 1)
                held(dve, (init, 2), (s_st, j + 1), (s_done, j))
                V.bn_aggr(mv[:, k, :], st[:, k, :]).then_inc(s_mv, 1)
                dve.wait_ge(s_rstd, j + 1)
                V.tensor_scalar(dst, src, mv[:, k, 0:1], rs[:, k, 1:2], ALU.subtract, ALU.mult).then_inc(s_done, 1)

            def norm1(i):
                held(dve, (init, 2), (xt_in, 16 * (i + 1)), (z1T_ready, i))
                normalise(xt[:, :], z1[:, :], 0, i, st1, mv1, rstd1, z1_done)

            def take_queries(i):
                dve.wait_ge(q_ready, i + 1)
                at_least(dve, qbd_done, 8 * i)
                for a in range(NH):
                    V.tensor_scalar(qs[:, a, :], M2[:, a, :], prm("bq")[:, a:a + 1], float(HD) ** -0.5,
                                    ALU.add, ALU.mult).then_inc(qs_done, 1)

            def attention_out(j):
                dve.wait_ge(ex_ready, j + 1)
                dve.wait_ge(ou_done, 4 * (j + 1))
                EX = M[:, :].rearrange("p (k a n) -> p k a n", k=2, a=NH)
                V.tensor_tensor(t1[:, :, :], EX[:, 0], ou[:, :, :], ALU.mult).then_inc(t_done, 1)
                V.tensor_tensor(t2[:, :, :].rearrange("p a (b q) -> p a b q", b=TB),
                                EX[:, 1].rearrange("p a (b q) -> p a b q", b=TB),
                                vl[:, :, bass.ds(TB * j, TB)].unsqueeze(3).broadcast_to([P, NH, TB, Q]),
                                ALU.mult).then_inc(t_done, 1)
                dve.wait_ge(t_done, 2 * (j + 1))
                at_least(dve, wo_ready, j)
                for a in range(NH):
                    V.scalar_tensor_tensor(aT[:, a, :], t1[:, a, :], prm("bv")[:, a:a + 1], t2[:, a, :],
                                           ALU.add, ALU.add).then_inc(aT_done, 1)

            def residual1(j):
                dve.wait_ge(wo_ready, j + 1)
                dve.wait_ge(xb_done, j + 1)
                at_least(dve, x2_done, j)
                V.tensor_tensor(x1[:, :], M[:, 0:D], xr[:, :], ALU.add).then_inc(x1_done, 1)
                held(dve, (init, 2), (x1_done, j + 1), (z2T_ready, j))
                normalise(x1[:, :], z2[:, :], 1, j, st2, mv2, rstd2, z2_done)

            def soft_in(j):
                dve.wait_ge(dt_ready, j + 1)
                V.tensor_tensor(dtv[:, 0, :], M[:, 0:H], prm("dtb"), ALU.add).then_inc(dt_done, 1)
                dve.wait_ge(dt_done, j + 1)
                V.scalar_tensor_tensor(dtv[:, 1, :], dtv[:, 0, :], -1.0, dtv[:, 0, :], ALU.mult, ALU.min
                                       ).then_inc(nabs_done, 1)

            def softplus(j):
                k = [0]

                def link(ins):
                    k[0] += 1
                    ins.then_inc(soft, 1)
                    dve.wait_ge(soft, NSOFT * j + k[0])

                u, r, y, w, s = dtv[:, 2, :], dtv[:, 3, :], dtv[:, 4, :], dtv[:, 8, :], dtv[:, 9, :]
                dve.wait_ge(u_done, j + 1)
                link(V.tensor_scalar(r, u, 2.0, None, ALU.add))
                link(V.reciprocal(s, r))
                link(V.tensor_tensor(y, u, s, ALU.mult))
                link(V.tensor_tensor(w, y, y, ALU.mult))
                link(V.tensor_scalar(s, w, 1.0 / ATANH[0], None, ALU.mult))
                for c in ATANH[1:]:
                    link(V.scalar_tensor_tensor(s, s, 1.0 / c, w, ALU.add, ALU.mult))
                link(V.scalar_tensor_tensor(s, s, 1.0, y, ALU.add, ALU.mult))
                link(V.tensor_scalar(r, dtv[:, 0, :], 0.0, None, ALU.max))
                assert k[0] == NSOFT
                V.scalar_tensor_tensor(w, s, 2.0, r, ALU.mult, ALU.add).then_inc(soft_sum, 1)
                dve.wait_ge(soft_sum, j + 1)
                at_least(dve, cum_ready, j)
                V.tensor_tensor(dtv[:, 5, :], w, prm("apar"), ALU.mult).then_inc(a_done, 1)

            def norms(j):
                dve.wait_ge(c2_ready, j + 1)
                dve.wait_ge(ep_done, j + 1)
                V.tensor_tensor(dtv[:, 8, :], M[:, 0:H], dtv[:, 6, :], ALU.mult).then_inc(norm_done, 1)
                dve.wait_ge(norm_done, j + 1)
                V.reciprocal(dtv[:, 9, :], dtv[:, 8, :]).then_inc(rn_done, 1)

            def scale_y(j):
                dve.wait_ge(rn_done, j + 1)
                at_least(dve, ynT_ready, j)
                V.tensor_tensor(yn[:, :].rearrange("p (h d) -> p h d", h=H), y0[:, :].rearrange("p (h d) -> p h d", h=H),
                                dtv[:, 9, :].unsqueeze(2).broadcast_to([P, H, HD]), ALU.mult).then_inc(yn_done, 1)

            def residual2(j):
                dve.wait_ge(y_ready, j + 1)
                V.tensor_tensor(x2[:, bass.ds(j, 1), :], M[:, 0:D].unsqueeze(1), x1[:, :].unsqueeze(1), ALU.add
                                ).then_inc(x2_done, 1)
                held(dve, (init, 2), (x2_done, j + 1), (z3T_ready, j), (z3_out, 16 * j))
                src = x2[:, bass.ds(j, 1), :].rearrange("p t d -> p (t d)")
                normalise(src, z3[:, :], 2, j, st3, mv3, rstd3, z3_done)

            def select(j):
                k = [0]

                def link(ins):
                    k[0] += 1
                    ins.then_inc(route, 1)
                    held(dve, (init, 2), (route, NROUTE * j + k[0]))

                dve.wait_ge(lg_ready, j + 1)
                V.tensor_copy(lg[:, 0, :], M[:, 0:E]).then_inc(lg_done, 1)
                held(dve, (init, 2), (lg_done, j + 1))
                link(V.max(lg[:, 1, :], lg[:, 0, :]))
                link(V.max_index(mi[:, :], lg[:, 1, :], lg[:, 0, :]))
                link(V.tensor_copy(sv[:, 2, :], mi[:, 0:TOPK]))
                V.tensor_tensor(oh[:, :, :], cst("iota8").unsqueeze(1).broadcast_to([P, TOPK, E]),
                                sv[:, 2, :].unsqueeze(2).broadcast_to([P, TOPK, E]), ALU.is_equal).then_inc(oh_done, 1)
                dve.wait_ge(oh_done, j + 1)
                at_least(dve, rank_ready, j)
                V.tensor_tensor(lg[:, 2, :], oh[:, 0, :], oh[:, 1, :], ALU.add).then_inc(mm_done, 1)
                V.tensor_tensor(sv[:, 0, 0:1], lg[:, 1, 1:2], lg[:, 1, 0:1], ALU.subtract).then_inc(diff_done, 1)
                assert k[0] == 3

            def place(j):
                k = [3]

                def link(ins):
                    k[0] += 1
                    ins.then_inc(route, 1)
                    dve.wait_ge(route, NROUTE * j + k[0])

                dve.wait_ge(rank_ready, j + 1)
                link(V.tensor_tensor(ohr[:, :, :], oh[:, :, :], M[:, 0:E].unsqueeze(1).broadcast_to([P, TOPK, E]),
                                     ALU.mult))
                V.tensor_tensor(chosen[:, :], chosen[:, :], lg[:, 2, :], ALU.add).then_inc(chosen_done, 1)
                link(V.tensor_reduce(sv[:, 3, :], ohr[:, :, :], AX.X, ALU.add))
                link(V.tensor_copy(ri[:, 0, :], sv[:, 3, :]))
                link(V.tensor_scalar(ri[:, 1, :], ri[:, 0, :], 7, None, ALU.logical_shift_right))
                link(V.tensor_copy(sv[:, 4, :], ri[:, 1, :]))
                link(V.scalar_tensor_tensor(sv[:, 5, :], sv[:, 4, :], -float(P), sv[:, 3, :], ALU.mult, ALU.add))
                link(V.scalar_tensor_tensor(sv[:, 6, :], sv[:, 5, :], float(TCOL), sv[:, 4, :], ALU.mult, ALU.add))
                link(V.scalar_tensor_tensor(sv[:, 7, :], sv[:, 2, :], float(TPE), sv[:, 6, :], ALU.mult, ALU.add))
                at_least(dve, slots_out, 32 * j)
                at_least(dve, pay_done, 5 * j)
                V.tensor_copy(ri[:, 2, :], sv[:, 7, :]).then_inc(pay_done, 1)
                V.tensor_copy(pay[:, :, 0:2], tokf[:, :].rearrange("p (k c) -> p k c", k=TOPK)).then_inc(pay_done, 1)
                gate = pay[:, :, 2:3].bitcast(F32).rearrange("p k c -> p (k c)")
                dve.wait_ge(gate_e, j + 1)
                link(V.tensor_scalar(sv[:, 4, 0:1], sv[:, 1, 0:1], 1.0, None, ALU.add))
                assert k[0] == NROUTE, k[0]
                V.reciprocal(gate[:, 0:1], sv[:, 4, 0:1]).then_inc(pay_done, 1)
                dve.wait_ge(pay_done, 5 * j + 3)
                V.tensor_tensor(gate[:, 1:2], gate[:, 0:1], sv[:, 1, 0:1], ALU.mult).then_inc(pay_done, 1)
                V.tensor_scalar(tokf[:, :], tokf[:, :], float(P), None, ALU.add).then_inc(pay_done, 1)

            def ssd():
                k = [0]

                def link(ins):
                    k[0] += 1
                    ins.then_inc(ssd_dve, 1)
                    dve.wait_ge(ssd_dve, k[0])

                dve.wait_ge(ssd_pe, 1)
                link(V.memset(xp[:, :, 0:KC - 1], 0.0))
                link(V.tensor_copy(xp[:, :, KC - 1:], M[:, 0:NC * Q].rearrange("p (c l) -> p c l", c=NC)))
                taps = prm("convw").rearrange("p (c k) -> p c k", k=KC)

                def tap(n):
                    return taps[:, :, n:n + 1].broadcast_to([P, NC, Q])

                link(V.tensor_tensor(cv[:, 0], xp[:, :, 0:Q], tap(0), ALU.mult))
                for n in range(1, KC):
                    link(V.tensor_tensor(cv[:, 1], xp[:, :, n:n + Q], tap(n), ALU.mult))
                    link(V.tensor_tensor(cv[:, 0], cv[:, 0], cv[:, 1], ALU.add))
                link(V.tensor_tensor(cT, cv[:, 0], prm("convb").unsqueeze(2).broadcast_to([P, NC, Q]), ALU.add))
                n8 = P // HD
                for a in range(NH):
                    last = V.tensor_tensor(cbd[:, a], cT[:, a, :].unsqueeze(1).broadcast_to([P, n8, Q]),
                                           cst("bm8").unsqueeze(2).broadcast_to([P, n8, Q]), ALU.mult)
                link(last)
                le = cst("le")[0:Q, :].unsqueeze(1).broadcast_to([Q, H, Q])
                link(V.tensor_tensor(at_, dtv[0:Q, 5, :].unsqueeze(2).broadcast_to([Q, H, Q]), le, ALU.mult))
                dve.wait_ge(ssd_act, 2)
                link(V.tensor_tensor(ws, gs, ls, ALU.mult))
                for h in range(H):
                    last = V.tensor_tensor(w4[:, h], ws[:, h, :].unsqueeze(1).broadcast_to([Q, TB, Q]),
                                           cst("le")[0:Q, :].unsqueeze(1).broadcast_to([Q, TB, Q]), ALU.mult)
                link(last)
                assert k[0] == 14, k[0]
                dve.wait_ge(ssd_act, 4)

            def after(j):
                attention_out(j), residual1(j), soft_in(j), softplus(j), norms(j), scale_y(j)
                residual2(j), select(j), place(j)

            def tile(i, post=True, first=False, more=True):
                j = i - 1
                for b in range(TB):
                    nxt = (i, b + 1) if b < TB - 1 else (i + 1, 0)
                    ahead = b < TB - 1 or more
                    if ahead:
                        take_values(*nxt)
                    if post and b == 0:
                        attention_out(j)
                    if post and b == 1:
                        soft_in(j)
                    if post and b == 2:
                        norms(j)
                        if first:
                            ssd()
                        scale_y(j)
                    take_pt0(i, b)
                    reciprocals(i, b)
                    if more and b == 0:
                        norm1(i + 1)
                    if more and b == 1:
                        take_queries(i + 1)
                    if ahead:
                        maxima(*nxt)
                    if post and b == 0:
                        residual1(j)
                    if post and b == 1:
                        softplus(j)
                    if post and b == 3:
                        select(j)
                    take_output(i, b)
                    if post and b == 2:
                        residual2(j)
                    if post and b == 3:
                        place(j)

            V.memset(chosen[:, :], 0.0).then_inc(chosen_done, 1)
            V.memset(pay[:, :, :].rearrange("p k c -> p (k c)"), 0).then_inc(init, 1)
            dve.wait_ge(con_in, 16)
            V.tensor_copy(tokf[:, :], cst("tok")).then_inc(init, 1)
            dve.wait_ge(init, 2)
            norm1(0)
            dve.wait_ge(vl_ready, 1)
            dve.wait_ge(par_in, 16)
            V.tensor_copy(vl[:, :, :], M2).then_inc(vl_done, 1)
            take_queries(0)
            take_values(0, 0)
            maxima(0, 0)
            tile(0, post=False)
            tile(1, first=True)
            with dve.Fori(2, NT - 1) as i:
                tile(i)
            tile(NT - 1, more=False)
            after(NT - 1)

        @block.gpsimd
        def _(pool):
            G = nc.gpsimd

            def power(k, j, s_mv, s_var, s_rstd):
                pool.wait_ge(s_mv, j + 1)
                G.tensor_tensor(rs[:, k, 0:1], mv[:, k, 1:2], cst("eps"), ALU.add).then_inc(s_var, 1)
                pool.wait_ge(s_var, j + 1)
                G.tensor_tensor(rs[:, k, 1:2], rs[:, k, 0:1], cst("nhalf"), ALU.pow).then_inc(s_rstd, 1)

            def lay_queries(i, b):
                n = 4 * i + b
                pool.wait_ge(qs_done, NH * (i + 1))
                at_least(pool, s_ready, 4 * (n - 3))
                for a in range(NH):
                    G.tensor_tensor(qbd[:, b, 2 * a:2 * a + 2, :].rearrange("p g (h q) -> p g h q", h=HG),
                                    qs[:, a, b * Q:(b + 1) * Q].unsqueeze(1).unsqueeze(1).broadcast_to([P, 2, HG, Q]),
                                    cst("bm").rearrange("p (g h) -> p g h", g=2).unsqueeze(3)
                                    .broadcast_to([P, 2, HG, Q]), ALU.mult).then_inc(qbd_done, 1)

            def last_probs(i, b):
                n = 4 * i + b
                pool.wait_ge(rec_done, n + 1)
                G.tensor_tensor(rr[:, 1, :], pr[:, :, LAST], rr[:, 0, :], ALU.mult).then_inc(pl_done, 1)
                pool.wait_ge(pl_done, n + 1)
                at_least(pool, o_ready, n)
                G.tensor_tensor(px[:, :, :], rr[:, :, :].rearrange("p k g -> p (k g)").unsqueeze(2)
                                .broadcast_to([P, 2 * NG, HG]),
                                cst("dm").unsqueeze(1).broadcast_to([P, 2 * NG, HG]), ALU.mult).then_inc(px_done, 1)

            def add_bias(j):
                pool.wait_ge(xr_in, 16 * (j + 1))
                G.tensor_tensor(xr[:, :], xr[:, :], prm("bo"), ALU.add).then_inc(xb_done, 1)

            def write_slots(j):
                held(pool, (con_in, 16), (pay_done, 5 * j + 5))
                for k in range(TOPK):
                    G.indirect_dma_start(table[:, :], bass.IndirectOffsetOnAxis(ri[:, 2, k:k + 1].bitcast(U32), 0),
                                         pay[:, k, :], None).then_inc(slots_out, 16)

            def after(j):
                add_bias(j), power(1, j, mv2, var2, rstd2), power(2, j, mv3, var3, rstd3), write_slots(j)

            def tile(i, post=True, more=True):
                j = i - 1
                for b in range(TB):
                    if post and b == 0:
                        add_bias(j)
                    last_probs(i, b)
                    if more and b == 0:
                        power(0, i + 1, mv1, var1, rstd1)
                    if post and b == 0:
                        power(1, j, mv2, var2, rstd2)
                    if more and b == 1:
                        lay_queries(i + 1, 0)
                    if more and b == 2:
                        lay_queries(i + 1, 1)
                        lay_queries(i + 1, 2)
                    if post and b == 2:
                        power(2, j, mv3, var3, rstd3)
                    if more and b == 3:
                        lay_queries(i + 1, 3)
                    if post and b == 3:
                        write_slots(j)

            pool.wait_ge(con_in, 16)
            pool.wait_ge(par_in, 16)
            power(0, 0, mv1, var1, rstd1)
            for b in range(TB):
                lay_queries(0, b)
            tile(0, post=False)
            pool.wait_ge(pad_in, 16)
            with pool.Fori(1, NT - 1) as i:
                tile(i)
            tile(NT - 1, more=False)
            after(NT - 1)
            pool.wait_ge(slots_out, 32 * NT)


def experts(nc, zbuf, table, ybuf, wdd, outd, cst, wg, wu, x2, chosen, w_in):
    own = ExitStack()
    with own:
        def sb(name, shape, dt=F32):
            return own.enter_context(nc.sbuf_tensor(name, shape, dt))

        def sem(name):
            return own.enter_context(nc.semaphore(name))

        ident, ones = cst("ident"), cst("ones")
        wd = sb("wd", [P, E, FC, D])
        tab = sb("tab", [P, TCOL, 4], I32)
        info = sb("info", [P, 2, NSLOT], I32)
        cnt = sb("cnt", [P, 5, E])
        cnti = sb("cnti", [P, E], I32)
        past = sb("past", [P, 2, NSLOT, E])
        tl = sb("tl", [P, 5, NSLOT])
        gi = sb("gi", [P, 2, 4], I32)
        oi = sb("oi", [P, 2, 4], I32)
        zg = sb("zg", [P, 2, D])
        zT = sb("zT", [P, 2, NH, P])
        sg = sb("sg", [P, 2, FH])
        hb = sb("hb", [P, F])
        hT = sb("hT", [P, FC, P])
        yb = sb("yb", [P, 2, D])
        CH = 2
        ysum = sb("ysum", [P, 2, TOPK, CH, D])
        GB = own.enter_context(nc.psum_tensor("gate_p", [P, 2, 512], F32))
        UB = own.enter_context(nc.psum_tensor("up_p", [P, 2, 512], F32))
        HB = [own.enter_context(nc.psum_tensor(f"ht_p{k}", [P, 512], F32)) for k in range(2)]
        YB = own.enter_context(nc.psum_tensor("y_p", [P, 512], F32))
        ZB = own.enter_context(nc.psum_tensor("z_p", [P, 512], F32))

        wd_in, tab_in = sem("wd_in"), sem("tab_in")
        cnt_ready, plan, info_done = sem("cnt_ready"), sem("plan"), sem("info_done")
        gi_done, oi_done = sem("gi_done"), sem("oi_done")
        zg_in = [sem(f"zg_in{s}") for s in range(2)]
        y_out = [sem(f"y_out{s}") for s in range(2)]
        zT_ready, zT_done = sem("zT_ready"), sem("zT_done")
        g_ready, u_ready, silu_done, h_done = sem("g_ready"), sem("u_ready"), sem("silu_done"), sem("h_done")
        hT_ready, hT0_done, hT1_done = sem("hT_ready"), sem("hT0_done"), sem("hT1_done")
        y_ready, y_done = sem("y_ready"), sem("y_done")
        ys_in = [sem(f"ys_in{s}") for s in range(2)]
        add1, add2, outs = sem("add1"), sem("add2"), sem("outs")
        NCH = NT // CH

        block = own.enter_context(nc.Block())

        def tiles(eng, body):
            body(0, 0, first=True)
            with eng.Fori(1, NSLOT - 1, 2) as t:
                body(t, 1)
                body(t + 1, 0)
            body(NSLOT - 1, 1, last=True)

        @block.sync
        def _(sp):
            sp.dma_start(tab[:, :, :], table.rearrange("(p n) c -> p n c", p=P)).then_inc(tab_in, 16)
            for e in range(E):
                sp.dma_start(wd[:, e], wdd[:, e]).then_inc(wd_in, 16)
            for s in range(2):
                sp.wait_ge(y_out[s], 16 * (NSLOT // 2))
            for c in range(NCH):
                if c >= 2:
                    sp.wait_ge(add2, c - 1)
                for k in range(TOPK):
                    rows = ybuf[k * TOK + c * CH * P:k * TOK + (c + 1) * CH * P, :]
                    sp.dma_start(ysum[:, c % 2, k], rows.rearrange("(t p) d -> p t d", p=P)).then_inc(ys_in[c % 2], 16)

        @block.tensor
        def _(pe):
            def mm(out, lhsT, rhs, start=True, stop=True):
                return nc.tensor.matmul(out, lhsT, rhs, start=start, stop=stop)

            def turn_z(t, s):
                pe.wait_ge(zg_in[s], 16 * (t // 2 + 1) if isinstance(t, int) else 16 * ((t - s) // 2 + 1))
                at_least(pe, zT_done, t)
                for a in range(NH):
                    last = nc.tensor.transpose(ZB[:, a * P:(a + 1) * P], zg[:, s, a * P:(a + 1) * P], ident)
                last.then_inc(zT_ready, 1)

            def expert_of(t):
                return nc.tensor.value_load(info[0:1, 1, bass.ds(t, 1)], min_val=0, max_val=E - 1)

            def up(t, s):
                e = expert_of(t)
                pe.wait_ge(zT_done, t + 1)
                for bank, w, free, done in ((GB, wg, silu_done, g_ready), (UB, wu, h_done, u_ready)):
                    at_least(pe, free, t)
                    for f in range(2):
                        for c in range(NH):
                            last = mm(bank[:, f, 0:FH], zT[:, s, c, :],
                                      w[:, bass.ds(e, 1), c, f * FH:(f + 1) * FH].rearrange("p o n -> p (o n)"),
                                      c == 0, c == NH - 1)
                    last.then_inc(done, 1)

            def turn_h(t):
                pe.wait_ge(h_done, t + 1)
                for k in range(2):
                    at_least(pe, (hT0_done, hT1_done)[k], t if k == 0 else 2 * t)
                    for c in range(4 * k, min(4 * k + 4, FC)):
                        n = P if c < FC - 1 else FL
                        last = nc.tensor.transpose(HB[k][0:n, (c % 4) * P:(c % 4 + 1) * P], hb[:, c * P:c * P + n], ident)
                    last.then_inc(hT_ready, 1)

            def down(t):
                e = expert_of(t)
                pe.wait_ge(hT0_done, t + 1)
                pe.wait_ge(hT1_done, 2 * t + 2)
                at_least(pe, y_done, t)
                for c in range(FC):
                    n = P if c < FC - 1 else FL
                    last = mm(YB[:, 0:D], hT[0:n, c, :], wd[0:n, bass.ds(e, 1), c, :].rearrange("p o n -> p (o n)"),
                              c == 0, c == FC - 1)
                last.then_inc(y_ready, 1)

            def body(t, s, first=False, last=False):
                if first:
                    turn_z(t, s)
                else:
                    turn_h(t - 1)
                if not last:
                    turn_z(t + 1, 1 - s)
                up(t, s)
                if not first:
                    down(t - 1)

            mm(YB[:, 0:E], ones, chosen[:, :]).then_inc(cnt_ready, 1)
            pe.wait_ge(info_done, 2)
            pe.wait_ge(w_in, 16 * 2 * E)
            pe.wait_ge(wd_in, 16 * E)
            tiles(pe, body)
            turn_h(NSLOT - 1)
            down(NSLOT - 1)

        @block.scalar
        def _(act):
            def silu(t):
                act.wait_ge(g_ready, t + 1)
                at_least(act, h_done, t)
                nc.scalar.activation(sg[:, :, :], GB[:, :, 0:FH], ACT.Silu).then_inc(silu_done, 1)

            def take_h0(t):
                act.wait_ge(hT_ready, 2 * t + 1)
                at_least(act, y_ready, t)
                nc.scalar.activation(hT[:, 0:4, :].rearrange("p c n -> p (c n)"), HB[0][:, :], ACT.Copy
                                     ).then_inc(hT0_done, 1)

            def take_y(t, s):
                act.wait_ge(y_ready, t + 1)
                act.wait_ge(oi_done, t + 1)
                nc.scalar.activation(yb[:, s, :], YB[:, 0:D], ACT.Copy, scale=oi[:, s, 2:3].bitcast(F32)
                                     ).then_inc(y_done, 1)

            def body(t, s, first=False, last=False):
                if not first:
                    take_h0(t - 1)
                silu(t)
                if not first:
                    take_y(t - 1, 1 - s)

            tiles(act, body)
            take_h0(NSLOT - 1)
            take_y(NSLOT - 1, 1)
            for c in range(NCH):
                act.wait_ge(add2, c + 1)
                act.dma_start(outd[c * CH * P:(c + 1) * CH * P, :].rearrange("(t p) d -> p t d", p=P),
                              x2[:, c * CH:(c + 1) * CH, :]).then_inc(outs, 16)
            act.wait_ge(outs, 16 * NCH)

        @block.vector
        def _(dve):
            V = nc.vector
            k = [0]

            def link(ins):
                k[0] += 1
                ins.then_inc(plan, 1)
                dve.wait_ge(plan, k[0])

            dve.wait_ge(cnt_ready, 1)
            link(V.tensor_scalar(cnti[:, :], YB[:, 0:E], float(P - 1), None, ALU.add))
            link(V.tensor_scalar(cnti[:, :], cnti[:, :], 7, None, ALU.logical_shift_right))
            link(V.tensor_copy(cnt[:, 0, :], cnti[:, :]))
            link(V.tensor_tensor_scan(cnt[:, 1, :], ones[:, 0:E], cnt[:, 0, :], 0.0, ALU.mult, ALU.add))
            number = cst("iotat")
            link(V.tensor_tensor(past[:, 0], number.unsqueeze(2).broadcast_to([P, NSLOT, E]),
                                 cnt[:, 1, :].unsqueeze(1).broadcast_to([P, NSLOT, E]), ALU.is_ge))
            link(V.tensor_tensor(past[:, 1], past[:, 0], cnt[:, 0, :].unsqueeze(1).broadcast_to([P, NSLOT, E]), ALU.mult))
            link(V.tensor_reduce(tl[:, 0, :], past[:, 0], AX.X, ALU.add))
            link(V.tensor_reduce(tl[:, 1, :], past[:, 1], AX.X, ALU.add))
            link(V.tensor_tensor(tl[:, 2, :], number, tl[:, 1, :], ALU.subtract))
            link(V.scalar_tensor_tensor(tl[:, 3, :], tl[:, 0, :], float(TPE), tl[:, 2, :], ALU.mult, ALU.add))
            link(V.tensor_scalar(tl[:, 4, :], tl[:, 0, :], float(E - 1), None, ALU.min))
            V.tensor_copy(info[:, 0, :], tl[:, 3, :]).then_inc(info_done, 1)
            V.tensor_copy(info[:, 1, :], tl[:, 4, :]).then_inc(info_done, 1)

            def take_z(t, s):
                dve.wait_ge(zT_ready, t + 1)
                at_least(dve, u_ready, t - 1)
                V.tensor_copy(zT[:, s, :, :].rearrange("p a n -> p (a n)"), ZB[:, 0:NH * P]).then_inc(zT_done, 1)

            def gate_up(t):
                dve.wait_ge(silu_done, t + 1)
                dve.wait_ge(u_ready, t + 1)
                at_least(dve, hT_ready, 2 * t)
                V.tensor_tensor(hb[:, :].rearrange("p (f n) -> p f n", f=2), sg[:, :, :], UB[:, :, 0:FH], ALU.mult
                                ).then_inc(h_done, 1)

            def take_h1(t):
                dve.wait_ge(hT_ready, 2 * t + 2)
                at_least(dve, y_ready, t)
                V.tensor_copy(hT[:, 4, :], HB[1][:, 0:P]).then_inc(hT1_done, 1)
                V.tensor_copy(hT[0:FL, 5, :], HB[1][0:FL, P:2 * P]).then_inc(hT1_done, 1)

            def body(t, s, first=False, last=False):
                if first:
                    take_z(t, s)
                else:
                    take_h1(t - 1)
                if not last:
                    take_z(t + 1, 1 - s)
                gate_up(t)

            tiles(dve, body)
            take_h1(NSLOT - 1)
            for c in range(NCH):
                dve.wait_ge(ys_in[c % 2], 16 * TOPK * (c // 2 + 1))
                x = x2[:, c * CH:(c + 1) * CH, :]
                V.tensor_tensor(x, x, ysum[:, c % 2, 0], ALU.add).then_inc(add1, 1)
                dve.wait_ge(add1, c + 1)
                V.tensor_tensor(x, x, ysum[:, c % 2, 1], ALU.add).then_inc(add2, 1)

        @block.gpsimd
        def _(pool):
            G = nc.gpsimd

            def owners(dst, t, done):
                col = G.value_load(info[0:1, 0, bass.ds(t, 1)], min_val=0, max_val=TCOL - 1)
                G.tensor_copy(dst.unsqueeze(1), tab[:, bass.ds(col, 1), :]).then_inc(done, 1)
                held(pool, (tab_in, 16), (done, t + 1))

            def gather(t, s):
                at_least(pool, zT_ready, t - 1)
                owners(gi[:, s, :], t, gi_done)
                G.indirect_dma_start(zg[:, s, :], None, zbuf[:, :],
                                     bass.IndirectOffsetOnAxis(gi[:, s, 0:1].bitcast(U32), 0)).then_inc(zg_in[s], 16)

            def scatter(t, s):
                if not isinstance(t, int) or t >= 2:
                    pool.wait_ge(y_out[s], 16 * (t // 2) if isinstance(t, int) else 16 * ((t - s) // 2))
                owners(oi[:, s, :], t, oi_done)
                pool.wait_ge(y_done, t + 1)
                G.indirect_dma_start(ybuf[:, :], bass.IndirectOffsetOnAxis(oi[:, s, 1:2].bitcast(U32), 0),
                                     yb[:, s, :], None).then_inc(y_out[s], 16)

            def body(t, s, first=False, last=False):
                if not last:
                    gather(t + 2, s) if not isinstance(t, int) or t + 2 < NSLOT else None
                if not first:
                    scatter(t - 1, 1 - s)

            pool.wait_ge(info_done, 2)
            pool.wait_ge(tab_in, 16)
            gather(0, 0)
            gather(1, 1)
            body(0, 0, first=True)
            body(1, 1)
            body(2, 0)
            with pool.Fori(3, NSLOT - 3, 2) as t:
                body(t, 1)
                body(t + 1, 0)
            body(NSLOT - 3, 1)
            body(NSLOT - 2, 0, last=True)
            body(NSLOT - 1, 1, last=True)
            scatter(NSLOT - 1, 1)


def kernel(**inputs):
    import numpy as np
    import concourse.bacc as bacc
    from concourse.bass_utils import run_bass_kernel_spmd as run

    a = {k: np.asarray(v) for k, v in inputs.items()}

    def rows(w):
        return np.ascontiguousarray(w.reshape(-1, P, w.shape[1]).transpose(1, 0, 2)).reshape(P, -1)

    def wide(x):
        return np.broadcast_to(x.reshape(1, -1), (P, x.size))

    w_in = a["L0_attn_W_in"].T
    packed = dict(wq=rows(a["L0_xattn_Wq"].T), wk=rows(a["L0_xattn_Wk"].T), wv=rows(a["L0_xattn_Wv"].T),
                  wo=rows(a["L0_xattn_Wo"].T), wxbc=rows(w_in[:, :3 * D]), wdt=rows(w_in[:, 3 * D:]),
                  wout=rows(a["L0_attn_W_out"].T), wrt=rows(a["L0_ffn_w_router"].T),
                  bq=a["L0_xattn_bq"].reshape(NH, P).T, bk=a["L0_xattn_bk"].reshape(NH, P).T,
                  bv=a["L0_xattn_bv"].reshape(NH, P).T, bo=wide(a["L0_xattn_bo"]), convw=rows(a["L0_attn_conv_w"]),
                  convb=a["L0_attn_conv_b"].reshape(NC, P).T, apar=wide(a["L0_attn_A_param"]),
                  dtb=wide(a["L0_attn_dt_bias"]))
    par = np.concatenate([packed[n] for n in PARAMS], axis=1)

    p, f32 = np.arange(P)[:, None], np.float32
    ch, q = np.arange(D)[None], np.arange(Q)[None]
    m = np.arange(P)[None]
    const = dict(ident=p == m, sel=p % Q == q, hm=p // HD % HG == np.arange(HG),
                 bm=p // HD == np.arange(2 * HG), dm=p // Q == np.arange(HG), er=ch // HD == p,
                 ep=ch // HD == p - H, trib=(p // Q == m // Q) & (p <= m), tris=p < m, ones=p + m >= 0,
                 gt=p > q, le=p <= q, bm8=p // HD == np.arange(P // HD), iota8=p * 0 + np.arange(E),
                 iotat=p * 0 + np.arange(NSLOT), tok=p + np.array([0, 0, 0, TOK]), nhalf=p * 0 - 0.5,
                 eps=p * 0 + EPS)
    con = np.concatenate([const[n].astype(f32) for n in CONSTS], axis=1)
    pad = np.zeros((P, TCOL, 4), np.int32)
    pad[:, :, 1] = TOPK * TOK + np.arange(TCOL) * P + p

    ctx = a["ctx_1024"]
    ctxT = np.zeros((P, B, NH, SP), ctx.dtype)
    ctxT[..., :S] = ctx.transpose(2, 0, 1).reshape(NH, P, B, S).transpose(1, 2, 0, 3)
    down = np.zeros((E, FC * P, D), ctx.dtype)
    down[:, :F] = a["L0_ffn_w_down"]

    def cols(w):
        return w.reshape(E, -1, P, w.shape[2]).transpose(2, 0, 1, 3)

    arrays = dict(x=a["x"].reshape(TOK, D), ctx=ctxT, ctx_last=ctxT[:, :, :, LAST].transpose(0, 2, 1),
                  mask=a["mask_BxSxS2_ff0"], par=par, con=con, pad=pad.reshape(P, -1),
                  wg=cols(a["L0_ffn_w_gate"]), wu=cols(a["L0_ffn_w_up"]), wd=cols(down))
    arrays = {f"in_{k}": np.ascontiguousarray(v) for k, v in arrays.items()}
    nc = bacc.Bacc("TRN2", target_bir_lowering=False, num_devices=1)
    aps = [nc.dram_tensor(k, v.shape, mybir.dt.from_np(v.dtype), kind="ExternalInput").ap() for k, v in arrays.items()]
    out = nc.dram_tensor("out", (TOK, D), F32, kind="ExternalOutput").ap()
    perceiver(nc, *aps, out)
    r = run(nc, [arrays], core_ids=[0])
    return r.results[0]["out"].reshape(B, Q, D)
```

```python
import concourse.bass as bass
from concourse import mybir
from contextlib import ExitStack

F32 = mybir.dt.float32
F32R = mybir.dt.float32r
I32 = mybir.dt.int32
U32 = mybir.dt.uint32
ALU = mybir.AluOpType
ACT = mybir.ActivationFunctionType
AX = mybir.AxisListType

P = 128
B, Q, S, D = 128, 32, 257, 256
H, HD = 16, 16
E, F, TOPK = 8, 704, 2
NH = D // P
SP = S + 1
TB = P // Q
NT = B * Q // P
TOK = B * Q
HG = P // Q
NG = H // HG
GW = HG * HD
TC = 2
LAST = TC * P
KC = 4
NC = 3 * D // P
EPS = 1e-5
FC = (F + P - 1) // P
FL = F - (FC - 1) * P
FH = F // 2
NSLOT = (TOK * TOPK + E * (P - 1)) // P + 1
NSLOT += NSLOT % 2
TPE = TOK // P
TCOL = (E + 1) * TPE
ATANH = [2 * k + 1 for k in range(7, 0, -1)]

PARAMS = dict(wq=NH * D, wk=NH * D, wv=NH * D, wo=NH * D, wdt=NH * H, wout=NH * D,
              wrt=NH * E, bq=NH, bk=NH, bv=NH, bo=D, convw=NC * KC, convb=NC, apar=H, dtb=H)
CONSTS = dict(ident=P, sel=Q, hm=HG, bm=2 * HG, dm=HG, er=D, ep=D, trib=P, tris=P, ones=P, gt=Q, le=Q,
              bm8=P // HD, iota8=E, iotat=NSLOT, tok=2 * TOPK, nhalf=1, eps=1)


def columns(widths):
    at, out = 0, {}
    for name, w in widths.items():
        out[name] = (at, at + w)
        at += w
    return out, at


PCOL, NPAR = columns(PARAMS)
CCOL, NCON = columns(CONSTS)


def held(eng, met, *waits):
    for _, value in waits:
        if not isinstance(value, int):
            eng.compute_val(value)
    eng.wait_ge(*met)
    for sem, value in waits:
        at_least(eng, sem, value)


def at_least(eng, sem, value):
    if not isinstance(value, int) or value > 0:
        eng.wait_ge(sem, value)


def perceiver(nc, xd, ctxd, ctxl, maskd, pard, wxbcd, cond, padd, wgd, wud, wdd, outd):
    zbuf = nc.dram_tensor("zbuf", (TOK, D), F32).ap()
    table = nc.dram_tensor("slot_table", (P * TCOL, 4), I32).ap()
    keep = ExitStack()
    with keep:
        con = keep.enter_context(nc.sbuf_tensor("con", [P, NCON], F32))
        wg = keep.enter_context(nc.sbuf_tensor("wg", [P, E, NH, F], F32))
        wu = keep.enter_context(nc.sbuf_tensor("wu", [P, E, NH, F], F32))
        wd = keep.enter_context(nc.sbuf_tensor("wd", [P, E, FC, D], F32))
        chosen = keep.enter_context(nc.sbuf_tensor("chosen", [P, E], F32))
        w_in = keep.enter_context(nc.semaphore("w_in"))
        wd_in = keep.enter_context(nc.semaphore("wd_in"))

        def cst(name):
            a, b = CCOL[name]
            return con[:, a:b]

        attend(nc, xd, ctxd, ctxl, maskd, pard, wxbcd, cond, padd, wgd, wud, wdd, zbuf, table, outd, con, cst, wg, wu, wd,
               chosen, w_in, wd_in)
        experts(nc, zbuf, table, outd, cst, wg, wu, wd, chosen, w_in, wd_in)


def runs(i):
    return not isinstance(i, int) or 0 <= i < NT


def attend(nc, xd, ctxd, ctxl, maskd, pard, wxbcd, cond, padd, wgd, wud, wdd, zbuf, table, outd, con, cst, wg, wu, wd,
           chosen, w_in, wd_in):
    own = ExitStack()
    with own:
        def sb(name, shape, dt=F32):
            return own.enter_context(nc.sbuf_tensor(name, shape, dt))

        def ps(name):
            return own.enter_context(nc.psum_tensor(name, [P, 512], F32))

        def sem(name):
            return own.enter_context(nc.semaphore(name))

        par = sb("par", [P, NPAR])

        def prm(name):
            a, b = PCOL[name]
            return par[:, a:b]

        def halves(name):
            return prm(name).rearrange("p (a n) -> p a n", a=NH)

        wq, wk, wv, wo = (halves(n) for n in ("wq", "wk", "wv", "wo"))
        wdt, wout, wrt = (halves(n) for n in ("wdt", "wout", "wrt"))
        ident, ones = cst("ident"), cst("ones")

        room = wd[:, :, :, :].rearrange("p e c d -> p (e c d)")
        used = [0]

        def part(n):
            used[0] += n
            assert used[0] <= E * FC * D
            return room[:, used[0] - n:used[0]]

        ctx = part(TB * NH * SP).rearrange("p (b c t) -> p b c t", b=TB, c=NH)
        ctx_hi = sb("ctx_hi", [P, 2, NH, SP], F32R)
        ctx_lo = sb("ctx_lo", [P, 2, NH, SP], F32R)
        wkh, wvh = sb("wkh", [P, NH, D], F32R), sb("wvh", [P, NH, D], F32R)
        wkl, wvl = sb("wkl", [P, NH, D], F32R), sb("wvl", [P, NH, D], F32R)
        msk = part(TB * S).rearrange("p (b t) -> p b t", b=TB)
        qbd = [sb(f"qbd_{h}", [P, 2, NG, P], F32R) for h in ("hi", "lo")]
        kT = [sb(f"kT_{h}", [P, NH, SP], F32R) for h in ("hi", "lo")]
        v = part(2 * TC * D).rearrange("p (b t d) -> p b t d", b=2, t=TC)
        sm = part(NG * S).rearrange("p (g t) -> p g t", g=NG)
        pr = part(NG * S).rearrange("p (g t) -> p g t", g=NG)
        pT = part(NG * TC * P).rearrange("p (g t n) -> p g t n", g=NG, t=TC)
        mx = sb("mx", [P, NG])
        nmx = sb("nmx", [P, NG])
        rsum = sb("rsum", [P, NG])
        rr = sb("rr", [P, 2, NG])
        px = sb("px", [P, 2 * NG, HG])
        om = sb("om", [P, NH, HG, Q])
        ou = sb("ou", [P, NH, P])
        rp = sb("rp", [2 * H, P])
        vl = sb("vl", [P, NH, B])
        kl = part(NH * B).rearrange("p (a n) -> p a n", a=NH)
        kl_parts = [sb(f"kl_{h}", [P, NH, B], F32R) for h in ("hi", "lo")]
        xt, z1 = part(D), part(D)
        z1T, qs = (part(NH * P).rearrange("p (a n) -> p a n", a=NH) for _ in range(2))
        q_parts = [sb(f"q_{h}", [P, NH, P], F32R) for h in ("hi", "lo")]
        xr, t1, t2, aT = sb("xr", [P, D]), sb("t1", [P, NH, P]), sb("t2", [P, NH, P]), sb("aT", [P, NH, P])
        x1, z2, z2T, yn = sb("x1", [P, D]), sb("z2", [P, D]), sb("z2T", [P, NH, P]), sb("yn", [P, D])
        ynT, z3, z3T = sb("ynT", [P, NH, P]), sb("z3", [P, D]), sb("z3T", [P, NH, P])
        y0, xk, x2 = sb("y0", [P, D]), sb("xk", [P, D]), sb("x2", [P, D])
        st = sb("st", [P, 3, 6])
        mv = sb("mv", [P, 3, 2])
        rs = sb("rs", [P, 3, 2])
        dtv = sb("dtv", [P, 11, H])
        lg = sb("lg", [P, 4, E])
        mi = sb("mi", [P, 8], U32)
        oh = sb("oh", [P, TOPK, E])
        ohr = sb("ohr", [P, TOPK, E])
        sv = sb("sv", [P, 8, TOPK])
        ri = sb("ri", [P, 3, TOPK], I32)
        pay = sb("pay", [P, TOPK, 4], I32)
        tokf = sb("tokf", [P, 2 * TOPK])
        spare = wg[:, :, :, :].rearrange("p e c n -> p (e c n)")
        cut = [0]

        def carve(n):
            cut[0] += n
            assert cut[0] <= E * NH * F
            return spare[:, cut[0] - n:cut[0]]

        wxbc = carve(NH * 3 * D).rearrange("p (a n) -> p a n", a=NH)
        ctl = carve(NH * B).rearrange("p (a n) -> p a n", a=NH)
        xp = carve(NC * (Q + KC - 1)).rearrange("p (c l) -> p c l", c=NC)
        cv = carve(2 * NC * Q).rearrange("p (k c l) -> p k c l", k=2, c=NC)
        cT = carve(NC * Q).rearrange("p (c l) -> p c l", c=NC)
        cbd = carve(NH * 8 * Q).rearrange("p (a h l) -> p a h l", a=NH, h=8)
        gs, at_, ls, ws = (carve(H * Q)[0:Q].rearrange("p (h l) -> p h l", h=H) for _ in range(4))
        w4 = carve(H * P)[0:Q].rearrange("p (h b l) -> p h b l", h=H, b=TB)
        xs = carve(D)[0:Q]

        K, V_ = ps("k"), ps("v_p")
        K2 = K[:, 0:NH * LAST].rearrange("p (a t) -> p a t", a=NH)
        SC = [ps("sc0"), ps("sc1")]
        PT = [ps("pt0"), ps("pt1")]
        O = ps("o")
        M = ps("m")
        OT = O[:, 0:NH * P].rearrange("p (a h q) -> p a h q", a=NH, h=HG)
        RP = O[0:2 * H, NH * P:NH * P + Q]
        M2 = M[:, 0:NH * P].rearrange("p (a n) -> p a n", a=NH)
        M2K = M[:, NH * P:2 * NH * P].rearrange("p (a n) -> p a n", a=NH)
        RK = M[:, 2 * H:2 * H + E]

        par_in, con_in, ctl_in, pad_in = sem("par_in"), sem("con_in"), sem("ctl_in"), sem("pad_in")
        wxbc_in = sem("wxbc_in")
        hi_done, lo_done, wh_done, wl_done = sem("hi_done"), sem("lo_done"), sem("wh_done"), sem("wl_done")
        ctx_in = [sem(f"ctx_in{b}") for b in range(TB)]
        msk_in = [sem(f"msk_in{b}") for b in range(TB)]
        xt_in, xr_in, z3_out, slots_out = sem("xt_in"), sem("xr_in"), sem("z3_out"), sem("slots_out")
        x2_out, blank_out = sem("x2_out"), sem("blank_out")
        vl_ready, vl_done, kl_sum, kl_high, kl_low, lows_done, q_high = (
            sem("vl_ready"), sem("vl_done"), sem("kl_sum"), sem("kl_high"), sem("kl_low"), sem("lows_done"),
            sem("q_high"))
        q_split = sem("q_split")
        k_ready, k_done, v_ready, v_done = sem("k_ready"), sem("k_done"), sem("v_ready"), sem("v_done")
        s_ready, max_done, nmx_done, exp_done = sem("s_ready"), sem("max_done"), sem("nmx_done"), sem("exp_done")
        pt_ready, pt_done = sem("pt_ready"), sem("pt_done")
        rec_done, pl_done, px_done = sem("rec_done"), sem("pl_done"), sem("px_done")
        o_ready, om_done, ou_done, rp_done = sem("o_ready"), sem("om_done"), sem("ou_done"), sem("rp_done")
        st1, mv1, var1, rstd1, z1_done = sem("st1"), sem("mv1"), sem("var1"), sem("rstd1"), sem("z1_done")
        z1T_ready, z1T_done, q_ready, qs_done, qbd_done = (sem("z1T_ready"), sem("z1T_done"), sem("q_ready"),
                                                           sem("qs_done"), sem("qbd_done"))
        ex_ready, t_done, t3_done, aT_done = sem("ex_ready"), sem("t_done"), sem("t3_done"), sem("aT_done")
        wo_ready, xb_done, x1_done, kept = sem("wo_ready"), sem("xb_done"), sem("x1_done"), sem("kept")
        st2, mv2, var2, rstd2, z2_done = sem("st2"), sem("mv2"), sem("var2"), sem("rstd2"), sem("z2_done")
        z2T_ready, z2T_done = sem("z2T_ready"), sem("z2T_done")
        dt_ready, dt_done, nabs_done, u_done, soft, a_done = (sem("dt_ready"), sem("dt_done"), sem("nabs_done"),
                                                              sem("u_done"), sem("soft"), sem("a_done"))
        cum_ready, ep_done, en_done, c2_ready = sem("cum_ready"), sem("ep_done"), sem("en_done"), sem("c2_ready")
        norm_done, rn_done, yn_done = sem("norm_done"), sem("rn_done"), sem("yn_done")
        ynT_ready, ynT_done, y_ready, x2_done = sem("ynT_ready"), sem("ynT_done"), sem("y_ready"), sem("x2_done")
        st3, mv3, var3, rstd3, z3_done = sem("st3"), sem("mv3"), sem("var3"), sem("rstd3"), sem("z3_done")
        z3T_ready, z3T_done, lg_ready, lg_done = sem("z3T_ready"), sem("z3T_done"), sem("lg_ready"), sem("lg_done")
        top_done, index_done, expert_done, oh_done, mm_done, diff_done, gate_e = (
            sem("top_done"), sem("index_done"), sem("expert_done"), sem("oh_done"), sem("mm_done"), sem("diff_done"),
            sem("gate_e"))
        ranked, rank_done, gate_sum, whole, col_done, row_a, row_b = (
            sem("ranked"), sem("rank_done"), sem("gate_sum"), sem("whole"), sem("col_done"), sem("row_a"), sem("row_b"))
        pay_done, chosen_done = sem("pay_done"), sem("chosen_done")
        ssd_pe, ssd_act, ssd_dve = sem("ssd_pe"), sem("ssd_act"), sem("ssd_dve")
        init, soft_sum, soft_max = sem("init"), sem("soft_sum"), sem("soft_max")
        NSOFT = len(ATANH) + 5

        block = own.enter_context(nc.Block())

        def steps(eng, tile):
            for i in range(4):
                tile(i)
            with eng.Fori(4, NT - 3) as i:
                tile(i)
            for i in range(NT - 3, NT + 3):
                tile(i)

        def following(i, b, by=1):
            return i + (b + by) // TB, (b + by) % TB

        @block.sync
        def _(sp):
            def load_ctx(i, b):
                if not (isinstance(i, int) and i == 0):
                    sp.wait_ge(lo_done, 4 * i + b - 3)
                sp.dma_start(ctx[:, b:b + 1], ctxd[:, bass.ds(4 * i + b, 1), :, :]).then_inc(ctx_in[b], 16)

            def load_mask(i, b):
                if not (isinstance(i, int) and i == 0):
                    sp.wait_ge(max_done, 4 * (4 * i + b - 3))
                for h in range(HG):
                    sp.dma_start(msk[h * Q:(h + 1) * Q, b:b + 1, :],
                                 maskd[bass.ds(4 * i + b, 1), :, :].rearrange("b q t -> q b t")
                                 ).then_inc(msk_in[b], 16)

            def load_x(i):
                if not (isinstance(i, int) and i == 0):
                    sp.wait_ge(z1_done, i)
                sp.dma_start(xt[:, :], xd[bass.ds(P * i, P), :]).then_inc(xt_in, 16)

            def load_residual(j):
                if not (isinstance(j, int) and j == 0):
                    sp.wait_ge(x1_done, j)
                sp.dma_start(xr[:, :], xd[bass.ds(P * j, P), :]).then_inc(xr_in, 16)

            def store_z3(j):
                sp.wait_ge(z3_done, j + 1)
                sp.dma_start(outd[bass.ds(P * j, P), :], x2[:, :]).then_inc(x2_out, 16)
                sp.dma_start(zbuf[bass.ds(P * j, P), :], z3[:, :]).then_inc(z3_out, 16)

            load_x(0)
            sp.dma_start(con[:, :], cond).then_inc(con_in, 16)
            sp.dma_start(par[:, :], pard).then_inc(par_in, 16)
            load_ctx(0, 0)
            sp.dma_start(ctl, ctxl).then_inc(ctl_in, 16)
            load_mask(0, 0)
            load_x(1)
            for b in range(1, TB):
                load_ctx(0, b)
                load_mask(0, b)
            load_x(2)
            load_residual(0)
            sp.dma_start(outd[TOK:TOK + P, :], xd[0:P, :]).then_inc(blank_out, 16)
            sp.dma_start(wxbc, wxbcd).then_inc(wxbc_in, 16)
            sp.dma_start(table.rearrange("(p n) c -> p (n c)", p=P), padd).then_inc(pad_in, 16)

            def load_expert(e):
                one = bass.ds(e, 1)
                sp.dma_start(wg[:, one], wgd[:, one]).then_inc(w_in, 16)
                sp.dma_start(wu[:, one], wud[:, one]).then_inc(w_in, 16)

            def tile(i):
                for b in range(TB):
                    if runs(i + 1):
                        load_mask(i + 1, b)
                        load_ctx(i + 1, b)
                    if b == 2 and runs(i) and not (isinstance(i, int) and i == 0):
                        load_residual(i)
                    if b == 3 and runs(i - 2):
                        store_z3(i - 2)
                    if b == 3 and runs(i + 3):
                        load_x(i + 3)

            tile(0), tile(1), tile(2)
            sp.wait_ge(ssd_act, 4)
            sp.wait_ge(vl_done, 3)
            with sp.Fori(3, 3 + E) as i:
                tile(i)
                load_expert(i - 3)
            with sp.Fori(3 + E, NT - 3) as i:
                tile(i)
            for i in range(NT - 3, NT):
                tile(i)
            sp.wait_ge(o_ready, B)
            sp.wait_ge(px_done, B)
            for e in range(E):
                sp.dma_start(wd[:, e], wdd[:, e]).then_inc(wd_in, 16)
            tile(NT), tile(NT + 1)
            sp.wait_ge(z3_out, 16 * NT)
            sp.wait_ge(x2_out, 16 * NT)
            sp.wait_ge(blank_out, 16)

        @block.tensor
        def _(pe):
            def mm(out, lhsT, rhs, start=True, stop=True):
                return nc.tensor.matmul(out, lhsT, rhs, start=start, stop=stop)

            def last_values():
                pe.wait_ge(par_in, 16)
                pe.wait_ge(con_in, 16)
                pe.wait_ge(ctl_in, 16)
                for a in range(NH):
                    for c in range(NH):
                        mm(M2[:, a, :], wv[:, c, a * P:(a + 1) * P], ctl[:, c, :], c == 0, c == NH - 1)
                    for c in range(NH):
                        last = mm(M2K[:, a, :], wk[:, c, a * P:(a + 1) * P], ctl[:, c, :], c == 0, c == NH - 1)
                last.then_inc(vl_ready, 1)

            def project_k(i, b):
                n = 4 * i + b
                pe.wait_ge(lo_done, n + 1)
                hi, lo = ctx_hi[:, b % 2], ctx_lo[:, b % 2]
                at_least(pe, lows_done, 2 * n)
                for a in range(NH):
                    for c in range(NH):
                        for k, (w, x) in enumerate(((wkh, hi), (wkh, lo), (wkl, hi))):
                            last = mm(K2[:, a, :], w[:, c, a * P:(a + 1) * P], x[:, c, 0:LAST],
                                      c == 0 and k == 0, c == NH - 1 and k == 2)
                last.then_inc(k_ready, 1)

            def project_v(i, b):
                n = 4 * i + b
                hi, lo = ctx_hi[:, b % 2], ctx_lo[:, b % 2]
                at_least(pe, v_done, n)
                for t in range(TC):
                    for c in range(NH):
                        for k, (x, w) in enumerate(((hi, wvh), (hi, wvl), (lo, wvh))):
                            last = mm(V_[:, t * D:(t + 1) * D], x[:, c, t * P:(t + 1) * P], w[:, c, :],
                                      c == 0 and k == 0, c == NH - 1 and k == 2)
                last.then_inc(v_ready, 1)

            def scores(i, b, groups):
                n = 4 * i + b
                pe.wait_ge(qbd_done, 4 * n + 4)
                pe.wait_ge(k_done, 4 * n + 4)
                pe.wait_ge(lows_done, 2 * n + 2)
                for g in groups:
                    at_least(pe, max_done, 4 * n + g - 1)
                    for k, (q, x) in enumerate(((0, 0), (0, 1), (1, 0))):
                        last = mm(SC[g % 2][:, 0:SP], qbd[q][:, b % 2, g, :], kT[x][:, g // 2, :], k == 0, k == 2)
                    last.then_inc(s_ready, 1)

            def transpose_probs(i, b):
                n = 4 * i + b
                for d in range(2):
                    pe.wait_ge(exp_done, 4 * n + 2 * d + 2)
                    at_least(pe, pt_done, 2 * n + d - 1)
                    for g in (2 * d, 2 * d + 1):
                        for t in range(TC):
                            o = ((g % 2) * TC + t) * P
                            last = nc.tensor.transpose(PT[d][:, o:o + P], pr[:, g, t * P:(t + 1) * P], ident)
                    last.then_inc(pt_ready, 1)

            def weigh_values(i, b):
                n = 4 * i + b
                pe.wait_ge(pt_done, 2 * n + 2)
                pe.wait_ge(v_done, n + 1)
                at_least(pe, om_done, n)
                at_least(pe, rp_done, n)
                for a in range(NH):
                    for t in range(TC):
                        for g in (2 * a, 2 * a + 1):
                            r = (g % 2) * GW
                            mm(O[r:r + GW, a * P:(a + 1) * P], v[:, b % 2, t, g * GW:(g + 1) * GW], pT[:, g, t, :],
                               t == 0, t == TC - 1)
                pe.wait_ge(px_done, n + 1)
                mm(RP, px[:, :, :].rearrange("p n h -> p (n h)"), cst("sel")).then_inc(o_ready, 1)

            def transpose2(src, done):
                for a in range(NH):
                    last = nc.tensor.transpose(M2[:, a, :], src[:, a * P:(a + 1) * P], ident)
                last.then_inc(done, 1)

            def turn_z1(i):
                pe.wait_ge(z1_done, i + 1)
                transpose2(z1, z1T_ready)

            def queries(i):
                pe.wait_ge(z1T_done, i + 1)
                for a in range(NH):
                    for c in range(NH):
                        last = mm(M2[:, a, :], wq[:, c, a * P:(a + 1) * P], z1T[:, c, :], c == 0, c == NH - 1)
                last.then_inc(q_ready, 1)

            def expand(j):
                pe.wait_ge(rp_done, 4 * (j + 1))
                for k, e in enumerate(("er", "ep")):
                    for a in range(NH):
                        o = (k * NH + a) * P
                        last = mm(M[:, o:o + P], cst(e)[0:2 * H, a * P:(a + 1) * P], rp[:, :])
                last.then_inc(ex_ready, 1)

            def project_out(j):
                pe.wait_ge(aT_done, NH * (j + 1))
                for a in range(NH):
                    last = mm(M[:, 0:D], aT[:, a, :], wo[:, a, :], a == 0, a == NH - 1)
                last.then_inc(wo_ready, 1)

            def turn_z2(j):
                pe.wait_ge(z2_done, j + 1)
                transpose2(z2, z2T_ready)

            def project_dt(j):
                pe.wait_ge(z2T_done, j + 1)
                for a in range(NH):
                    last = mm(M[:, 0:H], z2T[:, a, :], wdt[:, a, :], a == 0, a == NH - 1)
                last.then_inc(dt_ready, 1)

            def sum_a(j):
                pe.wait_ge(a_done, j + 1)
                mm(M[:, 0:H], cst("trib"), dtv[:, 5, :]).then_inc(cum_ready, 1)

            def sum_decay_and_rank(j, k):
                if runs(j):
                    pe.wait_ge(en_done, j + 1)
                    last = mm(M[:, 0:H], cst("trib"), dtv[:, 7, :])
                if runs(k):
                    pe.wait_ge(mm_done, k + 1)
                    pe.wait_ge(chosen_done, k + 1)
                    mm(RK, cst("tris"), lg[:, 2, :], True, False)
                    last = mm(RK, ones, chosen[:, :], False, True)
                last.then_inc(c2_ready, 1)

            def turn_y(j):
                pe.wait_ge(yn_done, j + 1)
                transpose2(yn, ynT_ready)

            def project_y(j):
                pe.wait_ge(ynT_done, j + 1)
                for a in range(NH):
                    last = mm(M[:, 0:D], ynT[:, a, :], wout[:, a, :], a == 0, a == NH - 1)
                last.then_inc(y_ready, 1)

            def turn_z3(j):
                pe.wait_ge(z3_done, j + 1)
                transpose2(z3, z3T_ready)

            def router(j):
                pe.wait_ge(z3T_done, j + 1)
                for a in range(NH):
                    last = mm(M[:, 0:E], z3T[:, a, :], wrt[:, a, :], a == 0, a == NH - 1)
                last.then_inc(lg_ready, 1)

            def ssd():
                pe.wait_ge(wxbc_in, 16)
                pe.wait_ge(a_done, 1)
                pe.wait_ge(norm_done, 1)
                for c in range(NC):
                    for a in range(NH):
                        last = mm(M[:, c * Q:(c + 1) * Q], wxbc[:, a, c * P:(c + 1) * P], z2T[:, a, 0:Q],
                                  a == 0, a == NH - 1)
                last.then_inc(ssd_pe, 1)
                pe.wait_ge(ssd_dve, 11)
                for a in range(NH):
                    last = mm(M[0:Q, a * 8 * Q:(a + 1) * 8 * Q], cT[:, 2 + a, :],
                              cbd[:, a, :, :].rearrange("p h l -> p (h l)"))
                last.then_inc(ssd_pe, 1)
                pe.wait_ge(ssd_act, 1)
                pe.wait_ge(ssd_dve, 12)
                mm(M[0:Q, :], cst("gt")[0:Q, :], at_[:, :, :].rearrange("p h l -> p (h l)")).then_inc(ssd_pe, 1)
                pe.wait_ge(ssd_act, 2)
                for a in range(NH):
                    last = nc.tensor.transpose(M[0:Q, a * P:(a + 1) * P], cT[:, 4 + a, :], ident)
                last.then_inc(ssd_pe, 1)
                pe.wait_ge(ssd_act, 3)
                pe.wait_ge(ssd_dve, 14)
                for h in range(H):
                    last = mm(M[:, h * HD:(h + 1) * HD], w4[:, h, :, :].rearrange("p b l -> p (b l)"),
                              xs[:, h * HD:(h + 1) * HD])
                last.then_inc(ssd_pe, 1)
                pe.wait_ge(ssd_act, 4)

            def turn_a(i, b):
                if b == 0 and runs(i - 1):
                    if runs(i - 2):
                        pe.wait_ge(en_done, i - 1)
                    if isinstance(i, int) and i == 1:
                        pe.wait_ge(z1T_done, 3)
                    expand(i - 1)
                if b == 1 and runs(i - 2):
                    if runs(i - 1):
                        pe.wait_ge(x1_done, i)
                    else:
                        pe.wait_ge(chosen_done, i - 1)
                    turn_y(i - 2)
                if b == 2 and runs(i + 1):
                    if runs(i - 1):
                        pe.wait_ge(z2T_done, i)
                    queries(i + 1)
                if b == 3 and runs(i - 2):
                    router(i - 2)

            def turn_b(i, b):
                if b == 0 and (runs(i - 2) or runs(i - 3)):
                    if runs(i - 1):
                        pe.wait_ge(t_done, 2 * i)
                    sum_decay_and_rank(i - 2, i - 3)
                    if isinstance(i, int) and i == 2:
                        ssd()
                if b == 1 and runs(i - 2):
                    project_y(i - 2)
                if b == 2 and runs(i - 1):
                    if runs(i + 1):
                        pe.wait_ge(qs_done, NH * (i + 2))
                    project_dt(i - 1)
                if b == 3 and runs(i + 2):
                    if runs(i - 2):
                        pe.wait_ge(lg_done, i - 1)
                    elif runs(i - 1):
                        pe.wait_ge(dt_done, i)
                    else:
                        pe.wait_ge(qs_done, NH * (i + 2))
                    turn_z1(i + 2)

            def turn_c(i, b):
                if b == 0 and runs(i - 1):
                    if runs(i - 2):
                        pe.wait_ge(norm_done, i - 1)
                    if runs(i - 3):
                        pe.wait_ge(chosen_done, i - 1)
                    project_out(i - 1)
                if b == 1 and runs(i - 1):
                    if runs(i - 2):
                        pe.wait_ge(x2_done, i - 1)
                    turn_z2(i - 1)
                if b == 2 and runs(i - 2):
                    if runs(i - 1):
                        pe.wait_ge(dt_done, i)
                    turn_z3(i - 2)
                if b == 3 and runs(i - 1):
                    if runs(i + 2):
                        pe.wait_ge(z1T_done, i + 3)
                    elif runs(i - 2):
                        pe.wait_ge(lg_done, i - 1)
                    sum_a(i - 1)

            def tile(i):
                for b in range(TB):
                    nxt = following(i, b)
                    if runs(nxt[0]):
                        project_k(*nxt)
                        project_v(*nxt)
                    turn_a(i, b)
                    if runs(i):
                        transpose_probs(i, b)
                    if runs(nxt[0]):
                        scores(*nxt, (0, 1))
                    turn_b(i, b)
                    if runs(i):
                        weigh_values(i, b)
                    if runs(nxt[0]):
                        scores(*nxt, (2, 3))
                    turn_c(i, b)

            last_values()
            pe.wait_ge(vl_done, 3)
            turn_z1(0)
            queries(0)
            pe.wait_ge(wl_done, 2)
            project_k(0, 0)
            project_v(0, 0)
            scores(0, 0, range(NG))
            pe.wait_ge(qs_done, NH)
            turn_z1(1)
            steps(pe, tile)

        @block.scalar
        def _(act):
            def copy(out, in_, **kw):
                return nc.scalar.activation(out, in_, ACT.Copy, **kw)

            def take_keys(i, b):
                n = 4 * i + b
                at_least(act, s_ready, 4 * n)
                act.wait_ge(k_ready, n + 1)
                for a in range(NH):
                    nc.scalar.activation(kT[0][:, a, 0:LAST], K2[:, a, :], ACT.Identity,
                                         bias=prm("bk")[:, a:a + 1]).then_inc(k_done, 1)
                for x, y in zip(kT, kl_parts):
                    copy(x[:, :, LAST:SP], y[:, :, bass.ds(n, 1)].bitcast(F32).broadcast_to([P, NH, SP - LAST])
                         ).then_inc(k_done, 1)

            def split_high(i, b):
                n = 4 * i + b
                act.wait_ge(ctx_in[b], 16 * (i + 1))
                at_least(act, v_ready, n - 1)
                copy(ctx_hi[:, b % 2].rearrange("p c t -> p (c t)"), ctx[:, b].rearrange("p c t -> p (c t)")
                     ).then_inc(hi_done, 1)

            def take_values(i, b):
                n = 4 * i + b
                act.wait_ge(v_ready, n + 1)
                at_least(act, o_ready, n - 1)
                copy(v[:, b % 2, :, :].rearrange("p t d -> p (t d)"), V_[:, :]).then_inc(v_done, 1)

            def exponentials(i, b, *groups):
                n = 4 * i + b
                for g in groups:
                    act.wait_ge(nmx_done, 4 * n + g + 1)
                    if g == 0:
                        at_least(act, px_done, n)
                        at_least(act, rec_done, n)
                        at_least(act, pt_ready, 2 * n)
                    nc.scalar.activation(pr[:, g, :], sm[:, g, :], ACT.Exp, bias=nmx[:, g:g + 1],
                                         accum_out=rsum[:, g:g + 1]).then_inc(exp_done, 1)

            def take_probs(i, b):
                n = 4 * i + b
                for d in range(2):
                    act.wait_ge(pt_ready, 2 * n + d + 1)
                    if d == 0:
                        at_least(act, o_ready, n)
                    copy(pT[:, 2 * d:2 * d + 2, :, :].rearrange("p g t n -> p (g t n)"), PT[d][:, :]).then_inc(pt_done, 1)

            def take_rp(i, b):
                n = 4 * i + b
                act.wait_ge(om_done, n + 1)
                if b == 0:
                    at_least(act, ex_ready, i)
                copy(rp[:, b * Q:(b + 1) * Q], RP).then_inc(rp_done, 1)

            def take2(dst, ready, done, j):
                act.wait_ge(ready, j + 1)
                copy(dst[:, :, :], M2).then_inc(done, 1)

            def take_z1T(i):
                take2(z1T, z1T_ready, z1T_done, i)

            def keep(j):
                act.wait_ge(x1_done, j + 1)
                at_least(act, x2_done, j)
                copy(xk[:, :], x1[:, :]).then_inc(kept, 1)

            def decays(j):
                act.wait_ge(cum_ready, j + 1)
                at_least(act, rn_done, j)
                nc.scalar.activation(dtv[:, 6, :], M[:, 0:H], ACT.Exp).then_inc(ep_done, 1)
                nc.scalar.activation(dtv[:, 7, :], M[:, 0:H], ACT.Exp, scale=-1.0).then_inc(en_done, 1)

            def soft_exp(j):
                act.wait_ge(nabs_done, j + 1)
                nc.scalar.activation(dtv[:, 2, :], dtv[:, 1, :], ACT.Exp).then_inc(u_done, 1)

            def gate_exp(j):
                act.wait_ge(diff_done, j + 1)
                nc.scalar.activation(sv[:, 1, 0:1], sv[:, 0, 0:1], ACT.Exp).then_inc(gate_e, 1)

            def ssd():
                act.wait_ge(ssd_pe, 2)
                copy(gs[:, :, :].rearrange("p h l -> p (h l)"), M[0:Q, :]).then_inc(ssd_act, 1)
                act.wait_ge(ssd_pe, 3)
                nc.scalar.activation(ls[:, :, :].rearrange("p h l -> p (h l)"), M[0:Q, :], ACT.Exp).then_inc(ssd_act, 1)
                act.wait_ge(ssd_pe, 4)
                copy(xs, M[0:Q, 0:D]).then_inc(ssd_act, 1)
                act.wait_ge(ssd_pe, 5)
                copy(y0[:, :], M[:, 0:D]).then_inc(ssd_act, 1)

            def take_z2T(j):
                take2(z2T, z2T_ready, z2T_done, j)

            def take_ynT(j):
                take2(ynT, ynT_ready, ynT_done, j)

            def take_z3T(j):
                take2(z3T, z3T_ready, z3T_done, j)

            def tile(i):
                for b in range(TB):
                    nxt = following(i, b)
                    two = following(i, b, 2)
                    if runs(two[0]):
                        split_high(*two)
                    if b == 1 and runs(i - 2):
                        take_ynT(i - 2)
                    if runs(i):
                        take_probs(i, b)
                    if b == 0 and runs(i - 3):
                        gate_exp(i - 3)
                    if b == 0 and isinstance(i, int) and i == 2:
                        ssd()
                    if b == 3 and runs(i + 2):
                        take_z1T(i + 2)
                    if runs(nxt[0]):
                        exponentials(*nxt, 0, 1)
                        take_values(*nxt)
                    if b == 1 and runs(i - 1):
                        keep(i - 1)
                    if b == 2 and runs(i - 1):
                        soft_exp(i - 1)
                    if runs(nxt[0]):
                        exponentials(*nxt, 2)
                    if b == 1 and runs(i - 1):
                        take_z2T(i - 1)
                    if b == 2 and runs(i - 2):
                        take_z3T(i - 2)
                    if b == 3 and runs(i - 1):
                        decays(i - 1)
                    if runs(nxt[0]):
                        exponentials(*nxt, 3)
                    if runs(i):
                        take_rp(i, b)
                    if runs(two[0]):
                        take_keys(*two)

            act.wait_ge(par_in, 16)
            copy(wkh[:, :, :], wk).then_inc(wh_done, 1)
            copy(wvh[:, :, :], wv).then_inc(wh_done, 1)
            split_high(0, 0)
            take_z1T(0)
            act.wait_ge(kl_low, 1)
            take_keys(0, 0)
            split_high(0, 1)
            take_values(0, 0)
            exponentials(0, 0, 0, 1, 2)
            take_z1T(1)
            exponentials(0, 0, 3)
            take_keys(0, 1)
            steps(act, tile)

        @block.vector
        def _(dve):
            V = nc.vector

            def maxima(i, b, d):
                n = 4 * i + b
                for g in (2 * d, 2 * d + 1):
                    if g == 0:
                        held(dve, (init, 2), (msk_in[b], 64 * (i + 1)), (exp_done, 4 * n), (s_ready, 4 * n + 1))
                    else:
                        held(dve, (init, 2), (s_ready, 4 * n + g + 1))
                    V.tensor_tensor_reduce(sm[:, g, :], SC[g % 2][:, 0:S], msk[:, b, :], 1.0, -3.0e38, ALU.add, ALU.max,
                                           mx[:, g:g + 1]).then_inc(max_done, 1)
                    dve.wait_ge(max_done, 4 * n + g + 1)
                    V.tensor_scalar(nmx[:, g:g + 1], mx[:, g:g + 1], -1.0, None, ALU.mult).then_inc(nmx_done, 1)

            def reciprocals(i, b):
                n = 4 * i + b
                dve.wait_ge(exp_done, 4 * n + 4)
                at_least(dve, px_done, n)
                V.reciprocal(rr[:, 0, :], rsum[:, :]).then_inc(rec_done, 1)

            def take_output(i, b):
                n = 4 * i + b
                dve.wait_ge(o_ready, n + 1)
                at_least(dve, ou_done, n)
                V.tensor_tensor(om[:, :, :, :], OT, cst("hm").unsqueeze(1).unsqueeze(3).broadcast_to([P, NH, HG, Q]),
                                ALU.mult).then_inc(om_done, 1)
                dve.wait_ge(om_done, n + 1)
                V.tensor_reduce(ou[:, :, b * Q:(b + 1) * Q], om[:, :, :, :].rearrange("p a h q -> p a q h"),
                                AX.X, ALU.add).then_inc(ou_done, 1)

            def statistics(src, k, j, s_st, s_mv, s_done):
                V.bn_stats(st[:, k, :], src).then_inc(s_st, 1)
                held(dve, (init, 2), (s_st, j + 1), (s_done, j))
                V.bn_aggr(mv[:, k, :], st[:, k, :]).then_inc(s_mv, 1)

            def statistics1(i):
                held(dve, (init, 2), (xt_in, 16 * (i + 1)))
                statistics(xt[:, :], 0, i, st1, mv1, z1_done)

            def take_queries(i):
                dve.wait_ge(q_ready, i + 1)
                at_least(dve, qbd_done, 16 * i)
                for a in range(NH):
                    V.tensor_scalar(qs[:, a, :], M2[:, a, :], prm("bq")[:, a:a + 1], float(HD) ** -0.5,
                                    ALU.add, ALU.mult).then_inc(qs_done, 1)
                dve.wait_ge(qs_done, NH * (i + 1))
                V.tensor_copy(q_parts[0][:, :, :], qs).then_inc(q_high, 1)
                dve.wait_ge(q_high, i + 1)
                V.tensor_tensor(q_parts[1][:, :, :], qs, q_parts[0][:, :, :].bitcast(F32), ALU.subtract
                                ).then_inc(q_split, 1)

            def key_lows(i, b):
                n = 4 * i + b
                dve.wait_ge(k_done, 4 * n + 2)
                for a in range(NH):
                    V.scalar_tensor_tensor(kT[1][:, a, 0:LAST], K2[:, a, :], prm("bk")[:, a:a + 1],
                                           kT[0][:, a, 0:LAST].bitcast(F32), ALU.add, ALU.subtract
                                           ).then_inc(lows_done, 1)

            def weigh(j):
                dve.wait_ge(ex_ready, j + 1)
                dve.wait_ge(ou_done, 4 * (j + 1))
                EX = M[:, :].rearrange("p (k a n) -> p k a n", k=2, a=NH)
                V.tensor_tensor(t1[:, :, :], EX[:, 0], ou[:, :, :], ALU.mult).then_inc(t_done, 1)
                V.tensor_tensor(t2[:, :, :].rearrange("p a (b q) -> p a b q", b=TB),
                                EX[:, 1].rearrange("p a (b q) -> p a b q", b=TB),
                                vl[:, :, bass.ds(TB * j, TB)].unsqueeze(3).broadcast_to([P, NH, TB, Q]),
                                ALU.mult).then_inc(t_done, 1)

            def attention_out(j):
                dve.wait_ge(t_done, 2 * (j + 1))
                at_least(dve, wo_ready, j)
                for a in range(NH):
                    V.scalar_tensor_tensor(aT[:, a, :], t1[:, a, :], prm("bv")[:, a:a + 1], t2[:, a, :],
                                           ALU.add, ALU.add).then_inc(aT_done, 1)

            def residual1(j):
                dve.wait_ge(wo_ready, j + 1)
                dve.wait_ge(xb_done, j + 1)
                at_least(dve, kept, j)
                at_least(dve, z2_done, j)
                V.tensor_tensor(x1[:, :], M[:, 0:D], xr[:, :], ALU.add).then_inc(x1_done, 1)

            def statistics2(j):
                held(dve, (init, 2), (x1_done, j + 1))
                statistics(x1[:, :], 1, j, st2, mv2, z2_done)

            def soft_in(j):
                dve.wait_ge(dt_ready, j + 1)
                V.tensor_tensor(dtv[:, 0, :], M[:, 0:H], prm("dtb"), ALU.add).then_inc(dt_done, 1)
                dve.wait_ge(dt_done, j + 1)
                V.tensor_scalar(dtv[:, 10, :], dtv[:, 0, :], 0.0, None, ALU.max).then_inc(soft_max, 1)
                V.scalar_tensor_tensor(dtv[:, 1, :], dtv[:, 0, :], -1.0, dtv[:, 0, :], ALU.mult, ALU.min
                                       ).then_inc(nabs_done, 1)

            def softplus(j, nxt):
                k = [0]

                def link(ins):
                    k[0] += 1
                    ins.then_inc(soft, 1)
                    dve.wait_ge(soft, NSOFT * j + k[0])

                u, r, y, w, s = dtv[:, 2, :], dtv[:, 3, :], dtv[:, 4, :], dtv[:, 8, :], dtv[:, 9, :]
                dve.wait_ge(u_done, j + 1)
                dve.wait_ge(soft_max, j + 1)
                link(V.tensor_scalar(r, u, 2.0, None, ALU.add))
                link(V.reciprocal(s, r))
                link(V.tensor_tensor(y, u, s, ALU.mult))
                if runs(nxt[0]):
                    key_lows(*nxt)
                link(V.tensor_tensor(w, y, y, ALU.mult))
                link(V.tensor_scalar(s, w, 1.0 / ATANH[0], None, ALU.mult))
                if runs(j - 1):
                    take_logits(j - 1)
                if runs(j + 1):
                    reciprocals(j + 1, TB - 1)
                for c in ATANH[1:]:
                    link(V.scalar_tensor_tensor(s, s, 1.0 / c, w, ALU.add, ALU.mult))
                link(V.scalar_tensor_tensor(s, s, 1.0, y, ALU.add, ALU.mult))
                assert k[0] == NSOFT
                V.scalar_tensor_tensor(w, s, 2.0, dtv[:, 10, :], ALU.mult, ALU.add).then_inc(soft_sum, 1)
                dve.wait_ge(soft_sum, j + 1)
                at_least(dve, cum_ready, j)
                V.tensor_tensor(dtv[:, 5, :], w, prm("apar"), ALU.mult).then_inc(a_done, 1)

            def norms(j):
                dve.wait_ge(c2_ready, j + 1)
                dve.wait_ge(ep_done, j + 1)
                V.tensor_tensor(dtv[:, 8, :], M[:, 0:H], dtv[:, 6, :], ALU.mult).then_inc(norm_done, 1)
                dve.wait_ge(norm_done, j + 1)
                V.reciprocal(dtv[:, 9, :], dtv[:, 8, :]).then_inc(rn_done, 1)

            def scale_y(j):
                dve.wait_ge(rn_done, j + 1)
                at_least(dve, ynT_ready, j)
                V.tensor_tensor(yn[:, :].rearrange("p (h d) -> p h d", h=H), y0[:, :].rearrange("p (h d) -> p h d", h=H),
                                dtv[:, 9, :].unsqueeze(2).broadcast_to([P, H, HD]), ALU.mult).then_inc(yn_done, 1)

            def residual2(j):
                dve.wait_ge(y_ready, j + 1)
                dve.wait_ge(kept, j + 1)
                at_least(dve, z3_done, j)
                at_least(dve, x2_out, 16 * j)
                V.tensor_tensor(x2[:, :], M[:, 0:D], xk[:, :], ALU.add).then_inc(x2_done, 1)
                held(dve, (init, 2), (x2_done, j + 1))
                statistics(x2[:, :], 2, j, st3, mv3, z3_done)

            def normalise3(j):
                dve.wait_ge(rstd3, j + 1)
                at_least(dve, z3T_ready, j)
                at_least(dve, z3_out, 16 * j)
                V.tensor_scalar(z3[:, :], x2[:, :], mv[:, 2, 0:1], rs[:, 2, 1:2], ALU.subtract, ALU.mult
                                ).then_inc(z3_done, 1)

            def normalise2(j):
                dve.wait_ge(rstd2, j + 1)
                at_least(dve, z2T_ready, j)
                V.tensor_scalar(z2[:, :], x1[:, :], mv[:, 1, 0:1], rs[:, 1, 1:2], ALU.subtract, ALU.mult
                                ).then_inc(z2_done, 1)

            def take_logits(j):
                dve.wait_ge(lg_ready, j + 1)
                V.tensor_copy(lg[:, 0, :], M[:, 0:E]).then_inc(lg_done, 1)

            def select(j):
                held(dve, (init, 2), (lg_done, j + 1))
                V.max(lg[:, 1, :], lg[:, 0, :]).then_inc(top_done, 1)
                held(dve, (init, 2), (top_done, j + 1))
                V.max_index(mi[:, :], lg[:, 1, :], lg[:, 0, :]).then_inc(index_done, 1)
                V.tensor_tensor(sv[:, 0, 0:1], lg[:, 1, 1:2], lg[:, 1, 0:1], ALU.subtract).then_inc(diff_done, 1)
                dve.wait_ge(index_done, j + 1)
                V.tensor_copy(sv[:, 2, :], mi[:, 0:TOPK]).then_inc(expert_done, 1)
                dve.wait_ge(expert_done, j + 1)
                V.tensor_tensor(oh[:, :, :], cst("iota8").unsqueeze(1).broadcast_to([P, TOPK, E]),
                                sv[:, 2, :].unsqueeze(2).broadcast_to([P, TOPK, E]), ALU.is_equal).then_inc(oh_done, 1)
                dve.wait_ge(oh_done, j + 1)
                at_least(dve, chosen_done, j + 1)
                V.tensor_tensor(lg[:, 2, :], oh[:, 0, :], oh[:, 1, :], ALU.add).then_inc(mm_done, 1)

            def take_ranks(j):
                dve.wait_ge(c2_ready, j + 2)
                V.tensor_tensor(ohr[:, :, :], oh[:, :, :], RK.unsqueeze(1).broadcast_to([P, TOPK, E]), ALU.mult
                                ).then_inc(ranked, 1)
                V.tensor_tensor(chosen[:, :], chosen[:, :], lg[:, 2, :], ALU.add).then_inc(chosen_done, 1)

            def place(j):
                gate = pay[:, :, 2:3].bitcast(F32).rearrange("p k c -> p (k c)")
                dve.wait_ge(ranked, j + 1)
                V.tensor_reduce(sv[:, 3, :], ohr[:, :, :], AX.X, ALU.add).then_inc(rank_done, 1)
                dve.wait_ge(gate_e, j + 1)
                V.tensor_scalar(sv[:, 4, 0:1], sv[:, 1, 0:1], 1.0, None, ALU.add).then_inc(gate_sum, 1)
                dve.wait_ge(rank_done, j + 1)
                V.tensor_copy(ri[:, 0, :], sv[:, 3, :]).then_inc(whole, 1)
                V.tensor_scalar(sv[:, 5, :], sv[:, 3, :], float(TCOL), None, ALU.mult).then_inc(row_a, 1)
                dve.wait_ge(whole, j + 1)
                V.tensor_scalar(ri[:, 1, :], ri[:, 0, :], P.bit_length() - 1, None, ALU.logical_shift_right
                                ).then_inc(col_done, 1)
                dve.wait_ge(gate_sum, j + 1)
                at_least(dve, slots_out, 32 * j)
                at_least(dve, pay_done, 5 * j)
                V.reciprocal(gate[:, 0:1], sv[:, 4, 0:1]).then_inc(pay_done, 1)
                dve.wait_ge(row_a, j + 1)
                V.scalar_tensor_tensor(sv[:, 6, :], sv[:, 2, :], float(TPE), sv[:, 5, :], ALU.mult, ALU.add
                                       ).then_inc(row_b, 1)
                V.tensor_copy(pay[:, :, 0:2], tokf[:, :].rearrange("p (k c) -> p k c", k=TOPK)).then_inc(pay_done, 1)
                dve.wait_ge(pay_done, 5 * j + 2)
                V.tensor_tensor(gate[:, 1:2], gate[:, 0:1], sv[:, 1, 0:1], ALU.mult).then_inc(pay_done, 1)
                V.tensor_scalar(tokf[:, :], tokf[:, :], float(P), None, ALU.add).then_inc(pay_done, 1)
                dve.wait_ge(col_done, j + 1)
                dve.wait_ge(row_b, j + 1)
                V.scalar_tensor_tensor(ri[:, 2, :], ri[:, 1, :], 1.0 - P * TCOL, sv[:, 6, :], ALU.mult, ALU.add
                                       ).then_inc(pay_done, 1)

            def ssd():
                k = [0]

                def link(ins):
                    k[0] += 1
                    ins.then_inc(ssd_dve, 1)
                    dve.wait_ge(ssd_dve, k[0])

                dve.wait_ge(ssd_pe, 1)
                link(V.memset(xp[:, :, 0:KC - 1], 0.0))
                link(V.tensor_copy(xp[:, :, KC - 1:], M[:, 0:NC * Q].rearrange("p (c l) -> p c l", c=NC)))
                taps = prm("convw").rearrange("p (c k) -> p c k", k=KC)

                def tap(n):
                    return taps[:, :, n:n + 1].broadcast_to([P, NC, Q])

                link(V.tensor_tensor(cv[:, 0], xp[:, :, 0:Q], tap(0), ALU.mult))
                for n in range(1, KC):
                    link(V.tensor_tensor(cv[:, 1], xp[:, :, n:n + Q], tap(n), ALU.mult))
                    link(V.tensor_tensor(cv[:, 0], cv[:, 0], cv[:, 1], ALU.add))
                link(V.tensor_tensor(cT, cv[:, 0], prm("convb").unsqueeze(2).broadcast_to([P, NC, Q]), ALU.add))
                n8 = P // HD
                for a in range(NH):
                    last = V.tensor_tensor(cbd[:, a], cT[:, a, :].unsqueeze(1).broadcast_to([P, n8, Q]),
                                           cst("bm8").unsqueeze(2).broadcast_to([P, n8, Q]), ALU.mult)
                link(last)
                le = cst("le")[0:Q, :].unsqueeze(1).broadcast_to([Q, H, Q])
                link(V.tensor_tensor(at_, dtv[0:Q, 5, :].unsqueeze(2).broadcast_to([Q, H, Q]), le, ALU.mult))
                dve.wait_ge(ssd_act, 2)
                link(V.tensor_tensor(ws, gs, ls, ALU.mult))
                for h in range(H):
                    last = V.tensor_tensor(w4[:, h], ws[:, h, :].unsqueeze(1).broadcast_to([Q, TB, Q]),
                                           cst("le")[0:Q, :].unsqueeze(1).broadcast_to([Q, TB, Q]), ALU.mult)
                link(last)
                assert k[0] == 14, k[0]
                dve.wait_ge(ssd_act, 4)

            def tile(i):
                for b in range(TB):
                    nxt = following(i, b)
                    if runs(nxt[0]) and not (b == 3 and runs(i - 1)):
                        key_lows(*nxt)
                    if b == 0 and runs(i - 3):
                        select(i - 3)
                    if b == 1 and runs(i - 3):
                        place(i - 3)
                    if b == 1 and runs(i - 1):
                        normalise2(i - 1)
                    if b == 2 and runs(i - 2):
                        normalise3(i - 2)
                    if b == 0 and runs(i - 1):
                        weigh(i - 1)
                    if b == 2 and runs(i + 1):
                        take_queries(i + 1)
                    if b == 3 and runs(i - 1):
                        softplus(i - 1, nxt)
                    elif b == 3 and runs(i - 2):
                        take_logits(i - 2)
                    if runs(i) and not (b == 3 and runs(i - 1)):
                        reciprocals(i, b)
                    if runs(nxt[0]):
                        maxima(*nxt, 0)
                    if b == 0 and runs(i - 1):
                        attention_out(i - 1)
                    if b == 0 and runs(i - 2):
                        norms(i - 2)
                    if b == 0 and runs(i - 3):
                        take_ranks(i - 3)
                    if b == 0 and isinstance(i, int) and i == 2:
                        ssd()
                    if b == 1 and runs(i - 2):
                        residual2(i - 2)
                    if b == 2 and runs(i - 1):
                        soft_in(i - 1)
                    if runs(nxt[0]):
                        maxima(*nxt, 1)
                    if b == 0 and runs(i - 2):
                        scale_y(i - 2)
                    if runs(i):
                        take_output(i, b)
                    if b == 0 and runs(i - 1):
                        residual1(i - 1)
                        statistics2(i - 1)
                    if b == 1 and runs(i + 2):
                        statistics1(i + 2)

            V.memset(chosen[:, :], 0.0).then_inc(chosen_done, 1)
            V.memset(pay[:, :, :].rearrange("p k c -> p (k c)"), 0).then_inc(init, 1)
            dve.wait_ge(con_in, 16)
            V.tensor_copy(tokf[:, :], cst("tok")).then_inc(init, 1)
            dve.wait_ge(init, 2)
            statistics1(0)
            for k, (w, h, l) in enumerate(((wk, wkh, wkl), (wv, wvh, wvl))):
                dve.wait_ge(wh_done, k + 1)
                V.tensor_tensor(l[:, :, :], w, h[:, :, :].bitcast(F32), ALU.subtract).then_inc(wl_done, 1)
            dve.wait_ge(vl_ready, 1)
            V.tensor_copy(vl[:, :, :], M2).then_inc(vl_done, 1)
            for a in range(NH):
                V.tensor_scalar(kl[:, a, :], M2K[:, a, :], prm("bk")[:, a:a + 1], None, ALU.add).then_inc(vl_done, 1)
            dve.wait_ge(vl_done, 3)
            V.tensor_copy(kl_parts[0][:, :, :], kl).then_inc(kl_high, 1)
            dve.wait_ge(kl_high, 1)
            V.tensor_tensor(kl_parts[1][:, :, :], kl, kl_parts[0][:, :, :].bitcast(F32), ALU.subtract).then_inc(kl_low, 1)
            take_queries(0)
            key_lows(0, 0)
            statistics1(1)
            maxima(0, 0, 0)
            maxima(0, 0, 1)
            steps(dve, tile)

        @block.gpsimd
        def _(pool):
            G = nc.gpsimd

            def power(k, j, s_mv, s_var, s_rstd):
                pool.wait_ge(s_mv, j + 1)
                G.tensor_tensor(rs[:, k, 0:1], mv[:, k, 1:2], cst("eps"), ALU.add).then_inc(s_var, 1)
                pool.wait_ge(s_var, j + 1)
                G.tensor_tensor(rs[:, k, 1:2], rs[:, k, 0:1], cst("nhalf"), ALU.pow).then_inc(s_rstd, 1)

            def normalise(k, src, dst, j, s_mv, s_var, s_rstd, s_turned, s_done):
                power(k, j, s_mv, s_var, s_rstd)
                held(pool, (con_in, 16), (s_rstd, j + 1), (s_turned, j))
                G.tensor_scalar(dst[:, :], src[:, :], mv[:, k, 0:1], rs[:, k, 1:2], ALU.subtract, ALU.mult
                                ).then_inc(s_done, 1)

            def normalise1(i):
                normalise(0, xt, z1, i, mv1, var1, rstd1, z1T_ready, z1_done)

            def split_low(i, b):
                n = 4 * i + b
                pool.wait_ge(hi_done, n + 1)
                G.tensor_tensor(ctx_lo[:, b % 2], ctx[:, b], ctx_hi[:, b % 2].bitcast(F32), ALU.subtract
                                ).then_inc(lo_done, 1)

            def lay_queries(i, b):
                n = 4 * i + b
                pool.wait_ge(q_split, i + 1)
                at_least(pool, s_ready, 4 * (n - 1))
                for dst, src in zip(qbd, q_parts):
                    for a in range(NH):
                        G.tensor_tensor(dst[:, b % 2, 2 * a:2 * a + 2, :].rearrange("p g (h q) -> p g h q", h=HG),
                                        src[:, a, b * Q:(b + 1) * Q].bitcast(F32).unsqueeze(1).unsqueeze(1)
                                        .broadcast_to([P, 2, HG, Q]),
                                        cst("bm").rearrange("p (g h) -> p g h", g=2).unsqueeze(3)
                                        .broadcast_to([P, 2, HG, Q]), ALU.mult).then_inc(qbd_done, 1)

            def last_probs(i, b):
                n = 4 * i + b
                pool.wait_ge(rec_done, n + 1)
                G.tensor_tensor(rr[:, 1, :], pr[:, :, LAST], rr[:, 0, :], ALU.mult).then_inc(pl_done, 1)
                pool.wait_ge(pl_done, n + 1)
                at_least(pool, o_ready, n)
                G.tensor_tensor(px[:, :, :], rr[:, :, :].rearrange("p k g -> p (k g)").unsqueeze(2)
                                .broadcast_to([P, 2 * NG, HG]),
                                cst("dm").unsqueeze(1).broadcast_to([P, 2 * NG, HG]), ALU.mult).then_inc(px_done, 1)

            def add_bias(j):
                pool.wait_ge(xr_in, 16 * (j + 1))
                G.tensor_tensor(xr[:, :], xr[:, :], prm("bo"), ALU.add).then_inc(xb_done, 1)

            def write_slots(j):
                held(pool, (con_in, 16), (pay_done, 5 * j + 5))
                for k in range(TOPK):
                    G.indirect_dma_start(table[:, :], bass.IndirectOffsetOnAxis(ri[:, 2, k:k + 1].bitcast(U32), 0),
                                         pay[:, k, :], None).then_inc(slots_out, 16)

            def tile(i):
                for b in range(TB):
                    two = following(i, b, 2)
                    if b == 2 and runs(i - 2):
                        power(2, i - 2, mv3, var3, rstd3)
                    if b == 1 and runs(i - 1):
                        power(1, i - 1, mv2, var2, rstd2)
                    if runs(two[0]):
                        split_low(*two)
                    if runs(i):
                        last_probs(i, b)
                    if b == 0 and runs(i - 1):
                        add_bias(i - 1)
                    if runs(two[0]):
                        lay_queries(*two)
                    if b == 2 and runs(i + 2):
                        normalise1(i + 2)
                    if b == 3 and runs(i - 3):
                        write_slots(i - 3)

            pool.wait_ge(con_in, 16)
            pool.wait_ge(par_in, 16)
            normalise1(0)
            split_low(0, 0)
            lay_queries(0, 0)
            normalise1(1)
            split_low(0, 1)
            lay_queries(0, 1)
            pool.wait_ge(pad_in, 16)
            steps(pool, tile)
            pool.wait_ge(slots_out, 32 * NT)


def experts(nc, zbuf, table, outd, cst, wg, wu, wd, chosen, w_in, wd_in):
    own = ExitStack()
    with own:
        def sb(name, shape, dt=F32):
            return own.enter_context(nc.sbuf_tensor(name, shape, dt))

        def sem(name):
            return own.enter_context(nc.semaphore(name))

        ident, ones = cst("ident"), cst("ones")
        tab = sb("tab", [P, TCOL, 4], I32)
        info = sb("info", [P, 2, NSLOT], I32)
        cnt = sb("cnt", [P, 5, E])
        cnti = sb("cnti", [P, E], I32)
        past = sb("past", [P, 2, NSLOT, E])
        tl = sb("tl", [P, 5, NSLOT])
        gi = sb("gi", [P, 2, 4], I32)
        oi = sb("oi", [P, 2, 4], I32)
        zg = sb("zg", [P, 2, D])
        zT = sb("zT", [P, 2, NH, P])
        sg = sb("sg", [P, 2, FH])
        hb = sb("hb", [P, F])
        hT = sb("hT", [P, FC, P])
        yb = sb("yb", [P, 2, D])
        GB = own.enter_context(nc.psum_tensor("gate_p", [P, 2, 512], F32))
        UB = own.enter_context(nc.psum_tensor("up_p", [P, 2, 512], F32))
        HB = [own.enter_context(nc.psum_tensor(f"ht_p{k}", [P, 512], F32)) for k in range(2)]
        YB = own.enter_context(nc.psum_tensor("y_p", [P, 512], F32))
        ZB = own.enter_context(nc.psum_tensor("z_p", [P, 512], F32))

        tab_in = sem("tab_in")
        cnt_ready, plan, info_done = sem("cnt_ready"), sem("plan"), sem("info_done")
        gi_done, oi_done = sem("gi_done"), sem("oi_done")
        zg_in = [sem(f"zg_in{s}") for s in range(2)]
        y_out = sem("y_out")
        zT_ready, zT_done = sem("zT_ready"), sem("zT_done")
        g_ready, u_ready, silu_done, h_done = sem("g_ready"), sem("u_ready"), sem("silu_done"), sem("h_done")
        hT_ready, hT0_done, hT1_done = sem("hT_ready"), sem("hT0_done"), sem("hT1_done")
        y_ready, y_done = sem("y_ready"), sem("y_done")

        block = own.enter_context(nc.Block())

        def tiles(eng, body):
            body(0, 0, first=True)
            with eng.Fori(1, NSLOT - 1, 2) as t:
                body(t, 1)
                body(t + 1, 0)
            body(NSLOT - 1, 1, last=True)

        @block.sync
        def _(sp):
            sp.dma_start(tab[:, :, :], table.rearrange("(p n) c -> p n c", p=P)).then_inc(tab_in, 16)

        @block.tensor
        def _(pe):
            def mm(out, lhsT, rhs, start=True, stop=True):
                return nc.tensor.matmul(out, lhsT, rhs, start=start, stop=stop)

            def turn_z(t, s):
                pe.wait_ge(zg_in[s], 16 * (t // 2 + 1) if isinstance(t, int) else 16 * ((t - s) // 2 + 1))
                at_least(pe, zT_done, t)
                for a in range(NH):
                    last = nc.tensor.transpose(ZB[:, a * P:(a + 1) * P], zg[:, s, a * P:(a + 1) * P], ident)
                last.then_inc(zT_ready, 1)

            def expert_of(t):
                return nc.tensor.value_load(info[0:1, 1, bass.ds(t, 1)], min_val=0, max_val=E - 1)

            def up(t, s):
                e = expert_of(t)
                pe.wait_ge(zT_done, t + 1)
                for bank, w, free, done in ((GB, wg, silu_done, g_ready), (UB, wu, h_done, u_ready)):
                    at_least(pe, free, t)
                    for f in range(2):
                        for c in range(NH):
                            last = mm(bank[:, f, 0:FH], zT[:, s, c, :],
                                      w[:, bass.ds(e, 1), c, f * FH:(f + 1) * FH].rearrange("p o n -> p (o n)"),
                                      c == 0, c == NH - 1)
                    last.then_inc(done, 1)

            def turn_h(t):
                pe.wait_ge(h_done, t + 1)
                for k in range(2):
                    at_least(pe, (hT0_done, hT1_done)[k], t if k == 0 else 2 * t)
                    for c in range(4 * k, min(4 * k + 4, FC)):
                        n = P if c < FC - 1 else FL
                        last = nc.tensor.transpose(HB[k][0:n, (c % 4) * P:(c % 4 + 1) * P], hb[:, c * P:c * P + n], ident)
                    last.then_inc(hT_ready, 1)

            def down(t):
                e = expert_of(t)
                pe.wait_ge(hT0_done, t + 1)
                pe.wait_ge(hT1_done, 2 * t + 2)
                at_least(pe, y_done, t)
                for c in range(FC):
                    n = P if c < FC - 1 else FL
                    last = mm(YB[:, 0:D], hT[0:n, c, :], wd[0:n, bass.ds(e, 1), c, :].rearrange("p o n -> p (o n)"),
                              c == 0, c == FC - 1)
                last.then_inc(y_ready, 1)

            def body(t, s, first=False, last=False):
                if first:
                    turn_z(t, s)
                else:
                    turn_h(t - 1)
                if not last:
                    turn_z(t + 1, 1 - s)
                up(t, s)
                if first:
                    pe.wait_ge(wd_in, 16 * E)
                else:
                    down(t - 1)

            mm(YB[:, 0:E], ones, chosen[:, :]).then_inc(cnt_ready, 1)
            pe.wait_ge(info_done, 2)
            pe.wait_ge(w_in, 16 * 2 * E)
            tiles(pe, body)
            turn_h(NSLOT - 1)
            down(NSLOT - 1)

        @block.scalar
        def _(act):
            def silu(t):
                act.wait_ge(g_ready, t + 1)
                at_least(act, h_done, t)
                nc.scalar.activation(sg[:, :, :], GB[:, :, 0:FH], ACT.Silu).then_inc(silu_done, 1)

            def take_h0(t):
                act.wait_ge(hT_ready, 2 * t + 1)
                at_least(act, y_ready, t)
                nc.scalar.activation(hT[:, 0:4, :].rearrange("p c n -> p (c n)"), HB[0][:, :], ACT.Copy
                                     ).then_inc(hT0_done, 1)

            def take_y(t, s):
                act.wait_ge(y_ready, t + 1)
                act.wait_ge(oi_done, t + 1)
                nc.scalar.activation(yb[:, s, :], YB[:, 0:D], ACT.Copy, scale=oi[:, s, 2:3].bitcast(F32)
                                     ).then_inc(y_done, 1)

            def body(t, s, first=False, last=False):
                if not first:
                    take_h0(t - 1)
                silu(t)
                if not first:
                    take_y(t - 1, 1 - s)

            tiles(act, body)
            take_h0(NSLOT - 1)
            take_y(NSLOT - 1, 1)

        @block.vector
        def _(dve):
            V = nc.vector
            k = [0]

            def link(ins):
                k[0] += 1
                ins.then_inc(plan, 1)
                dve.wait_ge(plan, k[0])

            dve.wait_ge(cnt_ready, 1)
            link(V.tensor_scalar(cnti[:, :], YB[:, 0:E], float(P - 1), None, ALU.add))
            link(V.tensor_scalar(cnti[:, :], cnti[:, :], 7, None, ALU.logical_shift_right))
            link(V.tensor_copy(cnt[:, 0, :], cnti[:, :]))
            link(V.tensor_tensor_scan(cnt[:, 1, :], ones[:, 0:E], cnt[:, 0, :], 0.0, ALU.mult, ALU.add))
            number = cst("iotat")
            link(V.tensor_tensor(past[:, 0], number.unsqueeze(2).broadcast_to([P, NSLOT, E]),
                                 cnt[:, 1, :].unsqueeze(1).broadcast_to([P, NSLOT, E]), ALU.is_ge))
            link(V.tensor_tensor(past[:, 1], past[:, 0], cnt[:, 0, :].unsqueeze(1).broadcast_to([P, NSLOT, E]), ALU.mult))
            link(V.tensor_reduce(tl[:, 0, :], past[:, 0], AX.X, ALU.add))
            link(V.tensor_reduce(tl[:, 1, :], past[:, 1], AX.X, ALU.add))
            link(V.tensor_tensor(tl[:, 2, :], number, tl[:, 1, :], ALU.subtract))
            link(V.scalar_tensor_tensor(tl[:, 3, :], tl[:, 0, :], float(TPE), tl[:, 2, :], ALU.mult, ALU.add))
            link(V.tensor_scalar(tl[:, 4, :], tl[:, 0, :], float(E - 1), None, ALU.min))
            V.tensor_copy(info[:, 0, :], tl[:, 3, :]).then_inc(info_done, 1)
            V.tensor_copy(info[:, 1, :], tl[:, 4, :]).then_inc(info_done, 1)

            def take_z(t, s):
                dve.wait_ge(zT_ready, t + 1)
                at_least(dve, u_ready, t - 1)
                V.tensor_copy(zT[:, s, :, :].rearrange("p a n -> p (a n)"), ZB[:, 0:NH * P]).then_inc(zT_done, 1)

            def gate_up(t):
                dve.wait_ge(silu_done, t + 1)
                dve.wait_ge(u_ready, t + 1)
                at_least(dve, hT_ready, 2 * t)
                V.tensor_tensor(hb[:, :].rearrange("p (f n) -> p f n", f=2), sg[:, :, :], UB[:, :, 0:FH], ALU.mult
                                ).then_inc(h_done, 1)

            def take_h1(t):
                dve.wait_ge(hT_ready, 2 * t + 2)
                at_least(dve, y_ready, t)
                V.tensor_copy(hT[:, 4, :], HB[1][:, 0:P]).then_inc(hT1_done, 1)
                V.tensor_copy(hT[0:FL, 5, :], HB[1][0:FL, P:2 * P]).then_inc(hT1_done, 1)

            def body(t, s, first=False, last=False):
                if first:
                    take_z(t, s)
                else:
                    take_h1(t - 1)
                if not last:
                    take_z(t + 1, 1 - s)
                gate_up(t)

            tiles(dve, body)
            take_h1(NSLOT - 1)

        @block.gpsimd
        def _(pool):
            G = nc.gpsimd

            def owners(dst, t, done, *more):
                col = G.value_load(info[0:1, 0, bass.ds(t, 1)], min_val=0, max_val=TCOL - 1)
                G.tensor_copy(dst.unsqueeze(1), tab[:, bass.ds(col, 1), :]).then_inc(done, 1)
                held(pool, (tab_in, 16), (done, t + 1), *more)

            def gather(t, s):
                at_least(pool, zT_ready, t - 1)
                owners(gi[:, s, :], t, gi_done)
                G.indirect_dma_start(zg[:, s, :], None, zbuf[:, :],
                                     bass.IndirectOffsetOnAxis(gi[:, s, 0:1].bitcast(U32), 0)).then_inc(zg_in[s], 16)

            def scatter(t, s):
                owners(oi[:, s, :], t, oi_done, (y_done, t + 1), (y_out, 16 * t))
                G.indirect_dma_start(outd[:, :], bass.IndirectOffsetOnAxis(oi[:, s, 1:2].bitcast(U32), 0),
                                     yb[:, s, :], None, compute_op=ALU.add).then_inc(y_out, 16)

            def body(t, s, first=False, last=False):
                if not last:
                    gather(t + 2, s) if not isinstance(t, int) or t + 2 < NSLOT else None
                if not first:
                    scatter(t - 1, 1 - s)

            pool.wait_ge(info_done, 2)
            pool.wait_ge(tab_in, 16)
            gather(0, 0)
            gather(1, 1)
            body(0, 0, first=True)
            body(1, 1)
            body(2, 0)
            with pool.Fori(3, NSLOT - 3, 2) as t:
                body(t, 1)
                body(t + 1, 0)
            body(NSLOT - 3, 1)
            body(NSLOT - 2, 0, last=True)
            body(NSLOT - 1, 1, last=True)
            scatter(NSLOT - 1, 1)
            pool.wait_ge(y_out, 16 * NSLOT)


def kernel(**inputs):
    import numpy as np
    import concourse.bacc as bacc
    from concourse.bass_utils import run_bass_kernel_spmd as run

    a = {k: np.asarray(v) for k, v in inputs.items()}

    def rows(w):
        return np.ascontiguousarray(w.reshape(-1, P, w.shape[1]).transpose(1, 0, 2)).reshape(P, -1)

    def wide(x):
        return np.broadcast_to(x.reshape(1, -1), (P, x.size))

    w_in = a["L0_attn_W_in"].T
    packed = dict(wq=rows(a["L0_xattn_Wq"].T), wk=rows(a["L0_xattn_Wk"].T), wv=rows(a["L0_xattn_Wv"].T),
                  wo=rows(a["L0_xattn_Wo"].T), wdt=rows(w_in[:, 3 * D:]),
                  wout=rows(a["L0_attn_W_out"].T), wrt=rows(a["L0_ffn_w_router"].T),
                  bq=a["L0_xattn_bq"].reshape(NH, P).T, bk=a["L0_xattn_bk"].reshape(NH, P).T,
                  bv=a["L0_xattn_bv"].reshape(NH, P).T, bo=wide(a["L0_xattn_bo"]), convw=rows(a["L0_attn_conv_w"]),
                  convb=a["L0_attn_conv_b"].reshape(NC, P).T, apar=wide(a["L0_attn_A_param"]),
                  dtb=wide(a["L0_attn_dt_bias"]))
    par = np.concatenate([packed[n] for n in PARAMS], axis=1)

    p, f32 = np.arange(P)[:, None], np.float32
    ch, q = np.arange(D)[None], np.arange(Q)[None]
    m = np.arange(P)[None]
    const = dict(ident=p == m, sel=p % Q == q, hm=p // HD % HG == np.arange(HG),
                 bm=p // HD == np.arange(2 * HG), dm=p // Q == np.arange(HG), er=ch // HD == p,
                 ep=ch // HD == p - H, trib=(p // Q == m // Q) & (p <= m), tris=p < m, ones=p + m >= 0,
                 gt=p > q, le=p <= q, bm8=p // HD == np.arange(P // HD), iota8=p * 0 + np.arange(E),
                 iotat=p * 0 + np.arange(NSLOT), tok=p + np.array([0, 0, 0, 0]), nhalf=p * 0 - 0.5,
                 eps=p * 0 + EPS)
    con = np.concatenate([const[n].astype(f32) for n in CONSTS], axis=1)
    pad = np.zeros((P, TCOL, 4), np.int32)
    pad[:, :, 1] = TOK + p

    ctx = a["ctx_1024"]
    ctxT = np.zeros((P, B, NH, SP), ctx.dtype)
    ctxT[..., :S] = ctx.transpose(2, 0, 1).reshape(NH, P, B, S).transpose(1, 2, 0, 3)
    down = np.zeros((E, FC * P, D), ctx.dtype)
    down[:, :F] = a["L0_ffn_w_down"]

    def cols(w):
        return w.reshape(E, -1, P, w.shape[2]).transpose(2, 0, 1, 3)

    arrays = dict(x=a["x"].reshape(TOK, D), ctx=ctxT, ctx_last=ctxT[:, :, :, LAST].transpose(0, 2, 1),
                  mask=a["mask_BxSxS2_ff0"], par=par, wxbc=rows(w_in[:, :3 * D]).reshape(P, NH, 3 * D),
                  con=con, pad=pad.reshape(P, -1),
                  wg=cols(a["L0_ffn_w_gate"]), wu=cols(a["L0_ffn_w_up"]), wd=cols(down))
    arrays = {f"in_{k}": np.ascontiguousarray(v) for k, v in arrays.items()}
    nc = bacc.Bacc("TRN2", target_bir_lowering=False, num_devices=1)
    aps = [nc.dram_tensor(k, v.shape, mybir.dt.from_np(v.dtype), kind="ExternalInput").ap() for k, v in arrays.items()]
    out = nc.dram_tensor("out", (TOK + P, D), F32, kind="ExternalOutput").ap()
    perceiver(nc, *aps, out)
    r = run(nc, [arrays], core_ids=[0])
    return r.results[0]["out"][:TOK].reshape(B, Q, D)
```

```python
import concourse.bass as bass
from concourse import mybir
from contextlib import ExitStack

F32 = mybir.dt.float32
F32R = mybir.dt.float32r
I32 = mybir.dt.int32
U32 = mybir.dt.uint32
ALU = mybir.AluOpType
ACT = mybir.ActivationFunctionType
AX = mybir.AxisListType

P = 128
B, Q, S, D = 128, 32, 257, 256
H, HD = 16, 16
E, F, TOPK = 8, 704, 2
NH = D // P
SP = S + 1
TB = P // Q
NT = B * Q // P
TOK = B * Q
HG = P // Q
NG = H // HG
GW = HG * HD
TC = 2
LAST = TC * P
KC = 4
NC = 3 * D // P
EPS = 1e-5
FC = (F + P - 1) // P
FL = F - (FC - 1) * P
DV = 4
FH = F // 2
NSLOT = (TOK * TOPK + E * (P - 1)) // P
assert NSLOT % 2 == 1
TPE = TOK // P
TCOL = (E + 1) * TPE
ATANH = [2 * k + 1 for k in range(7, 0, -1)]

PARAMS = dict(wq=NH * D, wk=NH * D, wv=NH * D, wo=NH * D, wdt=NH * H, wout=NH * D,
              wrt=NH * E, bq=NH, bk=NH, bv=NH, bo=D, convw=NC * KC, convb=NC, apar=H, dtb=H)
CONSTS = dict(ident=P, sel=Q, hm=HG, bm=2 * HG, dm=HG, er=D, ep=D, trib=P, tris=P, ones=P, gt=Q, le=Q,
              bm8=P // HD, iota8=E, tok=2 * TOPK, nhalf=1, eps=1)


def columns(widths):
    at, out = 0, {}
    for name, w in widths.items():
        out[name] = (at, at + w)
        at += w
    return out, at


PCOL, NPAR = columns(PARAMS)
CCOL, NCON = columns(CONSTS)


def held(eng, met, *waits):
    for _, value in waits:
        if not isinstance(value, int):
            eng.compute_val(value)
    eng.wait_ge(*met)
    for sem, value in waits:
        at_least(eng, sem, value)


def at_least(eng, sem, value):
    if not isinstance(value, int) or value > 0:
        eng.wait_ge(sem, value)


def perceiver(nc, xd, ctxd, ctxl, maskd, pard, wxbcd, cond, padd, wgd, wud, wdd, outd):
    zbuf = nc.dram_tensor("zbuf", (TOK, D), F32).ap()
    table = nc.dram_tensor("slot_table", (P * TCOL, 4), I32).ap()
    keep = ExitStack()
    with keep:
        con = keep.enter_context(nc.sbuf_tensor("con", [P, NCON], F32))
        wg = keep.enter_context(nc.sbuf_tensor("wg", [P, E, NH, F], F32))
        wu = keep.enter_context(nc.sbuf_tensor("wu", [P, E, NH, F], F32))
        wd = keep.enter_context(nc.sbuf_tensor("wd", [P, E, FC, D], F32))
        par = keep.enter_context(nc.sbuf_tensor("par", [P, NPAR], F32))
        tab = par[:, 0:TCOL * 4].bitcast(I32).rearrange("p (n c) -> p n c", c=4)
        assert TCOL * 4 <= 3 * NH * D
        info = keep.enter_context(nc.sbuf_tensor("info", [P, 2, NSLOT + 1], I32))
        tab_in = keep.enter_context(nc.semaphore("tab_in"))
        info_done = keep.enter_context(nc.semaphore("info_done"))
        w_in = keep.enter_context(nc.semaphore("w_in"))
        wd_in = keep.enter_context(nc.semaphore("wd_in"))

        def cst(name):
            a, b = CCOL[name]
            return con[:, a:b]

        attend(nc, xd, ctxd, ctxl, maskd, pard, wxbcd, cond, padd, wgd, wud, wdd, zbuf, table, outd, con, cst, wg, wu, wd,
               par, tab, info, tab_in, info_done, w_in, wd_in)
        spare = [par[:, TCOL * 4:], con[:, CCOL["er"][0]:CCOL["tris"][1]]]
        experts(nc, zbuf, outd, cst, spare, wg, wu, wd, tab, info, tab_in, info_done, w_in, wd_in)


def runs(i):
    return not isinstance(i, int) or 0 <= i < NT


def attend(nc, xd, ctxd, ctxl, maskd, pard, wxbcd, cond, padd, wgd, wud, wdd, zbuf, table, outd, con, cst, wg, wu, wd,
           par, tab, info, tab_in, info_done, w_in, wd_in):
    own = ExitStack()
    with own:
        def sb(name, shape, dt=F32):
            return own.enter_context(nc.sbuf_tensor(name, shape, dt))

        def ps(name):
            return own.enter_context(nc.psum_tensor(name, [P, 512], F32))

        def sem(name):
            return own.enter_context(nc.semaphore(name))

        chosen = sb("chosen", [P, E])
        cnt = sb("cnt", [P, 2, E])
        cnti = sb("cnti", [P, E], I32)
        past = sb("past", [P, 2, E])
        tl = sb("tl", [P, 5])

        def prm(name):
            a, b = PCOL[name]
            return par[:, a:b]

        def halves(name):
            return prm(name).rearrange("p (a n) -> p a n", a=NH)

        wq, wk, wv, wo = (halves(n) for n in ("wq", "wk", "wv", "wo"))
        wdt, wout, wrt = (halves(n) for n in ("wdt", "wout", "wrt"))
        ident, ones = cst("ident"), cst("ones")

        room = wd[:, :, :, :].rearrange("p e c d -> p (e c d)")
        used = [0]

        def part(n):
            used[0] += n
            assert used[0] <= E * FC * D
            return room[:, used[0] - n:used[0]]

        ctx = part(TB * NH * SP).rearrange("p (b c t) -> p b c t", b=TB, c=NH)
        ctx_hi = sb("ctx_hi", [P, 2, NH, SP], F32R)
        ctx_lo = sb("ctx_lo", [P, 2, NH, SP], F32R)
        wkh, wvh = sb("wkh", [P, NH, D], F32R), sb("wvh", [P, NH, D], F32R)
        wkl, wvl = sb("wkl", [P, NH, D], F32R), sb("wvl", [P, NH, D], F32R)
        msk = part(TB * S).rearrange("p (b t) -> p b t", b=TB)
        qbd = [sb(f"qbd_{h}", [P, 2, NG, P], F32R) for h in ("hi", "lo")]
        kT = [sb(f"kT_{h}", [P, NH, SP], F32R) for h in ("hi", "lo")]
        v = part(2 * TC * D).rearrange("p (b t d) -> p b t d", b=2, t=TC)
        sm = part(NG * S).rearrange("p (g t) -> p g t", g=NG)
        pr = part(NG * S).rearrange("p (g t) -> p g t", g=NG)
        pT = part(NG * TC * P).rearrange("p (g t n) -> p g t n", g=NG, t=TC)
        mx = sb("mx", [P, NG])
        nmx = sb("nmx", [P, NG])
        rsum = sb("rsum", [P, NG])
        rr = sb("rr", [P, 2, NG])
        px = sb("px", [P, 2 * NG, HG])
        om = sb("om", [P, NH, HG, Q])
        ou = sb("ou", [P, NH, P])
        rp = sb("rp", [2 * H, P])
        vl = sb("vl", [P, NH, B])
        kl = part(NH * B).rearrange("p (a n) -> p a n", a=NH)
        kl_parts = [sb(f"kl_{h}", [P, NH, B], F32R) for h in ("hi", "lo")]
        xt, z1 = part(D), part(D)
        z1T, qs = (part(NH * P).rearrange("p (a n) -> p a n", a=NH) for _ in range(2))
        q_parts = [sb(f"q_{h}", [P, NH, P], F32R) for h in ("hi", "lo")]
        xr, t1, t2, aT = sb("xr", [P, D]), sb("t1", [P, NH, P]), sb("t2", [P, NH, P]), sb("aT", [P, NH, P])
        x1, z2, z2T, yn = sb("x1", [P, D]), sb("z2", [P, D]), sb("z2T", [P, NH, P]), sb("yn", [P, D])
        ynT, z3, z3T = sb("ynT", [P, NH, P]), sb("z3", [P, D]), sb("z3T", [P, NH, P])
        y0, xk, x2 = sb("y0", [P, D]), sb("xk", [P, D]), sb("x2", [P, D])
        st = sb("st", [P, 3, 6])
        mv = sb("mv", [P, 3, 2])
        rs = sb("rs", [P, 3, 2])
        dtv = sb("dtv", [P, 11, H])
        lg = sb("lg", [P, 4, E])
        mi = sb("mi", [P, 8], U32)
        oh = sb("oh", [P, TOPK, E])
        ohr = sb("ohr", [P, TOPK, E])
        sv = sb("sv", [P, 8, TOPK])
        ri = sb("ri", [P, 3, TOPK], I32)
        pay = sb("pay", [P, TOPK, 4], I32)
        tokf = sb("tokf", [P, 2 * TOPK])
        spare = wg[:, :, :, :].rearrange("p e c n -> p (e c n)")
        cut = [0]

        def carve(n):
            cut[0] += n
            assert cut[0] <= E * NH * F
            return spare[:, cut[0] - n:cut[0]]

        wxbc = carve(NH * 3 * D).rearrange("p (a n) -> p a n", a=NH)
        ctl = carve(NH * B).rearrange("p (a n) -> p a n", a=NH)
        xp = carve(NC * (Q + KC - 1)).rearrange("p (c l) -> p c l", c=NC)
        cv = carve(2 * NC * Q).rearrange("p (k c l) -> p k c l", k=2, c=NC)
        cT = carve(NC * Q).rearrange("p (c l) -> p c l", c=NC)
        cbd = carve(NH * 8 * Q).rearrange("p (a h l) -> p a h l", a=NH, h=8)
        gs, at_, ls, ws = (carve(H * Q)[0:Q].rearrange("p (h l) -> p h l", h=H) for _ in range(4))
        w4 = carve(H * P)[0:Q].rearrange("p (h b l) -> p h b l", h=H, b=TB)
        xs = carve(D)[0:Q]

        K, V_ = ps("k"), ps("v_p")
        K2 = K[:, 0:NH * LAST].rearrange("p (a t) -> p a t", a=NH)
        SC = [ps("sc0"), ps("sc1")]
        PT = [ps("pt0"), ps("pt1")]
        O = ps("o")
        M = ps("m")
        OT = O[:, 0:NH * P].rearrange("p (a h q) -> p a h q", a=NH, h=HG)
        RP = O[0:2 * H, NH * P:NH * P + Q]
        M2 = M[:, 0:NH * P].rearrange("p (a n) -> p a n", a=NH)
        M2K = M[:, NH * P:2 * NH * P].rearrange("p (a n) -> p a n", a=NH)
        RK = M[:, 2 * H:2 * H + E]

        par_in, con_in, ctl_in, pad_in = sem("par_in"), sem("con_in"), sem("ctl_in"), sem("pad_in")
        wxbc_in = sem("wxbc_in")
        hi_done, lo_done, wh_done, wl_done = sem("hi_done"), sem("lo_done"), sem("wh_done"), sem("wl_done")
        ctx_in = [sem(f"ctx_in{b}") for b in range(TB)]
        msk_in = [sem(f"msk_in{b}") for b in range(TB)]
        xt_in, xr_in, z3_out, slots_out = sem("xt_in"), sem("xr_in"), sem("z3_out"), sem("slots_out")
        x2_out, blank_out = sem("x2_out"), sem("blank_out")
        vl_ready, vl_done, kl_sum, kl_high, kl_low, lows_done, q_high = (
            sem("vl_ready"), sem("vl_done"), sem("kl_sum"), sem("kl_high"), sem("kl_low"), sem("lows_done"),
            sem("q_high"))
        q_split = sem("q_split")
        k_ready, k_done, v_ready, v_done = sem("k_ready"), sem("k_done"), sem("v_ready"), sem("v_done")
        s_ready, max_done, nmx_done, exp_done = sem("s_ready"), sem("max_done"), sem("nmx_done"), sem("exp_done")
        pt_ready, pt_done = sem("pt_ready"), sem("pt_done")
        rec_done, pl_done, px_done = sem("rec_done"), sem("pl_done"), sem("px_done")
        o_ready, om_done, ou_done, rp_done = sem("o_ready"), sem("om_done"), sem("ou_done"), sem("rp_done")
        st1, mv1, var1, rstd1, z1_done = sem("st1"), sem("mv1"), sem("var1"), sem("rstd1"), sem("z1_done")
        z1T_ready, z1T_done, q_ready, qs_done, qbd_done = (sem("z1T_ready"), sem("z1T_done"), sem("q_ready"),
                                                           sem("qs_done"), sem("qbd_done"))
        ex_ready, t_done, t3_done, aT_done = sem("ex_ready"), sem("t_done"), sem("t3_done"), sem("aT_done")
        wo_ready, xb_done, x1_done, kept = sem("wo_ready"), sem("xb_done"), sem("x1_done"), sem("kept")
        st2, mv2, var2, rstd2, z2_done = sem("st2"), sem("mv2"), sem("var2"), sem("rstd2"), sem("z2_done")
        z2T_ready, z2T_done = sem("z2T_ready"), sem("z2T_done")
        dt_ready, dt_done, nabs_done, u_done, soft, a_done = (sem("dt_ready"), sem("dt_done"), sem("nabs_done"),
                                                              sem("u_done"), sem("soft"), sem("a_done"))
        cum_ready, ep_done, en_done, c2_ready = sem("cum_ready"), sem("ep_done"), sem("en_done"), sem("c2_ready")
        norm_done, rn_done, yn_done = sem("norm_done"), sem("rn_done"), sem("yn_done")
        ynT_ready, ynT_done, y_ready, x2_done = sem("ynT_ready"), sem("ynT_done"), sem("y_ready"), sem("x2_done")
        st3, mv3, var3, rstd3, z3_done = sem("st3"), sem("mv3"), sem("var3"), sem("rstd3"), sem("z3_done")
        z3T_ready, z3T_done, lg_ready, lg_done = sem("z3T_ready"), sem("z3T_done"), sem("lg_ready"), sem("lg_done")
        top_done, index_done, expert_done, oh_done, mm_done, diff_done, gate_e = (
            sem("top_done"), sem("index_done"), sem("expert_done"), sem("oh_done"), sem("mm_done"), sem("diff_done"),
            sem("gate_e"))
        ranked, rank_done, gate_sum, whole, col_done, row_a, row_b = (
            sem("ranked"), sem("rank_done"), sem("gate_sum"), sem("whole"), sem("col_done"), sem("row_a"), sem("row_b"))
        pay_done, chosen_done = sem("pay_done"), sem("chosen_done")
        ssd_pe, ssd_act, ssd_dve = sem("ssd_pe"), sem("ssd_act"), sem("ssd_dve")
        init, soft_sum, soft_max = sem("init"), sem("soft_sum"), sem("soft_max")
        NSOFT = len(ATANH) + 5
        PLAN = 10

        cnt_ready, plan, plan_ready = sem("cnt_ready"), sem("plan"), sem("plan_ready")

        block = own.enter_context(nc.Block())

        def steps(eng, tile):
            for i in range(4):
                tile(i)
            with eng.Fori(4, NT - 3) as i:
                tile(i)
            for i in range(NT - 3, NT + 3):
                tile(i)

        def following(i, b, by=1):
            return i + (b + by) // TB, (b + by) % TB

        @block.sync
        def _(sp):
            def load_ctx(i, b):
                if not (isinstance(i, int) and i == 0):
                    sp.wait_ge(lo_done, 4 * i + b - 3)
                sp.dma_start(ctx[:, b:b + 1], ctxd[:, bass.ds(4 * i + b, 1), :, :]).then_inc(ctx_in[b], 16)

            def load_mask(i, b):
                if not (isinstance(i, int) and i == 0):
                    sp.wait_ge(max_done, 4 * (4 * i + b - 3))
                for h in range(HG):
                    sp.dma_start(msk[h * Q:(h + 1) * Q, b:b + 1, :],
                                 maskd[bass.ds(4 * i + b, 1), :, :].rearrange("b q t -> q b t")
                                 ).then_inc(msk_in[b], 16)

            def load_x(i):
                if not (isinstance(i, int) and i == 0):
                    sp.wait_ge(z1_done, i)
                sp.dma_start(xt[:, :], xd[bass.ds(P * i, P), :]).then_inc(xt_in, 16)

            def load_residual(j):
                if not (isinstance(j, int) and j == 0):
                    sp.wait_ge(x1_done, j)
                sp.dma_start(xr[:, :], xd[bass.ds(P * j, P), :]).then_inc(xr_in, 16)

            def store_z3(j):
                sp.wait_ge(z3_done, j + 1)
                sp.dma_start(outd[bass.ds(P * j, P), :], x2[:, :]).then_inc(x2_out, 16)
                sp.dma_start(zbuf[bass.ds(P * j, P), :], z3[:, :]).then_inc(z3_out, 16)

            load_x(0)
            sp.dma_start(con[:, :], cond).then_inc(con_in, 16)
            sp.dma_start(par[:, :], pard).then_inc(par_in, 16)
            load_ctx(0, 0)
            sp.dma_start(ctl, ctxl).then_inc(ctl_in, 16)
            load_mask(0, 0)
            load_x(1)
            for b in range(1, TB):
                load_ctx(0, b)
                load_mask(0, b)
            load_x(2)
            load_residual(0)
            sp.dma_start(outd[TOK:TOK + P, :], xd[0:P, :]).then_inc(blank_out, 16)
            sp.dma_start(wxbc, wxbcd).then_inc(wxbc_in, 16)
            sp.dma_start(table.rearrange("(p n) c -> p (n c)", p=P), padd).then_inc(pad_in, 16)

            def load_expert(e):
                one = bass.ds(e, 1)
                sp.dma_start(wg[:, one], wgd[:, one]).then_inc(w_in, 16)
                sp.dma_start(wu[:, one], wud[:, one]).then_inc(w_in, 16)

            def tile(i):
                for b in range(TB):
                    if runs(i + 1):
                        load_mask(i + 1, b)
                        load_ctx(i + 1, b)
                    if b == 2 and runs(i) and not (isinstance(i, int) and i == 0):
                        load_residual(i)
                    if b == 3 and runs(i - 2):
                        store_z3(i - 2)
                    if b == 3 and runs(i + 3):
                        load_x(i + 3)

            tile(0), tile(1), tile(2)
            sp.wait_ge(ssd_act, 4)
            sp.wait_ge(vl_done, 3)
            with sp.Fori(3, 3 + E) as i:
                tile(i)
                load_expert(i - 3)
            with sp.Fori(3 + E, NT - 3) as i:
                tile(i)
            for i in range(NT - 3, NT):
                tile(i)
            sp.wait_ge(o_ready, B)
            sp.wait_ge(px_done, B)
            for e in range(E):
                sp.dma_start(wd[:, e], wdd[:, e]).then_inc(wd_in, 16)
            tile(NT), tile(NT + 1)
            sp.wait_ge(z3_out, 16 * NT)
            sp.wait_ge(x2_out, 16 * NT)
            sp.wait_ge(blank_out, 16)
            sp.wait_ge(slots_out, 32 * NT)
            sp.dma_start(tab[:, :, :], table.rearrange("(p n) c -> p n c", p=P)).then_inc(tab_in, 16)

        @block.tensor
        def _(pe):
            def mm(out, lhsT, rhs, start=True, stop=True):
                return nc.tensor.matmul(out, lhsT, rhs, start=start, stop=stop)

            def last_values():
                pe.wait_ge(par_in, 16)
                pe.wait_ge(con_in, 16)
                pe.wait_ge(ctl_in, 16)
                for a in range(NH):
                    for c in range(NH):
                        mm(M2[:, a, :], wv[:, c, a * P:(a + 1) * P], ctl[:, c, :], c == 0, c == NH - 1)
                    for c in range(NH):
                        last = mm(M2K[:, a, :], wk[:, c, a * P:(a + 1) * P], ctl[:, c, :], c == 0, c == NH - 1)
                last.then_inc(vl_ready, 1)

            def project_k(i, b):
                n = 4 * i + b
                pe.wait_ge(lo_done, n + 1)
                hi, lo = ctx_hi[:, b % 2], ctx_lo[:, b % 2]
                at_least(pe, lows_done, 2 * n)
                for a in range(NH):
                    for c in range(NH):
                        for k, (w, x) in enumerate(((wkh, hi), (wkh, lo), (wkl, hi))):
                            last = mm(K2[:, a, :], w[:, c, a * P:(a + 1) * P], x[:, c, 0:LAST],
                                      c == 0 and k == 0, c == NH - 1 and k == 2)
                last.then_inc(k_ready, 1)

            def project_v(i, b):
                n = 4 * i + b
                hi, lo = ctx_hi[:, b % 2], ctx_lo[:, b % 2]
                at_least(pe, v_done, n)
                for t in range(TC):
                    for c in range(NH):
                        for k, (x, w) in enumerate(((hi, wvh), (hi, wvl), (lo, wvh))):
                            last = mm(V_[:, t * D:(t + 1) * D], x[:, c, t * P:(t + 1) * P], w[:, c, :],
                                      c == 0 and k == 0, c == NH - 1 and k == 2)
                last.then_inc(v_ready, 1)

            def scores(i, b, groups):
                n = 4 * i + b
                pe.wait_ge(qbd_done, 4 * n + 4)
                pe.wait_ge(k_done, 4 * n + 4)
                pe.wait_ge(lows_done, 2 * n + 2)
                for g in groups:
                    at_least(pe, max_done, 4 * n + g - 1)
                    for k, (q, x) in enumerate(((0, 0), (0, 1), (1, 0))):
                        last = mm(SC[g % 2][:, 0:SP], qbd[q][:, b % 2, g, :], kT[x][:, g // 2, :], k == 0, k == 2)
                    last.then_inc(s_ready, 1)

            def transpose_probs(i, b):
                n = 4 * i + b
                for d in range(2):
                    pe.wait_ge(exp_done, 4 * n + 2 * d + 2)
                    at_least(pe, pt_done, 2 * n + d - 1)
                    for g in (2 * d, 2 * d + 1):
                        for t in range(TC):
                            o = ((g % 2) * TC + t) * P
                            last = nc.tensor.transpose(PT[d][:, o:o + P], pr[:, g, t * P:(t + 1) * P], ident)
                    last.then_inc(pt_ready, 1)

            def weigh_values(i, b):
                n = 4 * i + b
                pe.wait_ge(pt_done, 2 * n + 2)
                pe.wait_ge(v_done, n + 1)
                at_least(pe, om_done, n)
                at_least(pe, rp_done, n)
                for a in range(NH):
                    for t in range(TC):
                        for g in (2 * a, 2 * a + 1):
                            r = (g % 2) * GW
                            mm(O[r:r + GW, a * P:(a + 1) * P], v[:, b % 2, t, g * GW:(g + 1) * GW], pT[:, g, t, :],
                               t == 0, t == TC - 1)
                pe.wait_ge(px_done, n + 1)
                mm(RP, px[:, :, :].rearrange("p n h -> p (n h)"), cst("sel")).then_inc(o_ready, 1)

            def transpose2(src, done):
                for a in range(NH):
                    last = nc.tensor.transpose(M2[:, a, :], src[:, a * P:(a + 1) * P], ident)
                last.then_inc(done, 1)

            def turn_z1(i):
                pe.wait_ge(z1_done, i + 1)
                transpose2(z1, z1T_ready)

            def queries(i):
                pe.wait_ge(z1T_done, i + 1)
                for a in range(NH):
                    for c in range(NH):
                        last = mm(M2[:, a, :], wq[:, c, a * P:(a + 1) * P], z1T[:, c, :], c == 0, c == NH - 1)
                last.then_inc(q_ready, 1)

            def expand(j):
                pe.wait_ge(rp_done, 4 * (j + 1))
                for k, e in enumerate(("er", "ep")):
                    for a in range(NH):
                        o = (k * NH + a) * P
                        last = mm(M[:, o:o + P], cst(e)[0:2 * H, a * P:(a + 1) * P], rp[:, :])
                last.then_inc(ex_ready, 1)

            def project_out(j):
                pe.wait_ge(aT_done, NH * (j + 1))
                for a in range(NH):
                    last = mm(M[:, 0:D], aT[:, a, :], wo[:, a, :], a == 0, a == NH - 1)
                last.then_inc(wo_ready, 1)

            def turn_z2(j):
                pe.wait_ge(z2_done, j + 1)
                transpose2(z2, z2T_ready)

            def project_dt(j):
                pe.wait_ge(z2T_done, j + 1)
                for a in range(NH):
                    last = mm(M[:, 0:H], z2T[:, a, :], wdt[:, a, :], a == 0, a == NH - 1)
                last.then_inc(dt_ready, 1)

            def sum_a(j):
                pe.wait_ge(a_done, j + 1)
                mm(M[:, 0:H], cst("trib"), dtv[:, 5, :]).then_inc(cum_ready, 1)

            def sum_decay_and_rank(j, k):
                if runs(j):
                    pe.wait_ge(en_done, j + 1)
                    last = mm(M[:, 0:H], cst("trib"), dtv[:, 7, :])
                if runs(k):
                    pe.wait_ge(mm_done, k + 1)
                    pe.wait_ge(chosen_done, k + 1)
                    mm(RK, cst("tris"), lg[:, 2, :], True, False)
                    last = mm(RK, ones, chosen[:, :], False, True)
                last.then_inc(c2_ready, 1)

            def turn_y(j):
                pe.wait_ge(yn_done, j + 1)
                transpose2(yn, ynT_ready)

            def project_y(j):
                pe.wait_ge(ynT_done, j + 1)
                for a in range(NH):
                    last = mm(M[:, 0:D], ynT[:, a, :], wout[:, a, :], a == 0, a == NH - 1)
                last.then_inc(y_ready, 1)

            def turn_z3(j):
                pe.wait_ge(z3_done, j + 1)
                transpose2(z3, z3T_ready)

            def router(j):
                pe.wait_ge(z3T_done, j + 1)
                for a in range(NH):
                    last = mm(M[:, 0:E], z3T[:, a, :], wrt[:, a, :], a == 0, a == NH - 1)
                last.then_inc(lg_ready, 1)

            def ssd():
                pe.wait_ge(wxbc_in, 16)
                pe.wait_ge(a_done, 1)
                pe.wait_ge(norm_done, 1)
                for c in range(NC):
                    for a in range(NH):
                        last = mm(M[:, c * Q:(c + 1) * Q], wxbc[:, a, c * P:(c + 1) * P], z2T[:, a, 0:Q],
                                  a == 0, a == NH - 1)
                last.then_inc(ssd_pe, 1)
                pe.wait_ge(ssd_dve, 11)
                for a in range(NH):
                    last = mm(M[0:Q, a * 8 * Q:(a + 1) * 8 * Q], cT[:, 2 + a, :],
                              cbd[:, a, :, :].rearrange("p h l -> p (h l)"))
                last.then_inc(ssd_pe, 1)
                pe.wait_ge(ssd_act, 1)
                pe.wait_ge(ssd_dve, 12)
                mm(M[0:Q, :], cst("gt")[0:Q, :], at_[:, :, :].rearrange("p h l -> p (h l)")).then_inc(ssd_pe, 1)
                pe.wait_ge(ssd_act, 2)
                for a in range(NH):
                    last = nc.tensor.transpose(M[0:Q, a * P:(a + 1) * P], cT[:, 4 + a, :], ident)
                last.then_inc(ssd_pe, 1)
                pe.wait_ge(ssd_act, 3)
                pe.wait_ge(ssd_dve, 14)
                for h in range(H):
                    last = mm(M[:, h * HD:(h + 1) * HD], w4[:, h, :, :].rearrange("p b l -> p (b l)"),
                              xs[:, h * HD:(h + 1) * HD])
                last.then_inc(ssd_pe, 1)
                pe.wait_ge(ssd_act, 4)

            def turn_a(i, b):
                if b == 0 and runs(i - 1):
                    if runs(i - 2):
                        pe.wait_ge(en_done, i - 1)
                    if isinstance(i, int) and i == 1:
                        pe.wait_ge(z1T_done, 3)
                    expand(i - 1)
                if b == 1 and runs(i - 2):
                    if runs(i - 1):
                        pe.wait_ge(x1_done, i)
                    else:
                        pe.wait_ge(chosen_done, i - 1)
                    turn_y(i - 2)
                if b == 2 and runs(i + 1):
                    if runs(i - 1):
                        pe.wait_ge(z2T_done, i)
                    queries(i + 1)
                if b == 3 and runs(i - 2):
                    router(i - 2)

            def turn_b(i, b):
                if b == 0 and (runs(i - 2) or runs(i - 3)):
                    if runs(i - 1):
                        pe.wait_ge(t_done, 2 * i)
                    sum_decay_and_rank(i - 2, i - 3)
                    if isinstance(i, int) and i == 2:
                        ssd()
                if b == 1 and runs(i - 2):
                    project_y(i - 2)
                if b == 2 and runs(i - 1):
                    if runs(i + 1):
                        pe.wait_ge(qs_done, NH * (i + 2))
                    project_dt(i - 1)
                if b == 3 and runs(i + 2):
                    if runs(i - 2):
                        pe.wait_ge(lg_done, i - 1)
                    elif runs(i - 1):
                        pe.wait_ge(dt_done, i)
                    else:
                        pe.wait_ge(qs_done, NH * (i + 2))
                    turn_z1(i + 2)

            def turn_c(i, b):
                if b == 0 and runs(i - 1):
                    if runs(i - 2):
                        pe.wait_ge(norm_done, i - 1)
                    if runs(i - 3):
                        pe.wait_ge(chosen_done, i - 1)
                    project_out(i - 1)
                if b == 1 and runs(i - 1):
                    if runs(i - 2):
                        pe.wait_ge(x2_done, i - 1)
                    turn_z2(i - 1)
                if b == 2 and runs(i - 2):
                    if runs(i - 1):
                        pe.wait_ge(dt_done, i)
                    turn_z3(i - 2)
                if b == 3 and runs(i - 1):
                    if runs(i + 2):
                        pe.wait_ge(z1T_done, i + 3)
                    elif runs(i - 2):
                        pe.wait_ge(lg_done, i - 1)
                    sum_a(i - 1)

            def tile(i):
                for b in range(TB):
                    nxt = following(i, b)
                    if runs(nxt[0]):
                        project_k(*nxt)
                        project_v(*nxt)
                    turn_a(i, b)
                    if runs(i):
                        transpose_probs(i, b)
                    if runs(nxt[0]):
                        scores(*nxt, (0, 1))
                    turn_b(i, b)
                    if runs(i):
                        weigh_values(i, b)
                    if runs(nxt[0]):
                        scores(*nxt, (2, 3))
                    turn_c(i, b)

            last_values()
            pe.wait_ge(vl_done, 3)
            turn_z1(0)
            queries(0)
            pe.wait_ge(wl_done, 2)
            project_k(0, 0)
            project_v(0, 0)
            scores(0, 0, range(NG))
            pe.wait_ge(qs_done, NH)
            turn_z1(1)
            steps(pe, tile)
            pe.wait_ge(chosen_done, NT + 1)
            mm(M[:, 0:E], ones, chosen[:, :]).then_inc(cnt_ready, 1)
            pe.wait_ge(plan, PLAN)
            for k in range(2):
                last = mm(M[0:1, (k + 1) * P:(k + 2) * P], tl[:, 3 + k:4 + k], ident)
            last.then_inc(plan_ready, 1)

        @block.scalar
        def _(act):
            def copy(out, in_, **kw):
                return nc.scalar.activation(out, in_, ACT.Copy, **kw)

            def take_keys(i, b):
                n = 4 * i + b
                at_least(act, s_ready, 4 * n)
                act.wait_ge(k_ready, n + 1)
                for a in range(NH):
                    nc.scalar.activation(kT[0][:, a, 0:LAST], K2[:, a, :], ACT.Identity,
                                         bias=prm("bk")[:, a:a + 1]).then_inc(k_done, 1)
                for x, y in zip(kT, kl_parts):
                    copy(x[:, :, LAST:SP], y[:, :, bass.ds(n, 1)].bitcast(F32).broadcast_to([P, NH, SP - LAST])
                         ).then_inc(k_done, 1)

            def split_high(i, b):
                n = 4 * i + b
                act.wait_ge(ctx_in[b], 16 * (i + 1))
                at_least(act, v_ready, n - 1)
                copy(ctx_hi[:, b % 2].rearrange("p c t -> p (c t)"), ctx[:, b].rearrange("p c t -> p (c t)")
                     ).then_inc(hi_done, 1)

            def take_values(i, b):
                n = 4 * i + b
                act.wait_ge(v_ready, n + 1)
                at_least(act, o_ready, n - 1)
                copy(v[:, b % 2, :, :].rearrange("p t d -> p (t d)"), V_[:, :]).then_inc(v_done, 1)

            def exponentials(i, b, *groups):
                n = 4 * i + b
                for g in groups:
                    act.wait_ge(nmx_done, 4 * n + g + 1)
                    if g == 0:
                        at_least(act, px_done, n)
                        at_least(act, rec_done, n)
                        at_least(act, pt_ready, 2 * n)
                    nc.scalar.activation(pr[:, g, :], sm[:, g, :], ACT.Exp, bias=nmx[:, g:g + 1],
                                         accum_out=rsum[:, g:g + 1]).then_inc(exp_done, 1)

            def take_probs(i, b):
                n = 4 * i + b
                for d in range(2):
                    act.wait_ge(pt_ready, 2 * n + d + 1)
                    if d == 0:
                        at_least(act, o_ready, n)
                    copy(pT[:, 2 * d:2 * d + 2, :, :].rearrange("p g t n -> p (g t n)"), PT[d][:, :]).then_inc(pt_done, 1)

            def take_rp(i, b):
                n = 4 * i + b
                act.wait_ge(om_done, n + 1)
                if b == 0:
                    at_least(act, ex_ready, i)
                copy(rp[:, b * Q:(b + 1) * Q], RP).then_inc(rp_done, 1)

            def take2(dst, ready, done, j):
                act.wait_ge(ready, j + 1)
                copy(dst[:, :, :], M2).then_inc(done, 1)

            def take_z1T(i):
                take2(z1T, z1T_ready, z1T_done, i)

            def keep(j):
                act.wait_ge(x1_done, j + 1)
                at_least(act, x2_done, j)
                copy(xk[:, :], x1[:, :]).then_inc(kept, 1)

            def decays(j):
                act.wait_ge(cum_ready, j + 1)
                at_least(act, rn_done, j)
                nc.scalar.activation(dtv[:, 6, :], M[:, 0:H], ACT.Exp).then_inc(ep_done, 1)
                nc.scalar.activation(dtv[:, 7, :], M[:, 0:H], ACT.Exp, scale=-1.0).then_inc(en_done, 1)

            def soft_exp(j):
                act.wait_ge(nabs_done, j + 1)
                nc.scalar.activation(dtv[:, 2, :], dtv[:, 1, :], ACT.Exp).then_inc(u_done, 1)

            def gate_exp(j):
                act.wait_ge(diff_done, j + 1)
                nc.scalar.activation(sv[:, 1, 0:1], sv[:, 0, 0:1], ACT.Exp).then_inc(gate_e, 1)

            def ssd():
                act.wait_ge(ssd_pe, 2)
                copy(gs[:, :, :].rearrange("p h l -> p (h l)"), M[0:Q, :]).then_inc(ssd_act, 1)
                act.wait_ge(ssd_pe, 3)
                nc.scalar.activation(ls[:, :, :].rearrange("p h l -> p (h l)"), M[0:Q, :], ACT.Exp).then_inc(ssd_act, 1)
                act.wait_ge(ssd_pe, 4)
                copy(xs, M[0:Q, 0:D]).then_inc(ssd_act, 1)
                act.wait_ge(ssd_pe, 5)
                copy(y0[:, :], M[:, 0:D]).then_inc(ssd_act, 1)

            def take_z2T(j):
                take2(z2T, z2T_ready, z2T_done, j)

            def take_ynT(j):
                take2(ynT, ynT_ready, ynT_done, j)

            def take_z3T(j):
                take2(z3T, z3T_ready, z3T_done, j)

            def tile(i):
                for b in range(TB):
                    nxt = following(i, b)
                    two = following(i, b, 2)
                    if runs(two[0]):
                        split_high(*two)
                    if b == 1 and runs(i - 2):
                        take_ynT(i - 2)
                    if runs(i):
                        take_probs(i, b)
                    if b == 0 and runs(i - 3):
                        gate_exp(i - 3)
                    if b == 0 and isinstance(i, int) and i == 2:
                        ssd()
                    if b == 3 and runs(i + 2):
                        take_z1T(i + 2)
                    if runs(nxt[0]):
                        exponentials(*nxt, 0, 1)
                        take_values(*nxt)
                    if b == 1 and runs(i - 1):
                        keep(i - 1)
                    if b == 2 and runs(i - 1):
                        soft_exp(i - 1)
                    if runs(nxt[0]):
                        exponentials(*nxt, 2)
                    if b == 1 and runs(i - 1):
                        take_z2T(i - 1)
                    if b == 2 and runs(i - 2):
                        take_z3T(i - 2)
                    if b == 3 and runs(i - 1):
                        decays(i - 1)
                    if runs(nxt[0]):
                        exponentials(*nxt, 3)
                    if runs(i):
                        take_rp(i, b)
                    if runs(two[0]):
                        take_keys(*two)

            act.wait_ge(par_in, 16)
            copy(wkh[:, :, :], wk).then_inc(wh_done, 1)
            copy(wvh[:, :, :], wv).then_inc(wh_done, 1)
            split_high(0, 0)
            take_z1T(0)
            act.wait_ge(kl_low, 1)
            take_keys(0, 0)
            split_high(0, 1)
            take_values(0, 0)
            exponentials(0, 0, 0, 1, 2)
            take_z1T(1)
            exponentials(0, 0, 3)
            take_keys(0, 1)
            steps(act, tile)

        @block.vector
        def _(dve):
            V = nc.vector

            def maxima(i, b, d):
                n = 4 * i + b
                for g in (2 * d, 2 * d + 1):
                    if g == 0:
                        held(dve, (init, 2), (msk_in[b], 64 * (i + 1)), (exp_done, 4 * n), (s_ready, 4 * n + 1))
                    else:
                        held(dve, (init, 2), (s_ready, 4 * n + g + 1))
                    V.tensor_tensor_reduce(sm[:, g, :], SC[g % 2][:, 0:S], msk[:, b, :], 1.0, -3.0e38, ALU.add, ALU.max,
                                           mx[:, g:g + 1]).then_inc(max_done, 1)
                    dve.wait_ge(max_done, 4 * n + g + 1)
                    V.tensor_scalar(nmx[:, g:g + 1], mx[:, g:g + 1], -1.0, None, ALU.mult).then_inc(nmx_done, 1)

            def reciprocals(i, b):
                n = 4 * i + b
                dve.wait_ge(exp_done, 4 * n + 4)
                at_least(dve, px_done, n)
                V.reciprocal(rr[:, 0, :], rsum[:, :]).then_inc(rec_done, 1)

            def take_output(i, b):
                n = 4 * i + b
                dve.wait_ge(o_ready, n + 1)
                at_least(dve, ou_done, n)
                V.tensor_tensor(om[:, :, :, :], OT, cst("hm").unsqueeze(1).unsqueeze(3).broadcast_to([P, NH, HG, Q]),
                                ALU.mult).then_inc(om_done, 1)
                dve.wait_ge(om_done, n + 1)
                V.tensor_reduce(ou[:, :, b * Q:(b + 1) * Q], om[:, :, :, :].rearrange("p a h q -> p a q h"),
                                AX.X, ALU.add).then_inc(ou_done, 1)

            def statistics(src, k, j, s_st, s_mv, s_done):
                V.bn_stats(st[:, k, :], src).then_inc(s_st, 1)
                held(dve, (init, 2), (s_st, j + 1), (s_done, j))
                V.bn_aggr(mv[:, k, :], st[:, k, :]).then_inc(s_mv, 1)

            def statistics1(i):
                held(dve, (init, 2), (xt_in, 16 * (i + 1)))
                statistics(xt[:, :], 0, i, st1, mv1, z1_done)

            def take_queries(i):
                dve.wait_ge(q_ready, i + 1)
                at_least(dve, qbd_done, 16 * i)
                for a in range(NH):
                    V.tensor_scalar(qs[:, a, :], M2[:, a, :], prm("bq")[:, a:a + 1], float(HD) ** -0.5,
                                    ALU.add, ALU.mult).then_inc(qs_done, 1)
                dve.wait_ge(qs_done, NH * (i + 1))
                V.tensor_copy(q_parts[0][:, :, :], qs).then_inc(q_high, 1)
                dve.wait_ge(q_high, i + 1)
                V.tensor_tensor(q_parts[1][:, :, :], qs, q_parts[0][:, :, :].bitcast(F32), ALU.subtract
                                ).then_inc(q_split, 1)

            def key_lows(i, b):
                n = 4 * i + b
                dve.wait_ge(k_done, 4 * n + 2)
                for a in range(NH):
                    V.scalar_tensor_tensor(kT[1][:, a, 0:LAST], K2[:, a, :], prm("bk")[:, a:a + 1],
                                           kT[0][:, a, 0:LAST].bitcast(F32), ALU.add, ALU.subtract
                                           ).then_inc(lows_done, 1)

            def weigh(j):
                dve.wait_ge(ex_ready, j + 1)
                dve.wait_ge(ou_done, 4 * (j + 1))
                EX = M[:, :].rearrange("p (k a n) -> p k a n", k=2, a=NH)
                V.tensor_tensor(t1[:, :, :], EX[:, 0], ou[:, :, :], ALU.mult).then_inc(t_done, 1)
                V.tensor_tensor(t2[:, :, :].rearrange("p a (b q) -> p a b q", b=TB),
                                EX[:, 1].rearrange("p a (b q) -> p a b q", b=TB),
                                vl[:, :, bass.ds(TB * j, TB)].unsqueeze(3).broadcast_to([P, NH, TB, Q]),
                                ALU.mult).then_inc(t_done, 1)

            def attention_out(j):
                dve.wait_ge(t_done, 2 * (j + 1))
                at_least(dve, wo_ready, j)
                for a in range(NH):
                    V.scalar_tensor_tensor(aT[:, a, :], t1[:, a, :], prm("bv")[:, a:a + 1], t2[:, a, :],
                                           ALU.add, ALU.add).then_inc(aT_done, 1)

            def residual1(j):
                dve.wait_ge(wo_ready, j + 1)
                dve.wait_ge(xb_done, j + 1)
                at_least(dve, kept, j)
                at_least(dve, z2_done, j)
                V.tensor_tensor(x1[:, :], M[:, 0:D], xr[:, :], ALU.add).then_inc(x1_done, 1)

            def statistics2(j):
                held(dve, (init, 2), (x1_done, j + 1))
                statistics(x1[:, :], 1, j, st2, mv2, z2_done)

            def soft_in(j):
                dve.wait_ge(dt_ready, j + 1)
                V.tensor_tensor(dtv[:, 0, :], M[:, 0:H], prm("dtb"), ALU.add).then_inc(dt_done, 1)
                dve.wait_ge(dt_done, j + 1)
                V.tensor_scalar(dtv[:, 10, :], dtv[:, 0, :], 0.0, None, ALU.max).then_inc(soft_max, 1)
                V.scalar_tensor_tensor(dtv[:, 1, :], dtv[:, 0, :], -1.0, dtv[:, 0, :], ALU.mult, ALU.min
                                       ).then_inc(nabs_done, 1)

            su, sr, sy, sw, ss = dtv[:, 2, :], dtv[:, 3, :], dtv[:, 4, :], dtv[:, 8, :], dtv[:, 9, :]

            def link(ins, j, k):
                ins.then_inc(soft, 1)
                dve.wait_ge(soft, NSOFT * j + k)

            def softplus_ratio(j):
                dve.wait_ge(u_done, j + 1)
                dve.wait_ge(soft_max, j + 1)
                link(V.tensor_scalar(sr, su, 2.0, None, ALU.add), j, 1)
                link(V.reciprocal(ss, sr), j, 2)
                V.tensor_tensor(sy, su, ss, ALU.mult).then_inc(soft, 1)

            def softplus_series(j, first, last):
                if first == 0:
                    dve.wait_ge(soft, NSOFT * j + 3)
                    link(V.tensor_tensor(sw, sy, sy, ALU.mult), j, 4)
                    V.tensor_scalar(ss, sw, 1.0 / ATANH[0], None, ALU.mult).then_inc(soft, 1)
                for k in range(max(first, 1), last):
                    dve.wait_ge(soft, NSOFT * j + 4 + k)
                    V.scalar_tensor_tensor(ss, ss, 1.0 / ATANH[k], sw, ALU.add, ALU.mult).then_inc(soft, 1)

            def softplus_end(j):
                dve.wait_ge(soft, NSOFT * j + NSOFT - 1)
                link(V.scalar_tensor_tensor(ss, ss, 1.0, sy, ALU.add, ALU.mult), j, NSOFT)
                V.scalar_tensor_tensor(sw, ss, 2.0, dtv[:, 10, :], ALU.mult, ALU.add).then_inc(soft_sum, 1)
                dve.wait_ge(soft_sum, j + 1)
                at_least(dve, cum_ready, j)
                V.tensor_tensor(dtv[:, 5, :], sw, prm("apar"), ALU.mult).then_inc(a_done, 1)

            def norms(j):
                dve.wait_ge(c2_ready, j + 1)
                dve.wait_ge(ep_done, j + 1)
                V.tensor_tensor(dtv[:, 8, :], M[:, 0:H], dtv[:, 6, :], ALU.mult).then_inc(norm_done, 1)
                dve.wait_ge(norm_done, j + 1)
                V.reciprocal(dtv[:, 9, :], dtv[:, 8, :]).then_inc(rn_done, 1)

            def scale_y(j):
                dve.wait_ge(rn_done, j + 1)
                at_least(dve, ynT_ready, j)
                V.tensor_tensor(yn[:, :].rearrange("p (h d) -> p h d", h=H), y0[:, :].rearrange("p (h d) -> p h d", h=H),
                                dtv[:, 9, :].unsqueeze(2).broadcast_to([P, H, HD]), ALU.mult).then_inc(yn_done, 1)

            def residual2(j):
                dve.wait_ge(y_ready, j + 1)
                dve.wait_ge(kept, j + 1)
                at_least(dve, z3_done, j)
                at_least(dve, x2_out, 16 * j)
                V.tensor_tensor(x2[:, :], M[:, 0:D], xk[:, :], ALU.add).then_inc(x2_done, 1)
                held(dve, (init, 2), (x2_done, j + 1))
                statistics(x2[:, :], 2, j, st3, mv3, z3_done)

            def normalise3(j):
                dve.wait_ge(rstd3, j + 1)
                at_least(dve, z3T_ready, j)
                at_least(dve, z3_out, 16 * j)
                V.tensor_scalar(z3[:, :], x2[:, :], mv[:, 2, 0:1], rs[:, 2, 1:2], ALU.subtract, ALU.mult
                                ).then_inc(z3_done, 1)

            def normalise2(j):
                dve.wait_ge(rstd2, j + 1)
                at_least(dve, z2T_ready, j)
                V.tensor_scalar(z2[:, :], x1[:, :], mv[:, 1, 0:1], rs[:, 1, 1:2], ALU.subtract, ALU.mult
                                ).then_inc(z2_done, 1)

            def take_logits(j):
                dve.wait_ge(lg_ready, j + 1)
                V.tensor_copy(lg[:, 0, :], M[:, 0:E]).then_inc(lg_done, 1)

            def select(j):
                held(dve, (init, 2), (lg_done, j + 1))
                V.max(lg[:, 1, :], lg[:, 0, :]).then_inc(top_done, 1)
                held(dve, (init, 2), (top_done, j + 1))
                V.max_index(mi[:, :], lg[:, 1, :], lg[:, 0, :]).then_inc(index_done, 1)
                V.tensor_tensor(sv[:, 0, 0:1], lg[:, 1, 1:2], lg[:, 1, 0:1], ALU.subtract).then_inc(diff_done, 1)
                dve.wait_ge(index_done, j + 1)
                V.tensor_copy(sv[:, 2, :], mi[:, 0:TOPK]).then_inc(expert_done, 1)
                dve.wait_ge(expert_done, j + 1)
                V.tensor_tensor(oh[:, :, :], cst("iota8").unsqueeze(1).broadcast_to([P, TOPK, E]),
                                sv[:, 2, :].unsqueeze(2).broadcast_to([P, TOPK, E]), ALU.is_equal).then_inc(oh_done, 1)
                dve.wait_ge(oh_done, j + 1)
                at_least(dve, chosen_done, j + 1)
                V.tensor_tensor(lg[:, 2, :], oh[:, 0, :], oh[:, 1, :], ALU.add).then_inc(mm_done, 1)

            def take_ranks(j):
                dve.wait_ge(c2_ready, j + 2)
                V.tensor_tensor(ohr[:, :, :], oh[:, :, :], RK.unsqueeze(1).broadcast_to([P, TOPK, E]), ALU.mult
                                ).then_inc(ranked, 1)
                V.tensor_tensor(chosen[:, :], chosen[:, :], lg[:, 2, :], ALU.add).then_inc(chosen_done, 1)

            def place(j):
                gate = pay[:, :, 2:3].bitcast(F32).rearrange("p k c -> p (k c)")
                dve.wait_ge(ranked, j + 1)
                V.tensor_reduce(sv[:, 3, :], ohr[:, :, :], AX.X, ALU.add).then_inc(rank_done, 1)
                dve.wait_ge(gate_e, j + 1)
                V.tensor_scalar(sv[:, 4, 0:1], sv[:, 1, 0:1], 1.0, None, ALU.add).then_inc(gate_sum, 1)
                dve.wait_ge(rank_done, j + 1)
                V.tensor_copy(ri[:, 0, :], sv[:, 3, :]).then_inc(whole, 1)
                V.tensor_scalar(sv[:, 5, :], sv[:, 3, :], float(TCOL), None, ALU.mult).then_inc(row_a, 1)
                dve.wait_ge(whole, j + 1)
                V.tensor_scalar(ri[:, 1, :], ri[:, 0, :], P.bit_length() - 1, None, ALU.logical_shift_right
                                ).then_inc(col_done, 1)
                dve.wait_ge(gate_sum, j + 1)
                at_least(dve, slots_out, 32 * j)
                at_least(dve, pay_done, 5 * j)
                V.reciprocal(gate[:, 0:1], sv[:, 4, 0:1]).then_inc(pay_done, 1)
                dve.wait_ge(row_a, j + 1)
                V.scalar_tensor_tensor(sv[:, 6, :], sv[:, 2, :], float(TPE), sv[:, 5, :], ALU.mult, ALU.add
                                       ).then_inc(row_b, 1)
                V.tensor_copy(pay[:, :, 0:2], tokf[:, :].rearrange("p (k c) -> p k c", k=TOPK)).then_inc(pay_done, 1)
                dve.wait_ge(pay_done, 5 * j + 2)
                V.tensor_tensor(gate[:, 1:2], gate[:, 0:1], sv[:, 1, 0:1], ALU.mult).then_inc(pay_done, 1)
                V.tensor_scalar(tokf[:, :], tokf[:, :], float(P), None, ALU.add).then_inc(pay_done, 1)
                dve.wait_ge(col_done, j + 1)
                dve.wait_ge(row_b, j + 1)
                V.scalar_tensor_tensor(ri[:, 2, :], ri[:, 1, :], 1.0 - P * TCOL, sv[:, 6, :], ALU.mult, ALU.add
                                       ).then_inc(pay_done, 1)

            def plan_tiles():
                k = [0]

                def link(ins):
                    k[0] += 1
                    ins.then_inc(plan, 1)
                    if k[0] < PLAN:
                        dve.wait_ge(plan, k[0])

                number = cst("tok")[:, 0:1]
                dve.wait_ge(cnt_ready, 1)
                link(V.tensor_scalar(cnti[:, :], M[:, 0:E], float(P - 1), None, ALU.add))
                link(V.tensor_scalar(cnti[:, :], cnti[:, :], P.bit_length() - 1, None, ALU.logical_shift_right))
                link(V.tensor_copy(cnt[:, 0, :], cnti[:, :]))
                link(V.tensor_tensor_scan(cnt[:, 1, :], ones[:, 0:E], cnt[:, 0, :], 0.0, ALU.mult, ALU.add))
                link(V.tensor_scalar(past[:, 0, :], cnt[:, 1, :], number, None, ALU.is_le))
                link(V.tensor_tensor(past[:, 1, :], past[:, 0, :], cnt[:, 0, :], ALU.mult))
                link(V.tensor_reduce(tl[:, 0:2], past[:, :, :], AX.X, ALU.add))
                link(V.tensor_tensor(tl[:, 2:3], number, tl[:, 1:2], ALU.subtract))
                link(V.scalar_tensor_tensor(tl[:, 3:4], tl[:, 0:1], float(TPE), tl[:, 2:3], ALU.mult, ALU.add))
                link(V.tensor_scalar(tl[:, 4:5], tl[:, 0:1], float(E - 1), None, ALU.min))
                dve.wait_ge(plan_ready, 1)
                V.tensor_copy(info[0:1, :, :], M[0:1, P:3 * P].rearrange("p (k n) -> p k n", k=2)[:, :, 0:NSLOT + 1]
                              ).then_inc(info_done, 1)

            def ssd():
                k = [0]

                def link(ins):
                    k[0] += 1
                    ins.then_inc(ssd_dve, 1)
                    dve.wait_ge(ssd_dve, k[0])

                dve.wait_ge(ssd_pe, 1)
                link(V.memset(xp[:, :, 0:KC - 1], 0.0))
                link(V.tensor_copy(xp[:, :, KC - 1:], M[:, 0:NC * Q].rearrange("p (c l) -> p c l", c=NC)))
                taps = prm("convw").rearrange("p (c k) -> p c k", k=KC)

                def tap(n):
                    return taps[:, :, n:n + 1].broadcast_to([P, NC, Q])

                link(V.tensor_tensor(cv[:, 0], xp[:, :, 0:Q], tap(0), ALU.mult))
                for n in range(1, KC):
                    link(V.tensor_tensor(cv[:, 1], xp[:, :, n:n + Q], tap(n), ALU.mult))
                    link(V.tensor_tensor(cv[:, 0], cv[:, 0], cv[:, 1], ALU.add))
                link(V.tensor_tensor(cT, cv[:, 0], prm("convb").unsqueeze(2).broadcast_to([P, NC, Q]), ALU.add))
                n8 = P // HD
                for a in range(NH):
                    last = V.tensor_tensor(cbd[:, a], cT[:, a, :].unsqueeze(1).broadcast_to([P, n8, Q]),
                                           cst("bm8").unsqueeze(2).broadcast_to([P, n8, Q]), ALU.mult)
                link(last)
                le = cst("le")[0:Q, :].unsqueeze(1).broadcast_to([Q, H, Q])
                link(V.tensor_tensor(at_, dtv[0:Q, 5, :].unsqueeze(2).broadcast_to([Q, H, Q]), le, ALU.mult))
                dve.wait_ge(ssd_act, 2)
                link(V.tensor_tensor(ws, gs, ls, ALU.mult))
                for h in range(H):
                    last = V.tensor_tensor(w4[:, h], ws[:, h, :].unsqueeze(1).broadcast_to([Q, TB, Q]),
                                           cst("le")[0:Q, :].unsqueeze(1).broadcast_to([Q, TB, Q]), ALU.mult)
                link(last)
                assert k[0] == 14, k[0]
                dve.wait_ge(ssd_act, 4)

            def tile(i):
                for b in range(TB):
                    nxt = following(i, b)
                    if b == 3 and runs(i - 1):
                        softplus_ratio(i - 1)
                    if runs(nxt[0]):
                        key_lows(*nxt)
                    if b == 3 and runs(i - 1):
                        softplus_series(i - 1, 0, 1)
                    if b == 3 and runs(i - 2):
                        take_logits(i - 2)
                    if b == 0 and runs(i - 3):
                        select(i - 3)
                    if b == 1 and runs(i - 3):
                        place(i - 3)
                    if b == 1 and runs(i - 1):
                        normalise2(i - 1)
                    if b == 2 and runs(i - 2):
                        normalise3(i - 2)
                    if b == 0 and runs(i - 1):
                        weigh(i - 1)
                    if b == 2 and runs(i + 1):
                        take_queries(i + 1)
                    if runs(i):
                        reciprocals(i, b)
                    if b == 3 and runs(i - 1):
                        softplus_series(i - 1, 1, 4)
                    if runs(nxt[0]):
                        maxima(*nxt, 0)
                    if b == 3 and runs(i - 1):
                        softplus_series(i - 1, 4, len(ATANH))
                        softplus_end(i - 1)
                    if b == 0 and runs(i - 1):
                        attention_out(i - 1)
                    if b == 0 and runs(i - 2):
                        norms(i - 2)
                    if b == 0 and runs(i - 3):
                        take_ranks(i - 3)
                    if b == 0 and isinstance(i, int) and i == 2:
                        ssd()
                    if b == 1 and runs(i - 2):
                        residual2(i - 2)
                    if b == 2 and runs(i - 1):
                        soft_in(i - 1)
                    if runs(nxt[0]):
                        maxima(*nxt, 1)
                    if b == 0 and runs(i - 2):
                        scale_y(i - 2)
                    if runs(i):
                        take_output(i, b)
                    if b == 0 and runs(i - 1):
                        residual1(i - 1)
                        statistics2(i - 1)
                    if b == 1 and runs(i + 2):
                        statistics1(i + 2)

            V.memset(chosen[:, :], 0.0).then_inc(chosen_done, 1)
            V.memset(pay[:, :, :].rearrange("p k c -> p (k c)"), 0).then_inc(init, 1)
            dve.wait_ge(con_in, 16)
            V.tensor_copy(tokf[:, :], cst("tok")).then_inc(init, 1)
            dve.wait_ge(init, 2)
            statistics1(0)
            for k, (w, h, l) in enumerate(((wk, wkh, wkl), (wv, wvh, wvl))):
                dve.wait_ge(wh_done, k + 1)
                V.tensor_tensor(l[:, :, :], w, h[:, :, :].bitcast(F32), ALU.subtract).then_inc(wl_done, 1)
            dve.wait_ge(vl_ready, 1)
            V.tensor_copy(vl[:, :, :], M2).then_inc(vl_done, 1)
            for a in range(NH):
                V.tensor_scalar(kl[:, a, :], M2K[:, a, :], prm("bk")[:, a:a + 1], None, ALU.add).then_inc(vl_done, 1)
            dve.wait_ge(vl_done, 3)
            V.tensor_copy(kl_parts[0][:, :, :], kl).then_inc(kl_high, 1)
            dve.wait_ge(kl_high, 1)
            V.tensor_tensor(kl_parts[1][:, :, :], kl, kl_parts[0][:, :, :].bitcast(F32), ALU.subtract).then_inc(kl_low, 1)
            take_queries(0)
            key_lows(0, 0)
            statistics1(1)
            maxima(0, 0, 0)
            maxima(0, 0, 1)
            steps(dve, tile)
            plan_tiles()

        @block.gpsimd
        def _(pool):
            G = nc.gpsimd

            def power(k, j, s_mv, s_var, s_rstd):
                pool.wait_ge(s_mv, j + 1)
                G.tensor_tensor(rs[:, k, 0:1], mv[:, k, 1:2], cst("eps"), ALU.add).then_inc(s_var, 1)
                pool.wait_ge(s_var, j + 1)
                G.tensor_tensor(rs[:, k, 1:2], rs[:, k, 0:1], cst("nhalf"), ALU.pow).then_inc(s_rstd, 1)

            def normalise(k, src, dst, j, s_mv, s_var, s_rstd, s_turned, s_done):
                power(k, j, s_mv, s_var, s_rstd)
                held(pool, (con_in, 16), (s_rstd, j + 1), (s_turned, j))
                G.tensor_scalar(dst[:, :], src[:, :], mv[:, k, 0:1], rs[:, k, 1:2], ALU.subtract, ALU.mult
                                ).then_inc(s_done, 1)

            def normalise1(i):
                normalise(0, xt, z1, i, mv1, var1, rstd1, z1T_ready, z1_done)

            def split_low(i, b):
                n = 4 * i + b
                pool.wait_ge(hi_done, n + 1)
                G.tensor_tensor(ctx_lo[:, b % 2], ctx[:, b], ctx_hi[:, b % 2].bitcast(F32), ALU.subtract
                                ).then_inc(lo_done, 1)

            def lay_queries(i, b):
                n = 4 * i + b
                pool.wait_ge(q_split, i + 1)
                at_least(pool, s_ready, 4 * (n - 1))
                for dst, src in zip(qbd, q_parts):
                    for a in range(NH):
                        G.tensor_tensor(dst[:, b % 2, 2 * a:2 * a + 2, :].rearrange("p g (h q) -> p g h q", h=HG),
                                        src[:, a, b * Q:(b + 1) * Q].bitcast(F32).unsqueeze(1).unsqueeze(1)
                                        .broadcast_to([P, 2, HG, Q]),
                                        cst("bm").rearrange("p (g h) -> p g h", g=2).unsqueeze(3)
                                        .broadcast_to([P, 2, HG, Q]), ALU.mult).then_inc(qbd_done, 1)

            def last_probs(i, b):
                n = 4 * i + b
                pool.wait_ge(rec_done, n + 1)
                G.tensor_tensor(rr[:, 1, :], pr[:, :, LAST], rr[:, 0, :], ALU.mult).then_inc(pl_done, 1)
                pool.wait_ge(pl_done, n + 1)
                at_least(pool, o_ready, n)
                G.tensor_tensor(px[:, :, :], rr[:, :, :].rearrange("p k g -> p (k g)").unsqueeze(2)
                                .broadcast_to([P, 2 * NG, HG]),
                                cst("dm").unsqueeze(1).broadcast_to([P, 2 * NG, HG]), ALU.mult).then_inc(px_done, 1)

            def add_bias(j):
                pool.wait_ge(xr_in, 16 * (j + 1))
                G.tensor_tensor(xr[:, :], xr[:, :], prm("bo"), ALU.add).then_inc(xb_done, 1)

            def write_slots(j):
                held(pool, (con_in, 16), (pay_done, 5 * j + 5))
                for k in range(TOPK):
                    G.indirect_dma_start(table[:, :], bass.IndirectOffsetOnAxis(ri[:, 2, k:k + 1].bitcast(U32), 0),
                                         pay[:, k, :], None).then_inc(slots_out, 16)

            def tile(i):
                for b in range(TB):
                    two = following(i, b, 2)
                    if b == 2 and runs(i - 2):
                        power(2, i - 2, mv3, var3, rstd3)
                    if b == 1 and runs(i - 1):
                        power(1, i - 1, mv2, var2, rstd2)
                    if runs(two[0]):
                        split_low(*two)
                    if runs(i):
                        last_probs(i, b)
                    if b == 0 and runs(i - 1):
                        add_bias(i - 1)
                    if runs(two[0]):
                        lay_queries(*two)
                    if b == 2 and runs(i + 2):
                        normalise1(i + 2)
                    if b == 3 and runs(i - 3):
                        write_slots(i - 3)

            pool.wait_ge(con_in, 16)
            pool.wait_ge(par_in, 16)
            normalise1(0)
            split_low(0, 0)
            lay_queries(0, 0)
            normalise1(1)
            split_low(0, 1)
            lay_queries(0, 1)
            pool.wait_ge(pad_in, 16)
            steps(pool, tile)
            pool.wait_ge(slots_out, 32 * NT)


def experts(nc, zbuf, outd, cst, spare, wg, wu, wd, tab, info, tab_in, info_done, w_in, wd_in):
    own = ExitStack()
    with own:
        def sb(name, shape, dt=F32):
            return own.enter_context(nc.sbuf_tensor(name, shape, dt))

        def sem(name):
            return own.enter_context(nc.semaphore(name))

        ident = cst("ident")
        gi = sb("gi", [P, 2, 4], I32)
        oi = sb("oi", [P, 2, 4], I32)
        zg, sg, yb = (spare[0][:, at:at + 2 * n].rearrange("p (s n) -> p s n", s=2)
                      for at, n in ((0, D), (2 * D, FH), (2 * D + F, D)))
        hb = spare[1][:, 0:F]
        zT = [sb(f"zT_{h}", [P, 2, NH, P], F32R) for h in ("hi", "lo")]
        hT = [sb(f"hT_{h}", [P, FC, P], F32R) for h in ("hi", "lo")]
        gw = [sb(f"gw_{h}", [P, 2, NH, F], F32R) for h in ("hi", "lo")]
        uw = [sb(f"uw_{h}", [P, NH, F], F32R) for h in ("hi", "lo")]
        dw = [sb(f"dw_{h}", [P, FC, D], F32R) for h in ("hi", "lo")]
        GB = own.enter_context(nc.psum_tensor("gate_p", [P, 2, 512], F32))
        UB = own.enter_context(nc.psum_tensor("up_p", [P, 2, 512], F32))
        HB = [own.enter_context(nc.psum_tensor(f"ht_p{k}", [P, 512], F32)) for k in range(2)]
        YB = own.enter_context(nc.psum_tensor("y_p", [P, 512], F32))
        ZB = own.enter_context(nc.psum_tensor("z_p", [P, 512], F32))

        gi_done, oi_done = sem("gi_done"), sem("oi_done")
        zg_in = [sem(f"zg_in{s}") for s in range(2)]
        y_out = sem("y_out")
        zT_ready, zT_done = sem("zT_ready"), sem("zT_done")
        g_ready, u_ready, silu_done, h_done = sem("g_ready"), sem("u_ready"), sem("silu_done"), sem("h_done")
        hT_ready, hT_high, zT_high = sem("hT_ready"), sem("hT_high"), sem("zT_high")
        hT0_done, hT1_done = sem("hT0_done"), sem("hT1_done")
        gw_high, gw_high_rest, gw_done, gw_rest = sem("gw_high"), sem("gw_high_rest"), sem("gw_done"), sem("gw_rest")
        uw_high, uw_done = sem("uw_high"), sem("uw_done")
        dw_high, dw_high_rest, dw_done, dw_rest = sem("dw_high"), sem("dw_high_rest"), sem("dw_done"), sem("dw_rest")
        y_ready, y_done = sem("y_ready"), sem("y_done")

        block = own.enter_context(nc.Block())

        def expert_of(t):
            return info[0:1, 1, bass.ds(t, 1)]

        def of(w, e, *at):
            one = w[:, bass.ds(e, 1)]
            return one[(slice(None), slice(None), *at)].rearrange("p o c n -> p (o c n)")

        def flat(part):
            return part.rearrange("p c n -> p (c n)")

        def tiles(eng, body):
            body(0, 0, first=True)
            with eng.Fori(1, NSLOT - 2, 2) as t:
                body(t, 1)
                body(t + 1, 0)
            body(NSLOT - 2, 1)
            body(NSLOT - 1, 0, last=True)

        @block.tensor
        def _(pe):
            def mm(out, lhsT, rhs, start=True, stop=True):
                return nc.tensor.matmul(out, lhsT, rhs, start=start, stop=stop)

            def turn_z(t, s):
                pe.wait_ge(zg_in[s], 16 * (t // 2 + 1) if isinstance(t, int) else 16 * ((t - s) // 2 + 1))
                at_least(pe, zT_done, t)
                for a in range(NH):
                    last = nc.tensor.transpose(ZB[:, a * P:(a + 1) * P], zg[:, s, a * P:(a + 1) * P], ident)
                last.then_inc(zT_ready, 1)

            def product(out, x, w, first, last):
                (xh, xl), (wh, wl) = x, w
                for k, (a, b) in enumerate(((xh, wh), (xh, wl), (xl, wh))):
                    ins = mm(out, a, b, first and k == 0, last and k == 2)
                return ins

            def gate(t, s):
                pe.wait_ge(zT_done, t + 1)
                pe.wait_ge(gw_done, t + 1)
                pe.wait_ge(gw_rest, t + 1)
                at_least(pe, silu_done, t)
                inner(GB, s, [w[:, s] for w in gw]).then_inc(g_ready, 1)

            def up(t, s):
                pe.wait_ge(uw_done, t + 1)
                at_least(pe, h_done, t)
                inner(UB, s, uw).then_inc(u_ready, 1)

            def inner(bank, s, w):
                for f in range(2):
                    for c in range(NH):
                        last = product(bank[:, f, 0:FH], [z[:, s, c, :] for z in zT],
                                       [p[:, c, f * FH:(f + 1) * FH] for p in w], c == 0, c == NH - 1)
                return last

            def turn_h(t):
                pe.wait_ge(h_done, t + 1)
                for k in range(2):
                    at_least(pe, (hT0_done, hT1_done)[k], t if k == 0 else 2 * t)
                    for c in range(4 * k, min(4 * k + 4, FC)):
                        n = P if c < FC - 1 else FL
                        last = nc.tensor.transpose(HB[k][0:n, (c % 4) * P:(c % 4 + 1) * P], hb[:, c * P:c * P + n], ident)
                    last.then_inc(hT_ready, 1)

            def down(t):
                pe.wait_ge(hT0_done, t + 1)
                pe.wait_ge(hT1_done, 2 * t + 2)
                pe.wait_ge(dw_done, t + 1)
                at_least(pe, y_done, t)
                for c in range(FC):
                    n = P if c < FC - 1 else FL
                    if c == DV:
                        pe.wait_ge(dw_rest, t + 1)
                    last = product(YB[:, 0:D], [h[0:n, c, :] for h in hT], [p[0:n, c, :] for p in dw],
                                   c == 0, c == FC - 1)
                last.then_inc(y_ready, 1)

            def body(t, s, first=False, last=False):
                if first:
                    turn_z(t, s)
                else:
                    turn_h(t - 1)
                gate(t, s)
                if not last:
                    turn_z(t + 1, 1 - s)
                up(t, s)
                if not first:
                    down(t - 1)

            tiles(pe, body)
            turn_h(NSLOT - 1)
            down(NSLOT - 1)

        @block.scalar
        def _(act):
            def silu(t):
                act.wait_ge(g_ready, t + 1)
                at_least(act, h_done, t)
                nc.scalar.activation(sg[:, :, :], GB[:, :, 0:FH], ACT.Silu).then_inc(silu_done, 1)

            def high(dst, src, done):
                nc.scalar.activation(dst, src, ACT.Copy).then_inc(done, 1)

            def take_z(t, s):
                act.wait_ge(zT_ready, t + 1)
                at_least(act, u_ready, t - 1)
                high(flat(zT[0][:, s]), ZB[:, 0:NH * P], zT_high)

            def split_gate(t, s):
                e = nc.scalar.value_load(expert_of(t), min_val=0, max_val=E - 1)
                at_least(act, g_ready, t - 1)
                high(gw[0][:, s, 1, :], of(wg, e, slice(1, 2)), gw_high_rest)
                high(gw[0][:, s, 0, :], of(wg, e, slice(0, 1)), gw_high)

            def split_up(t):
                e = nc.scalar.value_load(expert_of(t), min_val=0, max_val=E - 1)
                at_least(act, u_ready, t)
                high(flat(uw[0][:, :, :]), of(wu, e), uw_high)

            def split_down(t):
                e = nc.scalar.value_load(expert_of(t), min_val=0, max_val=E - 1)
                at_least(act, y_ready, t)
                high(flat(dw[0][:, 0:DV, :]), of(wd, e, slice(0, DV)), dw_high)
                high(flat(dw[0][:, DV:FC, :]), of(wd, e, slice(DV, FC)), dw_high_rest)

            def take_h(t):
                act.wait_ge(hT_ready, 2 * t + 1)
                at_least(act, y_ready, t)
                high(flat(hT[0][:, 0:4, :]), HB[0][:, :], hT_high)
                act.wait_ge(hT_ready, 2 * t + 2)
                high(hT[0][:, 4, :], HB[1][:, 0:P], hT_high)
                high(hT[0][0:FL, 5, :], HB[1][0:FL, P:2 * P], hT_high)

            def take_y(t, s):
                act.wait_ge(y_ready, t + 1)
                act.wait_ge(oi_done, t + 1)
                nc.scalar.activation(yb[:, s, :], YB[:, 0:D], ACT.Copy, scale=oi[:, s, 2:3].bitcast(F32)
                                     ).then_inc(y_done, 1)

            def body(t, s, first=False, last=False):
                if not first:
                    take_h(t - 1)
                    split_down(t - 1)
                silu(t)
                if not last:
                    take_z(t + 1, 1 - s)
                    split_gate(t + 1, 1 - s)
                    split_up(t + 1)
                if not first:
                    take_y(t - 1, 1 - s)

            act.wait_ge(info_done, 1)
            act.wait_ge(w_in, 16 * 2 * E)
            split_gate(0, 0)
            split_up(0)
            take_z(0, 0)
            act.wait_ge(wd_in, 16 * E)
            tiles(act, body)
            take_h(NSLOT - 1)
            split_down(NSLOT - 1)
            take_y(NSLOT - 1, 0)

        @block.vector
        def _(dve):
            V = nc.vector
            def low(dst, src, hi, done):
                V.tensor_tensor(dst, src, hi.bitcast(F32), ALU.subtract).then_inc(done, 1)

            def split_gate(t, s):
                e = V.value_load(expert_of(t), min_val=0, max_val=E - 1)
                dve.wait_ge(gw_high, t + 1)
                low(gw[1][:, s, 0, :], of(wg, e, slice(0, 1)), gw[0][:, s, 0, :], gw_done)

            def split_up(t):
                e = V.value_load(expert_of(t), min_val=0, max_val=E - 1)
                dve.wait_ge(uw_high, t + 1)
                low(flat(uw[1][:, :, :]), of(wu, e), flat(uw[0][:, :, :]), uw_done)

            def split_down(t):
                e = V.value_load(expert_of(t), min_val=0, max_val=E - 1)
                dve.wait_ge(dw_high, t + 1)
                low(flat(dw[1][:, 0:DV, :]), of(wd, e, slice(0, DV)), flat(dw[0][:, 0:DV, :]), dw_done)

            def take_z(t, s):
                dve.wait_ge(zT_high, t + 1)
                low(flat(zT[1][:, s]), ZB[:, 0:NH * P], flat(zT[0][:, s]), zT_done)

            def gate_up(t):
                dve.wait_ge(silu_done, t + 1)
                dve.wait_ge(u_ready, t + 1)
                at_least(dve, hT_ready, 2 * t)
                V.tensor_tensor(hb[:, :].rearrange("p (f n) -> p f n", f=2), sg[:, :, :], UB[:, :, 0:FH], ALU.mult
                                ).then_inc(h_done, 1)

            def take_h(t):
                dve.wait_ge(hT_high, 3 * t + 3)
                low(flat(hT[1][:, 0:4, :]), HB[0][:, :], flat(hT[0][:, 0:4, :]), hT0_done)
                low(hT[1][:, 4, :], HB[1][:, 0:P], hT[0][:, 4, :], hT1_done)
                low(hT[1][0:FL, 5, :], HB[1][0:FL, P:2 * P], hT[0][0:FL, 5, :], hT1_done)

            def body(t, s, first=False, last=False):
                if not first:
                    take_h(t - 1)
                    split_down(t - 1)
                gate_up(t)
                if not last:
                    take_z(t + 1, 1 - s)
                    split_gate(t + 1, 1 - s)
                    split_up(t + 1)

            dve.wait_ge(info_done, 1)
            split_gate(0, 0)
            split_up(0)
            take_z(0, 0)
            tiles(dve, body)
            take_h(NSLOT - 1)
            split_down(NSLOT - 1)

        @block.gpsimd
        def _(pool):
            G = nc.gpsimd

            def owners(dst, t, done):
                col = G.value_load(info[0:1, 0, bass.ds(t, 1)], min_val=0, max_val=TCOL - 1)
                G.tensor_copy(dst.unsqueeze(1), tab[:, bass.ds(col, 1), :]).then_inc(done, 1)

            def gather(t, s):
                at_least(pool, zT_ready, t - 1)
                owners(gi[:, s, :], t, gi_done)
                held(pool, (tab_in, 16), (gi_done, t + 1))
                G.indirect_dma_start(zg[:, s, :], None, zbuf[:, :],
                                     bass.IndirectOffsetOnAxis(gi[:, s, 0:1].bitcast(U32), 0)).then_inc(zg_in[s], 16)

            def scatter(t, s):
                held(pool, (tab_in, 16), (oi_done, t + 1), (y_done, t + 1), (y_out, 16 * t))
                G.indirect_dma_start(outd[:, :], bass.IndirectOffsetOnAxis(oi[:, s, 1:2].bitcast(U32), 0),
                                     yb[:, s, :], None, compute_op=ALU.add).then_inc(y_out, 16)

            def low(dst, src, hi, done):
                G.tensor_tensor(dst, src, hi.bitcast(F32), ALU.subtract).then_inc(done, 1)

            def split_gate(t, s):
                e = G.value_load(expert_of(t), min_val=0, max_val=E - 1)
                pool.wait_ge(gw_high_rest, t + 1)
                low(gw[1][:, s, 1, :], of(wg, e, slice(1, 2)), gw[0][:, s, 1, :], gw_rest)

            def split_down(t):
                e = G.value_load(expert_of(t), min_val=0, max_val=E - 1)
                pool.wait_ge(dw_high_rest, t + 1)
                low(flat(dw[1][:, DV:FC, :]), of(wd, e, slice(DV, FC)), flat(dw[0][:, DV:FC, :]), dw_rest)

            def body(t, s, first=False, last=False):
                if not first:
                    owners(oi[:, 1 - s, :], t - 1, oi_done)
                if not last:
                    gather(t + 2, s)
                if not first:
                    split_down(t - 1)
                if not isinstance(t, int) or t + 1 < NSLOT:
                    split_gate(t + 1, 1 - s)
                if not first:
                    scatter(t - 1, 1 - s)

            pool.wait_ge(info_done, 1)
            split_gate(0, 0)
            pool.wait_ge(tab_in, 16)
            gather(0, 0)
            gather(1, 1)
            body(0, 0, first=True)
            body(1, 1)
            body(2, 0)
            with pool.Fori(3, NSLOT - 2, 2) as t:
                body(t, 1)
                body(t + 1, 0)
            body(NSLOT - 2, 1, last=True)
            body(NSLOT - 1, 0, last=True)
            split_down(NSLOT - 1)
            owners(oi[:, 0, :], NSLOT - 1, oi_done)
            scatter(NSLOT - 1, 0)
            pool.wait_ge(y_out, 16 * NSLOT)


def kernel(**inputs):
    import numpy as np
    import concourse.bacc as bacc
    from concourse.bass_utils import run_bass_kernel_spmd as run

    a = {k: np.asarray(v) for k, v in inputs.items()}

    def rows(w):
        return np.ascontiguousarray(w.reshape(-1, P, w.shape[1]).transpose(1, 0, 2)).reshape(P, -1)

    def wide(x):
        return np.broadcast_to(x.reshape(1, -1), (P, x.size))

    w_in = a["L0_attn_W_in"].T
    packed = dict(wq=rows(a["L0_xattn_Wq"].T), wk=rows(a["L0_xattn_Wk"].T), wv=rows(a["L0_xattn_Wv"].T),
                  wo=rows(a["L0_xattn_Wo"].T), wdt=rows(w_in[:, 3 * D:]),
                  wout=rows(a["L0_attn_W_out"].T), wrt=rows(a["L0_ffn_w_router"].T),
                  bq=a["L0_xattn_bq"].reshape(NH, P).T, bk=a["L0_xattn_bk"].reshape(NH, P).T,
                  bv=a["L0_xattn_bv"].reshape(NH, P).T, bo=wide(a["L0_xattn_bo"]), convw=rows(a["L0_attn_conv_w"]),
                  convb=a["L0_attn_conv_b"].reshape(NC, P).T, apar=wide(a["L0_attn_A_param"]),
                  dtb=wide(a["L0_attn_dt_bias"]))
    par = np.concatenate([packed[n] for n in PARAMS], axis=1)

    p, f32 = np.arange(P)[:, None], np.float32
    ch, q = np.arange(D)[None], np.arange(Q)[None]
    m = np.arange(P)[None]
    const = dict(ident=p == m, sel=p % Q == q, hm=p // HD % HG == np.arange(HG),
                 bm=p // HD == np.arange(2 * HG), dm=p // Q == np.arange(HG), er=ch // HD == p,
                 ep=ch // HD == p - H, trib=(p // Q == m // Q) & (p <= m), tris=p < m, ones=p + m >= 0,
                 gt=p > q, le=p <= q, bm8=p // HD == np.arange(P // HD), iota8=p * 0 + np.arange(E),
                 tok=p + np.array([0, 0, 0, 0]), nhalf=p * 0 - 0.5,
                 eps=p * 0 + EPS)
    con = np.concatenate([const[n].astype(f32) for n in CONSTS], axis=1)
    pad = np.zeros((P, TCOL, 4), np.int32)
    pad[:, :, 1] = TOK + p

    ctx = a["ctx_1024"]
    ctxT = np.zeros((P, B, NH, SP), ctx.dtype)
    ctxT[..., :S] = ctx.transpose(2, 0, 1).reshape(NH, P, B, S).transpose(1, 2, 0, 3)
    down = np.zeros((E, FC * P, D), ctx.dtype)
    down[:, :F] = a["L0_ffn_w_down"]

    def cols(w):
        return w.reshape(E, -1, P, w.shape[2]).transpose(2, 0, 1, 3)

    arrays = dict(x=a["x"].reshape(TOK, D), ctx=ctxT, ctx_last=ctxT[:, :, :, LAST].transpose(0, 2, 1),
                  mask=a["mask_BxSxS2_ff0"], par=par, wxbc=rows(w_in[:, :3 * D]).reshape(P, NH, 3 * D),
                  con=con, pad=pad.reshape(P, -1),
                  wg=cols(a["L0_ffn_w_gate"]), wu=cols(a["L0_ffn_w_up"]), wd=cols(down))
    arrays = {f"in_{k}": np.ascontiguousarray(v) for k, v in arrays.items()}
    nc = bacc.Bacc("TRN2", target_bir_lowering=False, num_devices=1)
    aps = [nc.dram_tensor(k, v.shape, mybir.dt.from_np(v.dtype), kind="ExternalInput").ap() for k, v in arrays.items()]
    out = nc.dram_tensor("out", (TOK + P, D), F32, kind="ExternalOutput").ap()
    perceiver(nc, *aps, out)
    r = run(nc, [arrays], core_ids=[0])
    return r.results[0]["out"][:TOK].reshape(B, Q, D)
```
